# Optimizing a Trainium2 kernel written in Bass

```python
import numpy as np
import jax
import jax.numpy as jnp

def _softmax(x, axis=-1):
    return jax.nn.softmax(x, axis=axis)

def _gelu(x):
    return jax.nn.gelu(x, approximate=True)

def _silu(x):
    return jax.nn.silu(x)

def _sigmoid(x):
    return jax.nn.sigmoid(x)

def _layernorm(x, axis=-1, eps=1e-05):
    m = jnp.mean(x, axis=axis, keepdims=True)
    v = jnp.var(x, axis=axis, keepdims=True)
    return (x - m) / jnp.sqrt(v + eps)

def _scatter_add(tgt, idx, src, axis=0):
    return tgt.at[idx].add(src)

def _segment_sum(src, seg, n):
    return jax.ops.segment_sum(src, seg, n)
kernel_name = 'mk_gps_d1_gnn_r8_dd3b99'

def setup_inputs(seed: int=0):
    np.random.seed(seed)
    _w = jnp.asarray

    def _rec_inputs():
        import jax
        import jax.numpy as jnp
        _gk = jax.random.key(seed)
        x = -8.776e-05 + 1 * jax.random.normal(jax.random.fold_in(_gk, 1), (2500, 256), jnp.float32)
        _s = jax.random.randint(jax.random.fold_in(_gk, 2), (20000,), 0, 2500, jnp.int32)
        _d = jax.random.randint(jax.random.fold_in(_gk, 3), (20000,), 0, 2500, jnp.int32)
        _loop = jnp.arange(2500, dtype=jnp.int32)
        src = jnp.concatenate([_s, _d, _loop])
        dst = jnp.concatenate([_d, _s, _loop])
        _o = jnp.argsort(dst, stable=True)
        src = src[_o]
        dst = dst[_o]
        return (x, src, dst)
    x, src, dst = _rec_inputs()

    def _L0_gnn_setup():
        import jax, jax.numpy as jnp
        import numpy as np
        N = 2500
        E = 40000
        DIN = 256
        DOUT = 256
        L = 3

        def _edge_conv(x, src, dst, W, b):
            xi = x[dst]
            xj = x[src]
            m = jnp.concatenate([xi, xj - xi], axis=-1) @ W + b
            s = jax.ops.segment_sum(m, dst, num_segments=N)
            cnt = jax.ops.segment_sum(jnp.ones((dst.shape[0],), m.dtype), dst, num_segments=N)
            return s / jnp.maximum(cnt, 1.0)[:, None]
        key = jax.random.key(seed)
        ks = jax.random.split(key, 4 + 2 * L)
        x = jax.random.normal(ks[0], (N, DIN), dtype=jnp.float32)
        edge_index = jax.random.randint(ks[1], (2, E), 0, N, dtype=jnp.int64)
        scale = 0.05
        inp = {'x': x, 'edge_index': edge_index}
        din = DIN
        for l in range(L):
            inp[f'W{l}'] = jax.random.normal(ks[2 + l], (2 * din, DOUT), dtype=jnp.float32) * scale
            inp[f'b{l}'] = jnp.zeros((DOUT,), dtype=jnp.float32)
            din = DOUT
        cat_dim = DIN + L * DOUT
        inp['Wf'] = jax.random.normal(ks[2 + L], (cat_dim, DOUT), dtype=jnp.float32) * scale
        inp['bf'] = jnp.zeros((DOUT,), dtype=jnp.float32)
        return inp
    _L0_gnn_all = _L0_gnn_setup()
    _L0_gnn_in = {k: v for k, v in _L0_gnn_all.items() if k in ('W0', 'b0', 'W1', 'b1', 'W2', 'b2', 'Wf', 'bf')}
    del _L0_gnn_all

    def _L0_mix_setup():
        import jax, jax.numpy as jnp
        import numpy as np
        HEADS = 8
        DIM_HEAD = 32
        SCALE = DIM_HEAD ** (-0.5)
        EPS = 1e-05

        def _layernorm_gamma(x, gamma):
            mu = jnp.mean(x, axis=-1, keepdims=True)
            var = jnp.var(x, axis=-1, keepdims=True)
            return (x - mu) * jax.lax.rsqrt(var + EPS) * gamma
        key = jax.random.key(seed)
        k1, k2, k3 = jax.random.split(key, 3)
        B, N, D = (8, 2048, 256)
        hidden = HEADS * DIM_HEAD
        x = jax.random.normal(k1, (B, N, D), dtype=jnp.float32)
        Wqkv = jax.random.normal(k2, (D, 3 * hidden), dtype=jnp.float32) * D ** (-0.5)
        Wout = jax.random.normal(k3, (hidden, D), dtype=jnp.float32) * hidden ** (-0.5)
        gamma = jnp.ones((D,), dtype=jnp.float32)
        return {'x': x, 'Wqkv': Wqkv, 'Wout': Wout, 'gamma': gamma}
    _L0_mix_all = _L0_mix_setup()
    _L0_mix_in = {k: v for k, v in _L0_mix_all.items() if k in ('Wqkv', 'Wout', 'gamma')}
    del _L0_mix_all

    def _L0_ffn_setup():
        import jax, jax.numpy as jnp
        import numpy as np
        from jax import lax
        key = jax.random.key(seed)
        B, T, I, H = (64, 256, 256, 256)
        ks = jax.random.split(key, 13)
        s = 1.0 / np.sqrt(H)

        def w(k, shape):
            return jax.random.uniform(k, shape, jnp.float32, -s, s)
        return {'x': jax.random.normal(ks[0], (B, T, I), jnp.float32), 'U_i': w(ks[1], (I, H)), 'V_i': w(ks[2], (H, H)), 'b_i': w(ks[3], (H,)), 'U_f': w(ks[4], (I, H)), 'V_f': w(ks[5], (H, H)), 'b_f': w(ks[6], (H,)), 'U_c': w(ks[7], (I, H)), 'V_c': w(ks[8], (H, H)), 'b_c': w(ks[9], (H,)), 'U_o': w(ks[10], (I, H)), 'V_o': w(ks[11], (H, H)), 'b_o': w(ks[12], (H,))}
    _L0_ffn_all = _L0_ffn_setup()
    _L0_ffn_in = {k: v for k, v in _L0_ffn_all.items() if k in ('U_i', 'V_i', 'b_i', 'U_f', 'V_f', 'b_f', 'U_c', 'V_c', 'b_c', 'U_o', 'V_o', 'b_o')}
    del _L0_ffn_all
    return {'x': x, 'src': src, 'dst': dst, 'L0_gnn_W0': _L0_gnn_in['W0'], 'L0_gnn_b0': _L0_gnn_in['b0'], 'L0_gnn_W1': _L0_gnn_in['W1'], 'L0_gnn_b1': _L0_gnn_in['b1'], 'L0_gnn_W2': _L0_gnn_in['W2'], 'L0_gnn_b2': _L0_gnn_in['b2'], 'L0_gnn_Wf': _L0_gnn_in['Wf'], 'L0_gnn_bf': _L0_gnn_in['bf'], 'L0_mix_Wqkv': _L0_mix_in['Wqkv'], 'L0_mix_Wout': _L0_mix_in['Wout'], 'L0_mix_gamma': _L0_mix_in['gamma'], 'L0_ffn_U_i': _L0_ffn_in['U_i'], 'L0_ffn_V_i': _L0_ffn_in['V_i'], 'L0_ffn_b_i': _L0_ffn_in['b_i'], 'L0_ffn_U_f': _L0_ffn_in['U_f'], 'L0_ffn_V_f': _L0_ffn_in['V_f'], 'L0_ffn_b_f': _L0_ffn_in['b_f'], 'L0_ffn_U_c': _L0_ffn_in['U_c'], 'L0_ffn_V_c': _L0_ffn_in['V_c'], 'L0_ffn_b_c': _L0_ffn_in['b_c'], 'L0_ffn_U_o': _L0_ffn_in['U_o'], 'L0_ffn_V_o': _L0_ffn_in['V_o'], 'L0_ffn_b_o': _L0_ffn_in['b_o']}

def reference(x, src, dst, L0_gnn_W0, L0_gnn_b0, L0_gnn_W1, L0_gnn_b1, L0_gnn_W2, L0_gnn_b2, L0_gnn_Wf, L0_gnn_bf, L0_mix_Wqkv, L0_mix_Wout, L0_mix_gamma, L0_ffn_U_i, L0_ffn_V_i, L0_ffn_b_i, L0_ffn_U_f, L0_ffn_V_f, L0_ffn_b_f, L0_ffn_U_c, L0_ffn_V_c, L0_ffn_b_c, L0_ffn_U_o, L0_ffn_V_o, L0_ffn_b_o):
    import jax
    import jax.numpy as jnp

    def _L0_gnn_ref(x, edge_index, W0, b0, W1, b1, W2, b2, Wf, bf):
        import jax, jax.numpy as jnp
        import numpy as np
        N = 2500
        E = 40000
        DIN = 256
        DOUT = 256
        L = 3

        def _edge_conv(x, src, dst, W, b):
            xi = x[dst]
            xj = x[src]
            m = jnp.concatenate([xi, xj - xi], axis=-1) @ W + b
            s = jax.ops.segment_sum(m, dst, num_segments=N)
            cnt = jax.ops.segment_sum(jnp.ones((dst.shape[0],), m.dtype), dst, num_segments=N)
            return s / jnp.maximum(cnt, 1.0)[:, None]
        src, dst = (edge_index[0], edge_index[1])
        xs = [x]
        h = x
        for W, b in ((W0, b0), (W1, b1), (W2, b2)):
            h = jax.nn.relu(_edge_conv(h, src, dst, W, b))
            xs.append(h)
        cat = jnp.concatenate(xs, axis=-1)
        return cat @ Wf + bf

    def _L0_mix_ref(x, Wqkv, Wout, gamma):
        import jax, jax.numpy as jnp
        import numpy as np
        HEADS = 8
        DIM_HEAD = 32
        SCALE = DIM_HEAD ** (-0.5)
        EPS = 1e-05

        def _layernorm_gamma(x, gamma):
            mu = jnp.mean(x, axis=-1, keepdims=True)
            var = jnp.var(x, axis=-1, keepdims=True)
            return (x - mu) * jax.lax.rsqrt(var + EPS) * gamma
        B, N, D = x.shape
        qkv = x @ Wqkv
        q, k, v = jnp.split(qkv, 3, axis=-1)

        def to_heads(t):
            return t.reshape(B, N, HEADS, DIM_HEAD).transpose(0, 2, 1, 3)
        q, k, v = map(to_heads, (q, k, v))
        q = jax.nn.softmax(q, axis=-1) * SCALE
        k = jax.nn.softmax(k, axis=2)
        context = jnp.einsum('bhnd,bhne->bhde', k, v)
        out = jnp.einsum('bhde,bhnd->bhne', context, q)
        out = out.transpose(0, 2, 1, 3).reshape(B, N, HEADS * DIM_HEAD)
        out = out @ Wout
        return _layernorm_gamma(out, gamma)

    def _L0_ffn_ref(x, U_i, V_i, b_i, U_f, V_f, b_f, U_c, V_c, b_c, U_o, V_o, b_o):
        import jax, jax.numpy as jnp
        import numpy as np
        from jax import lax
        B, T, _ = x.shape
        H = U_i.shape[1]
        xt = jnp.swapaxes(x, 0, 1)
        xi = xt @ U_i + b_i
        xf = xt @ U_f + b_f
        xg = xt @ U_c + b_c
        xo = xt @ U_o + b_o
        h0 = jnp.zeros((B, H), x.dtype)
        c0 = jnp.zeros((B, H), x.dtype)

        def step(carry, xs):
            h, c = carry
            xi_t, xf_t, xg_t, xo_t = xs
            i_t = jax.nn.sigmoid(xi_t + h @ V_i)
            f_t = jax.nn.sigmoid(xf_t + h @ V_f)
            g_t = jnp.tanh(xg_t + h @ V_c)
            o_t = jax.nn.sigmoid(xo_t + h @ V_o)
            c_new = h * c + i_t * g_t
            h_new = o_t * jnp.tanh(c_new)
            return ((h_new, c_new), h_new)
        (_, _), hs = lax.scan(step, (h0, c0), (xi, xf, xg, xo))
        return jnp.swapaxes(hs, 0, 1)
    edge_index = jnp.stack([src, dst])
    xn = _layernorm(x, axis=-1)
    x = x + _L0_gnn_ref(xn, edge_index, L0_gnn_W0, L0_gnn_b0, L0_gnn_W1, L0_gnn_b1, L0_gnn_W2, L0_gnn_b2, L0_gnn_Wf, L0_gnn_bf) + _L0_mix_ref(xn[None], L0_mix_Wqkv, L0_mix_Wout, L0_mix_gamma)[0]
    x = x + _L0_ffn_ref(_layernorm(x, axis=-1)[None], L0_ffn_U_i, L0_ffn_V_i, L0_ffn_b_i, L0_ffn_U_f, L0_ffn_V_f, L0_ffn_b_f, L0_ffn_U_c, L0_ffn_V_c, L0_ffn_b_c, L0_ffn_U_o, L0_ffn_V_o, L0_ffn_b_o)[0]
    return x

_drawn_inputs = setup_inputs


def setup_inputs(seed=0):
    import zlib

    import numpy as np

    out = dict(_drawn_inputs(seed))
    spreads = {'L0_gnn_b0': (0.0, 0.1),
     'L0_gnn_b1': (0.0, 0.1),
     'L0_gnn_b2': (0.0, 0.1),
     'L0_gnn_bf': (0.0, 0.1),
     'L0_mix_gamma': (1.0, 0.2)}
    factors = {'L0_ffn_U_i': 3.234,
     'L0_ffn_V_i': 8.0,
     'L0_ffn_b_i': 8.0,
     'L0_ffn_V_c': 6.273,
     'L0_ffn_b_c': 8.0,
     'L0_ffn_U_o': 2.945,
     'L0_ffn_V_o': 8.0,
     'L0_ffn_b_o': 8.0}
    for name, (base, spread) in spreads.items():
        noise = np.random.default_rng([zlib.crc32(name.encode()), seed]).standard_normal(out[name].shape)
        drawn = base * np.exp(spread * noise) if base else spread * noise
        out[name] = jnp.asarray(drawn.astype(out[name].dtype))
    for name, factor in factors.items():
        out[name] = (out[name] * factor).astype(out[name].dtype)
    return out
```

```python
import concourse.bass as bass
from concourse import mybir
from contextlib import ExitStack

F32 = mybir.dt.float32
BF16 = mybir.dt.bfloat16
FP16 = mybir.dt.float16
I32 = mybir.dt.int32
U32 = mybir.dt.uint32
ALU = mybir.AluOpType
ACT = mybir.ActivationFunctionType
AX = mybir.AxisListType
ds = bass.ds


def graph_layer_kernel(nc, x, src, dst, W0, b0, W1, b1, W2, b2, Wf, bf, Wqkv, Wout, gamma,
                       U_i, V_i, b_i, U_f, V_f, b_f, U_c, V_c, b_c, U_o, V_o, b_o, out):
    P = nc.NUM_PARTITIONS
    N, D = x.shape
    E = src.shape[0]
    KH = D // P
    NT = -(-N // P)
    NP = NT * P
    LAST = N - (NT - 1) * P
    HEADS, DH = 8, 32
    SCALE = DH ** -0.5
    EPS = 1e-5
    LAYERS = 3

    G, CAP = 16, 4
    NG = 2 * (-(-N // (2 * G)))
    ND = NG * G
    COMB = NT * G
    OFF = COMB // 2
    ET = -(-E // P)
    EB = -(-ET // P)
    EL = E - (ET - 1) * P
    ETP = ET + CAP + 1
    CW = 512
    CHUNKS = [(c, min(CW, ND - c)) for c in range(0, ND, CW)]

    CH, L, UN = 64, 40, 8
    USED = -(-N // L)
    WARM = 6
    TOL = 2.0 ** -16
    GW = KH * CH
    assert CH * L == NP

    y_dram = nc.dram_tensor("y_dram", (NP, 3 * D), BF16, kind="Internal").ap()

    ctx = ExitStack()
    with ctx:
        def sb(name, shape, dt):
            return ctx.enter_context(nc.sbuf_tensor(name, shape, dt))

        def sem(name):
            return ctx.enter_context(nc.semaphore(name))

        ps = [ctx.enter_context(nc.psum_tensor(f"bank{i}", [P, 512], F32)) for i in range(8)]

        X = sb("X", [P, NT, D], F32)
        hT = sb("hT", [P, KH, NP], F32)
        AT = sb("AT", [P, NT, ND], BF16)
        Yp = sb("Yp", [P, NT, 3, D], BF16)
        rz = sb("rz", [P, ND + ND // 2], F32)
        inv = rz[:, 0:ND]
        some = rz[:, ND:ND + ND // 2].bitcast(BF16)
        Wcat = sb("Wcat", [P, 2, KH, 2 * D], F32)
        Wd = sb("Wd", [P, 2, KH, D], F32)
        tmp = sb("tmp", [P, KH, CW], F32)
        ident = sb("ident", [P, P], F32)
        ones_b = sb("ones_b", [P, P], BF16)
        bcol = sb("bcol", [P, LAYERS, KH], F32)
        gcol = sb("gcol", [P, 3, KH], F32)
        mean = sb("mean", [P, NT], F32)
        rstd = sb("rstd", [P, NT], F32)
        stat = sb("stat", [P, NT, 2], F32)
        bn6 = sb("bn6", [P, 2, 6], F32)
        flag = sb("flag", [1, 4], I32)
        warm = sb("warm", [1, 2], F32)

        gen_rows = sb("gen_rows", [P, 3 * D], BF16)
        gen_hot = sb("gen_hot", [P, CW], BF16)
        gen_iota = sb("gen_iota", [P, CW], I32)
        gen_src = sb("gen_src", [P, 1], U32)
        gen_dst = sb("gen_dst", [P, 1], I32)
        gen_col = sb("gen_col", [P, 1], F32)
        degree = sb("degree", [1, 4, 8], F32)

        at32 = AT[:, :, :].rearrange("p a b -> p (a b)").bitcast(F32)
        yp32 = Yp[:, :, :, :].rearrange("p a b c -> p (a b c)").bitcast(F32)
        cut = [0]

        def early(n):
            cut[0] += n
            return at32[:, cut[0] - n:cut[0]]

        wqkv = early(KH * 3 * D).rearrange("p (k n) -> p k n", k=KH)
        wout = early(KH * D).rearrange("p (k n) -> p k n", k=KH)
        gam = early(D)
        bfb = early(D)
        kmax = early(D)
        kmaxb = early(D)
        kshift = early(2 * D).rearrange("p (b n) -> p b n", b=2)
        kexp = early(2 * D).rearrange("p (b n) -> p b n", b=2)
        v1 = early(2 * KH * (P + 1)).rearrange("p (b k n) -> p b k n", b=2, k=KH)
        ctxn = early(KH * P).rearrange("p (k n) -> p k n", k=KH)
        ctxT = early(KH * P).rearrange("p (k n) -> p k n", k=KH)
        den = early(2 * KH)
        hmask = early(P)
        ctxw = early(KH * D).rearrange("p (k n) -> p k n", k=KH)
        qs = early(2 * D).rearrange("p (b n) -> p b n", b=2)
        qn = early(2 * D).rearrange("p (b n) -> p b n", b=2)
        qT = early(2 * D).rearrange("p (b k n) -> p b k n", b=2, k=KH)
        qmx = early(2 * 3 * HEADS).rearrange("p (b s h) -> p b s h", b=2, s=3)
        xn = early(2 * D).rearrange("p (b n) -> p b n", b=2)
        att = yp32[:, 0:NT * D].rearrange("p (t n) -> p t n", t=NT)

        cut2 = [0]

        def build(n32):
            cut2[0] += n32
            assert cut2[0] <= ND + ND // 2
            return rz[:, cut2[0] - n32:cut2[0]]

        onehot_u = build(2 * CAP * COMB // 2).bitcast(BF16).rearrange("p (b k n) -> p b k n", b=2, k=CAP)
        window = build(2 * 3 * CAP // 2).bitcast(BF16).rearrange("p (b s k) -> p b s k", b=2, s=3)
        bval = build(2 * CAP // 2).bitcast(BF16).rearrange("p (b k) -> p b k", b=2)
        tw = 3 * (ETP + ETP % 2) // 2
        table = build(tw + tw % 2)[:, 0:tw].bitcast(BF16).rearrange("p (s t) -> p s t", s=3)
        iota_u = sb("iota_u", [P, COMB], BF16)
        iota_b = sb("iota_b", [P, P], BF16)
        iota_g = sb("iota_g", [P, NG + 2], BF16)
        starts = sb("starts", [1, NG + 2], I32)
        onehot_b = tmp[:, :, :].rearrange("p k n -> p (k n)")[:, 0:2 * CAP * P // 2] \
            .bitcast(BF16).rearrange("p (b k n) -> p b k n", b=2, k=CAP)
        wd32 = Wd[:, :, :, :].rearrange("p a k n -> p (a k n)")
        raw = Wcat[:, :, :, :].rearrange("p a k n -> p (a k n)")
        sraw = raw[:, 0:EB * P].bitcast(I32).rearrange("p (b e) -> p b e", b=EB)
        draw = raw[:, EB * P:2 * EB * P].bitcast(I32).rearrange("p (b e) -> p b e", b=EB)
        f_i = raw[:, 2 * EB * P:3 * EB * P].bitcast(I32).rearrange("p (b e) -> p b e", b=EB)
        f_j = raw[:, 3 * EB * P:4 * EB * P].bitcast(I32).rearrange("p (b e) -> p b e", b=EB)
        fields = wd32[:, 0:EB * P].rearrange("p (b e) -> p b e", b=EB)
        fields2 = wd32[:, EB * P:2 * EB * P].rearrange("p (b e) -> p b e", b=EB)
        less = yp32[:, NT * D:NT * D + EB * (NG + 2)].rearrange("p (b g) -> p b g", b=EB)
        fields3 = yp32[:, NT * D + EB * (NG + 2):NT * D + EB * (NG + 2) + EB * P] \
            .rearrange("p (b e) -> p b e", b=EB)
        iota_16 = yp32[:, NT * D + 1000:NT * D + 1000 + NG + 2]
        first = yp32[:, NT * D + 1200:NT * D + 1200 + EB]
        onef = yp32[:, NT * D + 1210:NT * D + 1211]
        iota_i = yp32[:, NT * D + 1220:NT * D + 1220 + COMB].bitcast(I32)

        xg = at32[:, 0:(L + 1) * 3 * GW].rearrange("p (t n) -> p t n", t=L + 1)
        o1 = (L + 1) * 3 * GW
        hist = at32[:, o1:o1 + KH * (CH * L + 1)].rearrange("p (k n) -> p k n", k=KH)
        assert o1 + KH * (CH * L + 1) <= NT * ND // 2
        Ucat = Wcat[:, :, :, :].rearrange("p a k n -> p (a k n)")[:, 0:KH * 3 * D] \
            .rearrange("p (k n) -> p k n", k=KH)
        Vraw = rz[:, 0:KH * 3 * D].rearrange("p (k n) -> p k n", k=KH)
        Vhi = rz[:, KH * 3 * D:KH * 3 * D + KH * 3 * D // 2].bitcast(FP16) \
            .rearrange("p (k n) -> p k n", k=KH)
        Vlo = wd32[:, 0:KH * 3 * D // 2].bitcast(FP16).rearrange("p (k n) -> p k n", k=KH)
        xn2 = yp32[:, 0:2 * D].rearrange("p (b n) -> p b n", b=2)

        st = yp32[:, 2 * D:]
        cell = st[:, 0:2 * GW].rearrange("p (b n) -> p b n", b=2)
        cell0 = st[:, 2 * GW:3 * GW]
        h0 = st[:, 14 * GW:15 * GW]
        hc = st[:, 3 * GW:4 * GW]
        ig = st[:, 4 * GW:5 * GW]
        tc = st[:, 5 * GW:6 * GW]
        gates = st[:, 6 * GW:9 * GW].rearrange("p (s n) -> p s n", s=3)
        diff = st[:, 9 * GW:11 * GW].rearrange("p (b k c) -> p b k c", b=2, k=KH)
        moved = st[:, 11 * GW:11 * GW + 2]
        h_hi = st[:, 12 * GW:13 * GW].bitcast(FP16).rearrange("p (b n) -> p b n", b=2)
        h_lo = st[:, 13 * GW:14 * GW].bitcast(FP16).rearrange("p (b n) -> p b n", b=2)

        names = """x_loaded x_last_loaded wmix_loaded mixvec_loaded edges_loaded edge_tail_loaded
        bias_loaded
        const_ready iota_ready x_bn x_stat var_done std_done rstd_done xn_ready xt_done xt_copied
        k_done kmax_done kmaxb_ready kv_done kshift_done kexp_done v_copied v_ones ctx_done
        ctx_den ctx_norm ctx_tr ctx_trc ctxw_done ctxw_copied
        q_done qmax_done qsub_done qexp_done qsum_done qrec_done qn_done qt_done qt_copied
        att_done att_copied att_bn att_stats att_std att_rstd att_n att_g att_added bf_added
        raw_set field_step first_ready less_done starts_sum starts_f starts_done fields_tr table_done
        fields_f
        window_ready bval_ready ohu_ready ohb_ready counts_done counts_stored
        cnt_done inv_a inv_done some_done
        wd_done y_done y_hi res_done y_mid y_lo cat_added agg_done u_done t1_done t2_done t3_done h_done
        mean2_done
        std2_done rstd2_done x2_bn x2_stat xn2_ready xt2_done xt2_copied
        u_loaded v_loaded gb_loaded g_done g_stored g_wrap v_hi v_lo st_init
        cg_done ci_done co_done gg_done gi_done go_done hc_done ig_done c_done tc_done hhi_done h_f32
        hlo_done end_diff end_total end_max end_tr end_flag shift_c shift_h
verdict_seen gen_loaded gen_cols gen_hots gen_used y_stored gen_iota_ready deg_part deg_all deg_ok graph_flag scan_done ht_done y_added out_stored warm_done""".split()
        S = {n: sem(n) for n in names}
        for l_ in range(LAYERS + 1):
            for n_ in ("gen_edges", "gen_gathered"):
                S[n_, l_] = sem(f"{n_}{l_}")
            for n_ in ("wcat_loaded", "wf_loaded", "wd_loaded"):
                S[n_, l_] = sem(f"{n_}{l_}")

        block = ctx.enter_context(nc.Block())

        def col(t):
            return slice(t * P, (t + 1) * P)

        NC = len(CHUNKS)

        def edge_tiles(eng, body):
            body(0, P, True, False)
            with eng.Fori(1, ET - 1) as t:
                body(t, P, False, False)
            body(ET - 1, EL, False, True)

        def rounds(eng, steps, after):
            with eng.Fori(0, WARM) as r:
                steps(r)
                after(r, None)
            steps(WARM)
            after(WARM, 1)
            eng.wait_ge(S["end_flag"], 1)
            moving = eng.value_load(flag[0:1, 0:1], min_val=0, max_val=1)
            with eng.If(moving > 0):
                with eng.Fori(0, USED - WARM - 1) as r:
                    still = eng.value_load(flag[0:1, 0:1], min_val=0, max_val=1)
                    with eng.If(still > 0):
                        steps(r + (WARM + 1))
                        after(r + (WARM + 1), r + 2)
                        eng.wait_ge(S["end_flag"], r + 2)
                        eng.sem_inc(S["verdict_seen"], 1)
                    eng.nop()
                eng.nop()
            eng.nop()

        @block.sync
        def _(sp):
            sp.wait_ge(S["const_ready"], 1)
            full = x[0:(NT - 1) * P, :].rearrange("(t p) d -> p t d", p=P)
            sp.dma_start(X[:, 0:NT - 1, :], full).then_inc(S["x_loaded"], 16)
            sp.dma_start(X[0:LAST, NT - 1, :], x[(NT - 1) * P:N, :]).then_inc(S["x_last_loaded"], 16)
            sp.dma_start(wqkv, Wqkv.rearrange("(k p) n -> p k n", p=P)).then_inc(S["wmix_loaded"], 16)
            sp.dma_start(wout, Wout.rearrange("(k p) n -> p k n", p=P)).then_inc(S["wmix_loaded"], 16)
            sp.dma_start(gam, gamma.partition_broadcast(P)).then_inc(S["mixvec_loaded"], 16)
            sp.dma_start(bfb, bf.partition_broadcast(P)).then_inc(S["mixvec_loaded"], 16)
            with nc.allow_non_contiguous_dma("short bias columns"):
                for l, b in enumerate((b0, b1, b2)):
                    sp.dma_start(bcol[:, l, :], b.rearrange("(k p) -> p k", p=P)).then_inc(S["bias_loaded"], 16)
                for g, b in enumerate((b_i, b_c, b_o)):
                    sp.dma_start(gcol[:, g, :], b.rearrange("(k p) -> p k", p=P)).then_inc(S["gb_loaded"], 16)
            sp.wait_ge(S["raw_set"], 2)
            for raw_, e in ((sraw, src), (draw, dst)):
                full_b = (ET - 1) // P
                sp.dma_start(raw_[:, 0:full_b, :], e[0:full_b * P * P].rearrange("(b p e) -> p b e", p=P, e=P)) \
                    .then_inc(S["edges_loaded"], 16)
                rest = ET - 1 - full_b * P
                sp.dma_start(raw_[0:rest, full_b, :],
                             e[full_b * P * P:(ET - 1) * P].rearrange("(p e) -> p e", e=P)) \
                    .then_inc(S["edges_loaded"], 16)
                sp.dma_start(raw_[rest:rest + 1, full_b, 0:EL],
                             e[(ET - 1) * P:E].rearrange("(p e) -> p e", p=1)).then_inc(S["edges_loaded"], 16)
            Ws = (W0, W1, W2)
            for l in range(LAYERS + 1):
                if l == 0:
                    sp.wait_ge(S["fields_tr"], 9)
                if l >= 2:
                    sp.wait_ge(S["y_done"], NT * (l - 1))
                if l < LAYERS:
                    sp.dma_start(Wcat[:, l % 2, :, 0:D], Ws[l][D:2 * D, :].rearrange("(k p) n -> p k n", p=P)) \
                        .then_inc(S["wcat_loaded", l], 16)
                sp.dma_start(Wcat[:, l % 2, :, D:2 * D],
                             Wf[l * D:(l + 1) * D, :].rearrange("(k p) n -> p k n", p=P)) \
                    .then_inc(S["wf_loaded", l], 16)
                if l < LAYERS:
                    if l >= 2:
                        sp.wait_ge(S["u_done"], len(CHUNKS) * (l - 1))
                    sp.dma_start(Wd[:, l % 2, :, :], Ws[l][0:D, :].rearrange("(k p) n -> p k n", p=P)) \
                        .then_inc(S["wd_loaded", l], 16)
            sp.wait_ge(S["y_done"], NT * (LAYERS + 1))
            for g, u in enumerate((U_i, U_c, U_o)):
                sp.dma_start(Ucat[:, :, g * D:(g + 1) * D], u.rearrange("(k p) n -> p k n", p=P)) \
                    .then_inc(S["u_loaded"], 16)
            sp.wait_ge(S["h_done"], LAYERS * len(CHUNKS) * KH)
            for g, v in enumerate((V_i, V_c, V_o)):
                sp.dma_start(Vraw[:, :, g * D:(g + 1) * D], v.rearrange("(k p) n -> p k n", p=P)) \
                    .then_inc(S["v_loaded"], 16)
            for t in range(0, NT - 1, 4):
                n = min(4, NT - 1 - t)
                sp.wait_ge(S["y_added"], t + n)
                sp.dma_start(out[t * P:(t + n) * P, :].rearrange("(t p) d -> p t d", p=P),
                             X[:, t:t + n, :]).then_inc(S["out_stored"], 16)
            sp.wait_ge(S["y_added"], NT)
            sp.dma_start(out[(NT - 1) * P:N, :], X[0:LAST, NT - 1, :]).then_inc(S["out_stored"], 16)
            sp.wait_ge(S["out_stored"], 16 * (-(-(NT - 1) // 4) + 1))

        @block.gpsimd
        def _(pool):
            nc.gpsimd.memset(ident[:, :], 0.0).then_inc(S["iota_ready"], 1)
            nc.gpsimd.memset(hmask, 1.0).then_inc(S["iota_ready"], 1)
            nc.gpsimd.memset(ones_b[:, :], 1.0)
            nc.gpsimd.memset(onef, 1.0)
            pool.wait_ge(S["iota_ready"], 2)
            nc.gpsimd.affine_select(out=ident[:, :], in_=ident[:, :], compare_op=ALU.not_equal, fill=1.0,
                                    base=0, pattern=[[-1, P]], channel_multiplier=1).then_inc(S["iota_ready"], 1)
            hm = hmask.rearrange("p (h c) -> p h c", c=DH)
            nc.gpsimd.affine_select(out=hm, in_=hm, compare_op=ALU.is_ge, fill=0.0,
                                    base=0, pattern=[[-DH, P // DH], [0, DH]], channel_multiplier=1) \
                .then_inc(S["iota_ready"], 1)
            pool.wait_ge(S["iota_ready"], 4)
            nc.gpsimd.affine_select(out=hm, in_=hm, compare_op=ALU.is_ge, fill=0.0,
                                    base=DH - 1, pattern=[[DH, P // DH], [0, DH]], channel_multiplier=-1) \
                .then_inc(S["iota_ready"], 1)
            nc.gpsimd.iota(iota_i, [[1, COMB]], base=0, channel_multiplier=0).then_inc(S["iota_ready"], 1)
            pool.wait_ge(S["iota_ready"], 6)
            nc.gpsimd.tensor_scalar(iota_u[:, :], iota_i, 1.0, -float(OFF), ALU.mult, ALU.add) \
                .then_inc(S["iota_ready"], 1)
            nc.gpsimd.tensor_scalar(iota_b[:, :], iota_i[:, 0:P], 1.0, 1.0, ALU.mult, ALU.add) \
                .then_inc(S["iota_ready"], 1)
            nc.gpsimd.tensor_scalar(iota_g[:, :], iota_i[:, 0:NG + 2], 1.0, 0.0, ALU.mult, ALU.add) \
                .then_inc(S["iota_ready"], 1)
            nc.gpsimd.tensor_scalar(iota_16, iota_i[:, 0:NG + 2], float(G), 0.0, ALU.mult, ALU.add) \
                .then_inc(S["iota_ready"], 1)

            pool.wait_ge(S["kmax_done"], NT + 1)
            nc.gpsimd.partition_all_reduce(kmaxb, kmax, P, bass.bass_isa.ReduceOp.max) \
                .then_inc(S["kmaxb_ready"], 1)

            pool.wait_ge(S["table_done"], 4)
            pool.wait_ge(S["starts_done"], 1)
            with pool.Fori(0, NG // 2) as j:
                for b in range(2):
                    g = j * 2 + b
                    start = pool.value_load(starts[0:1, ds(g, 1)], min_val=0, max_val=ET - 1)
                    pool.wait_ge(S["ohu_ready"], g + 2)
                    nc.gpsimd.tensor_copy(window[:, b], table[:, :, ds(start, CAP)]) \
                        .then_inc(S["window_ready"], 1)


            nc.gpsimd.iota(gen_iota[:, :], [[1, CW]], base=0, channel_multiplier=0) \
                .then_inc(S["gen_iota_ready"], 1)
            pool.wait_ge(S["graph_flag"], 1)
            exact = pool.value_load(flag[0:1, 1:2], min_val=0, max_val=1)

            def load_edges(p, gather):
                def body(t, rows, first, last):
                    n = p * ET + t
                    pool.wait_ge(S["gen_used"], n + 1)
                    if rows == P:
                        s_, d_ = src[ds(t * P, P)], dst[ds(t * P, P)]
                    else:
                        s_, d_ = src[(ET - 1) * P:E], dst[(ET - 1) * P:E]
                    pool.dma_start(gen_src[0:rows, :], s_.bitcast(U32).rearrange("(p o) -> p o", o=1)) \
                        .then_inc(S["gen_edges", p // NC], 16)
                    pool.dma_start(gen_dst[0:rows, :], d_.rearrange("(p o) -> p o", o=1)) \
                        .then_inc(S["gen_edges", p // NC], 16)
                    if gather:
                        pool.wait_ge(S["gen_edges", p // NC], (t + (p % NC * ET + 1)) * 32)
                        pool.sem_inc(S["gen_loaded"], 1)
                        nc.gpsimd.indirect_dma_start(
                            out=gen_rows[0:rows, :], out_offset=None, in_=y_dram[:, :],
                            in_offset=bass.IndirectOffsetOnAxis(ap=gen_src[0:rows, 0:1], axis=0)) \
                            .then_inc(S["gen_gathered", p // NC], 16)

                with nc.allow_non_contiguous_dma("edges to partitions"):
                    edge_tiles(pool, body)

            with pool.If(exact < 1):
                for c in range(NC):
                    load_edges(c, False)
                for l in range(LAYERS):
                    pool.wait_ge(S["y_lo"], (l + 1) * NT)
                    pool.dma_start(y_dram.rearrange("(s p) m -> p s m", p=P),
                                   Yp[:, :, :, :].rearrange("p s a m -> p s (a m)")).then_inc(S["y_stored"], 16)
                    pool.wait_ge(S["y_stored"], 16 * (l + 1))
                    for c in range(NC):
                        load_edges((l + 1) * NC + c, True)
                pool.nop()
            pool.nop()

        @block.scalar
        def _(act):
            def transposed_copies(done, copied, dest):
                for t in range(NT):
                    act.wait_ge(S[done], t + 1)
                    nc.scalar.copy(dest[:, :, col(t)], ps[t % 2][:, 0:D].rearrange("p (k n) -> p k n", k=KH)) \
                        .then_inc(S[copied], 1)

            act.wait_ge(S["var_done"], 1)
            nc.scalar.activation(rstd[:, :], mean[:, :], ACT.Sqrt).then_inc(S["std_done"], 1)
            transposed_copies("xt_done", "xt_copied", hT)

            for t in range(NT):
                rows = LAST if t == NT - 1 else P
                act.wait_ge(S["kv_done"], t + 1)
                act.wait_ge(S["v_ones"], 1)
                if t >= 2:
                    act.wait_ge(S["ctx_done"], t - 1)
                nc.scalar.copy(v1[0:rows, t % 2, :, 0:P],
                               ps[4 + t % 2][0:rows, 0:D].rearrange("p (k n) -> p k n", k=KH)) \
                    .then_inc(S["v_copied"], 1)
                act.wait_ge(S["kshift_done"], t + 1)
                nc.scalar.activation(kexp[0:rows, t % 2], kshift[0:rows, t % 2], ACT.Exp) \
                    .then_inc(S["kexp_done"], 1)
            act.wait_ge(S["ctx_tr"], 1)
            nc.scalar.copy(ctxT, ps[4][:, 0:D].rearrange("p (k n) -> p k n", k=KH)).then_inc(S["ctx_trc"], 1)
            act.wait_ge(S["ctxw_done"], 1)
            nc.scalar.copy(ctxw, ps[5][:, :].rearrange("p (k n) -> p k n", k=KH)).then_inc(S["ctxw_copied"], 1)
            for t in range(-1, NT):
                if t + 1 < NT:
                    act.wait_ge(S["qsub_done"], t + 2)
                    nc.scalar.activation(qs[:, (t + 1) % 2], qs[:, (t + 1) % 2], ACT.Exp) \
                        .then_inc(S["qexp_done"], 1)
                if t >= 0:
                    act.wait_ge(S["qt_done"], t + 1)
                    nc.scalar.copy(qT[:, t % 2], ps[6][:, 0:D].rearrange("p (k n) -> p k n", k=KH)) \
                        .then_inc(S["qt_copied"], 1)
                    act.wait_ge(S["att_done"], t + 1)
                    nc.scalar.copy(att[:, t, :], ps[7][:, 0:D]).then_inc(S["att_copied"], 1)
            act.wait_ge(S["att_stats"], NT + 1)
            nc.scalar.activation(rstd[:, :], mean[:, :], ACT.Sqrt).then_inc(S["att_std"], 1)

            act.sem_inc(S["counts_stored"], 2)
            with act.Fori(0, NG // 2) as j:
                for b in range(2):
                    g = j * 2 + b
                    act.wait_ge(S["counts_done"], g + 3)
                    nc.scalar.copy(AT[:, :, ds(g * G, G)],
                                   ps[2 + b][:, 0:COMB].rearrange("p (a n) -> p a n", n=G)) \
                        .then_inc(S["counts_stored"], 1)

            for l in range(LAYERS):
                for t in range(NT):
                    n = l * NT + t
                    act.wait_ge(S["y_done"], n + 1)
                    nc.scalar.copy(Yp[:, t, 0, :], ps[t % 2][:, 0:D]).then_inc(S["y_hi"], 1)
                    act.wait_ge(S["res_done"], n + 1)
                    nc.scalar.copy(Yp[:, t, 1, :], tmp[:, t % 2, 0:D]).then_inc(S["y_mid"], 1)
                for c, (c0, w) in enumerate(CHUNKS):
                    for k in range(KH):
                        n = (l * len(CHUNKS) + c) * KH + k
                        act.wait_ge(S["t3_done"], n + 1)
                        act.wait_ge(S["u_done"], l * len(CHUNKS) + c + 1)
                        nc.scalar.activation(hT[:, k, c0:min(c0 + w, NP)], tmp[:, k, 0:min(w, NP - c0)],
                                             ACT.Relu).then_inc(S["h_done"], 1)

            act.wait_ge(S["mean2_done"], 1)
            nc.scalar.activation(rstd[:, :], mean[:, :], ACT.Sqrt).then_inc(S["std2_done"], 1)
            transposed_copies("xt2_done", "xt2_copied", hT)

            TW = 8 * L
            act.wait_ge(S["gb_loaded"], 48)
            for s in range(NP // TW):
                for b in range(3 * KH):
                    n = s * 3 * KH + b
                    act.wait_ge(S["g_done"], n + 1)
                    dest = xg[:, 0:L, b * CH + 8 * s:b * CH + 8 * s + 8].rearrange("p t c -> p c t")
                    nc.scalar.activation(dest, ps[n % 4][:, 0:TW].rearrange("p (c t) -> p c t", c=8),
                                         ACT.Identity, bias=gcol[:, b // KH, b % KH:b % KH + 1]) \
                        .then_inc(S["g_stored"], 1)
            act.wait_ge(S["warm_done"], 1)
            nc.scalar.activation(warm[:, 0:1], warm[:, 1:2], ACT.Sigmoid)

            def steps(r):
                with act.Fori(0, L // UN) as j:
                    n = r * L + j * UN
                    for u in range(UN):
                        act.wait_ge(S["cg_done"], n + (u + 1))
                        nc.scalar.activation(gates[:, 1], ps[2 + u % 2][:, 0:GW], ACT.Tanh) \
                            .then_inc(S["gg_done"], 1)
                        act.wait_ge(S["ci_done"], n + (u + 1))
                        nc.scalar.activation(gates[:, 0], ps[u % 2][:, 0:GW], ACT.Sigmoid) \
                            .then_inc(S["gi_done"], 1)
                        act.wait_ge(S["co_done"], n + (u + 1))
                        nc.scalar.activation(gates[:, 2], ps[4 + u % 2][:, 0:GW], ACT.Sigmoid) \
                            .then_inc(S["go_done"], 1)
                        act.wait_ge(S["c_done"], n + (u + 1))
                        nc.scalar.activation(tc, cell[:, (u + 1) % 2], ACT.Tanh).then_inc(S["tc_done"], 1)

            rounds(act, steps, lambda r, look: None)

        @block.vector
        def _(dve):
            nc.vector.memset(X[:, NT - 1, :], 0.0).then_inc(S["const_ready"], 1)
            nc.vector.memset(sraw, 0).then_inc(S["raw_set"], 1)
            nc.vector.memset(draw, 1 << 20).then_inc(S["raw_set"], 1)
            nc.vector.memset(kmax, -3.0e38).then_inc(S["kmax_done"], 1)
            nc.vector.memset(v1, 1.0).then_inc(S["v_ones"], 1)

            def norm_stats(data, ready, done, stats):
                for t in range(NT):
                    ready(t)
                    if t >= 2:
                        dve.wait_ge(S[stats], t - 1)
                    nc.vector.bn_stats(bn6[:, t % 2, :], data[:, t, :]).then_inc(S[done], 1)
                    dve.wait_ge(S[done], t + 1)
                    nc.vector.bn_aggr(stat[:, t, :], bn6[:, t % 2, :]).then_inc(S[stats], 1)
                dve.wait_ge(S[stats], NT)

            def x_ready(t):
                if t == 0:
                    dve.wait_ge(S["x_loaded"], 16)
                if t == NT - 1:
                    dve.wait_ge(S["x_last_loaded"], 16)

            norm_stats(X, x_ready, "x_bn", "x_stat")
            nc.vector.tensor_scalar(mean[:, :], stat[:, :, 1], EPS, None, ALU.add).then_inc(S["var_done"], 1)
            dve.wait_ge(S["std_done"], 1)
            nc.vector.reciprocal(rstd[:, :], rstd[:, :]).then_inc(S["rstd_done"], 1)
            dve.wait_ge(S["rstd_done"], 1)
            for t in range(NT):
                if t >= 2:
                    dve.wait_ge(S["xt_done"], t - 1)
                nc.vector.tensor_scalar(xn[:, t % 2], X[:, t, :], stat[:, t, 0:1], rstd[:, t:t + 1],
                                        ALU.subtract, ALU.mult).then_inc(S["xn_ready"], 1)

            for t in range(NT):
                rows = LAST if t == NT - 1 else P
                dve.wait_ge(S["k_done"], t + 1)
                dve.wait_ge(S["kmax_done"], t + 1)
                nc.vector.tensor_tensor(kmax[0:rows], ps[2 + t % 2][0:rows, 0:D], kmax[0:rows], ALU.max) \
                    .then_inc(S["kmax_done"], 1)
            dve.wait_ge(S["kmaxb_ready"], 1)
            for t in range(NT):
                rows = LAST if t == NT - 1 else P
                dve.wait_ge(S["kv_done"], t + 1)
                if t >= 2:
                    dve.wait_ge(S["kexp_done"], t - 1)
                nc.vector.tensor_tensor(kshift[0:rows, t % 2], ps[t % 2][0:rows, 0:D], kmaxb[0:rows],
                                        ALU.subtract).then_inc(S["kshift_done"], 1)
            dve.wait_ge(S["ctx_done"], NT)
            dve.wait_ge(S["iota_ready"], 5)
            for k in range(KH):
                nc.vector.reciprocal(den[:, 2 * k:2 * k + 1], ps[2 + k][:, P:P + 1]).then_inc(S["ctx_den"], 1)
                dve.wait_ge(S["ctx_den"], 2 * k + 1)
                nc.vector.tensor_scalar(den[:, 2 * k + 1:2 * k + 2], den[:, 2 * k:2 * k + 1], SCALE, None,
                                        ALU.mult).then_inc(S["ctx_den"], 1)
                dve.wait_ge(S["ctx_den"], 2 * k + 2)
                nc.vector.scalar_tensor_tensor(out=ctxn[:, k, :], in0=ps[2 + k][:, 0:P],
                                               scalar=den[:, 2 * k + 1:2 * k + 2], in1=hmask,
                                               op0=ALU.mult, op1=ALU.mult).then_inc(S["ctx_norm"], 1)
            for t in range(NT):
                b = t % 2
                mx, sm, rc = (qmx[:, b, i, :] for i in range(3))
                dve.wait_ge(S["q_done"], t + 1)
                q3 = ps[b][:, 0:D].rearrange("p (h c) -> p h c", c=DH)
                s3 = qs[:, b].rearrange("p (h c) -> p h c", c=DH)
                n3 = qn[:, b].rearrange("p (h c) -> p h c", c=DH)
                nc.vector.tensor_reduce(mx, q3, AX.X, ALU.max).then_inc(S["qmax_done"], 1)
                dve.wait_ge(S["qmax_done"], t + 1)
                if t >= 2:
                    dve.wait_ge(S["qn_done"], t - 1)
                nc.vector.tensor_tensor(s3, q3, mx.unsqueeze(2).to_broadcast([P, HEADS, DH]), ALU.subtract) \
                    .then_inc(S["qsub_done"], 1)
                dve.wait_ge(S["qexp_done"], t + 1)
                nc.vector.tensor_reduce(sm, s3, AX.X, ALU.add).then_inc(S["qsum_done"], 1)
                dve.wait_ge(S["qsum_done"], t + 1)
                nc.vector.reciprocal(rc, sm).then_inc(S["qrec_done"], 1)
                dve.wait_ge(S["qrec_done"], t + 1)
                if t >= 2:
                    dve.wait_ge(S["qt_done"], t - 1)
                nc.vector.tensor_tensor(n3, s3, rc.unsqueeze(2).to_broadcast([P, HEADS, DH]), ALU.mult) \
                    .then_inc(S["qn_done"], 1)
            norm_stats(att, lambda t: dve.wait_ge(S["att_copied"], t + 1), "att_bn", "att_stats")
            nc.vector.tensor_scalar(mean[:, :], stat[:, :, 1], EPS, None, ALU.add).then_inc(S["att_stats"], 1)
            dve.wait_ge(S["att_std"], 1)
            nc.vector.reciprocal(rstd[:, :], rstd[:, :]).then_inc(S["att_rstd"], 1)
            dve.wait_ge(S["att_rstd"], 1)
            dve.wait_ge(S["mixvec_loaded"], 32)
            for t in range(NT):
                nc.vector.tensor_tensor(X[:, t, :], X[:, t, :], bfb, ALU.add).then_inc(S["bf_added"], 1)
                nc.vector.tensor_scalar(att[:, t, :], att[:, t, :], stat[:, t, 0:1], rstd[:, t:t + 1],
                                        ALU.subtract, ALU.mult).then_inc(S["att_n"], 1)
                dve.wait_ge(S["att_n"], t + 1)
                nc.vector.tensor_tensor(att[:, t, :], att[:, t, :], gam, ALU.mult).then_inc(S["att_g"], 1)
                dve.wait_ge(S["att_g"], t + 1)
                dve.wait_ge(S["bf_added"], t + 1)
                nc.vector.tensor_tensor(X[:, t, :], X[:, t, :], att[:, t, :], ALU.add) \
                    .then_inc(S["att_added"], 1)

            done = [0]

            def step(ins):
                done[0] += 1
                ins.then_inc(S["field_step"], 1)
                dve.wait_ge(S["field_step"], done[0])

            dve.wait_ge(S["edges_loaded"], 96)
            log_p, log_g = P.bit_length() - 1, G.bit_length() - 1
            nc.vector.tensor_copy(first, draw[:, :, 0]).then_inc(S["first_ready"], 1)
            step(nc.vector.tensor_scalar(f_i, sraw, log_p, log_g, ALU.arith_shift_right, ALU.arith_shift_left))
            step(nc.vector.tensor_scalar(f_j, draw, G - 1, None, ALU.bitwise_and))
            step(nc.vector.tensor_tensor(f_i, f_i, f_j, ALU.bitwise_or))
            nc.vector.tensor_copy(fields, f_i).then_inc(S["fields_f"], 1)
            step(nc.vector.tensor_scalar(f_j, sraw, P - 1, None, ALU.bitwise_and))
            nc.vector.tensor_copy(fields2, f_j).then_inc(S["fields_f"], 1)
            dve.wait_ge(S["fields_f"], 2)
            step(nc.vector.tensor_scalar(f_i, draw, log_g, None, ALU.arith_shift_right))
            nc.vector.tensor_copy(fields3, f_i).then_inc(S["fields_f"], 1)
            dve.wait_ge(S["first_ready"], 1)
            dve.wait_ge(S["iota_ready"], 10)
            for b in range(EB):
                nc.vector.tensor_scalar(less[:, b, :], iota_16, first[:, b:b + 1], None, ALU.is_gt) \
                    .then_inc(S["less_done"], 1)
            dve.wait_ge(S["starts_sum"], 1)
            step(nc.vector.tensor_scalar(tmp[0:1, 0, 0:NG + 2], ps[0][0:1, 0:NG + 2], -1.0, 0.0,
                                         ALU.add, ALU.max))
            nc.vector.tensor_copy(starts[:, :], tmp[0:1, 0, 0:NG + 2]).then_inc(S["starts_done"], 1)
            nc.vector.memset(table, -1.0).then_inc(S["table_done"], 1)
            dve.wait_ge(S["table_done"], 1)
            for s, (m, a) in enumerate(((1.0, -float(OFF)), (1.0, 1.0), (1.0, 0.0))):
                dve.wait_ge(S["fields_tr"], EB * (s + 1))
                nc.vector.tensor_scalar(table[:, s, 0:ET], ps[4 + s][:, 0:ET], m, a, ALU.mult, ALU.add) \
                    .then_inc(S["table_done"], 1)

            dve.wait_ge(S["starts_done"], 1)
            nc.vector.memset(window, 0.0).then_inc(S["ohu_ready"], 2)
            with dve.Fori(0, NG // 2) as j:
                for b in range(2):
                    g = j * 2 + b
                    dve.wait_ge(S["window_ready"], g + 1)
                    nc.vector.scalar_tensor_tensor(out=bval[:, b], in0=window[:, b, 2, :],
                                                   scalar=iota_g[:, ds(g, 1)], in1=window[:, b, 1, :],
                                                   op0=ALU.is_equal, op1=ALU.mult).then_inc(S["bval_ready"], 1)
                    dve.wait_ge(S["counts_done"], g + 1)
                    dve.wait_ge(S["bval_ready"], g + 1)
                    for k in range(CAP):
                        ins = nc.vector.tensor_scalar(onehot_b[:, b, k, :], iota_b[:, :], bval[:, b, k:k + 1], None,
                                                      ALU.is_equal)
                    ins.then_inc(S["ohb_ready"], 1)
                    for k in range(CAP):
                        ins = nc.vector.tensor_scalar(onehot_u[:, b, k, :], iota_u[:, :],
                                                      window[:, b, 0, k:k + 1], None, ALU.is_equal)
                    ins.then_inc(S["ohu_ready"], 1)

            def from_degrees(c, n):
                c0, w = CHUNKS[c]
                dve.wait_ge(S["cnt_done"], n)
                bank = ps[4 + c % 2]
                nc.vector.tensor_scalar(tmp[:, c % 2, 0:w], bank[:, 0:w], 1.0, None, ALU.max) \
                    .then_inc(S["inv_a"], 1)
                nc.vector.tensor_scalar(some[:, c0:c0 + w], bank[:, 0:w], 1.0, None, ALU.min) \
                    .then_inc(S["some_done"], 1)
                dve.wait_ge(S["inv_a"], n)
                nc.vector.reciprocal(inv[:, c0:c0 + w], tmp[:, c % 2, 0:w]).then_inc(S["inv_done"], 1)

            dve.wait_ge(S["counts_stored"], NG + 2)
            for c, (c0, w) in enumerate(CHUNKS):
                dve.wait_ge(S["cnt_done"], c + 1)
                nc.vector.tensor_reduce(degree[:, 0, c:c + 1], ps[4 + c % 2][0:1, 0:w], AX.X, ALU.add) \
                    .then_inc(S["deg_part"], 1)
                nc.vector.tensor_reduce(degree[:, 1, c:c + 1], ps[4 + c % 2][0:1, 0:w], AX.X, ALU.max) \
                    .then_inc(S["deg_part"], 1)
                from_degrees(c, c + 1)
            dve.wait_ge(S["deg_part"], 2 * NC)
            nc.vector.tensor_reduce(degree[:, 2, 0:1], degree[:, 0, 0:NC], AX.X, ALU.add) \
                .then_inc(S["deg_all"], 1)
            nc.vector.tensor_reduce(degree[:, 2, 1:2], degree[:, 1, 0:NC], AX.X, ALU.max) \
                .then_inc(S["deg_all"], 1)
            dve.wait_ge(S["deg_all"], 2)
            nc.vector.tensor_scalar(degree[:, 2, 2:3], degree[:, 2, 0:1], float(E), None, ALU.is_equal) \
                .then_inc(S["deg_ok"], 1)
            nc.vector.tensor_scalar(degree[:, 2, 3:4], degree[:, 2, 1:2], 256.0, None, ALU.is_lt) \
                .then_inc(S["deg_ok"], 1)
            dve.wait_ge(S["deg_ok"], 2)
            nc.vector.tensor_tensor(flag[0:1, 1:2], degree[:, 2, 2:3], degree[:, 2, 3:4], ALU.mult) \
                .then_inc(S["graph_flag"], 1)
            dve.wait_ge(S["graph_flag"], 1)
            exact = dve.value_load(flag[0:1, 1:2], min_val=0, max_val=1)

            def hot_rows(p):
                c0, w = CHUNKS[p % NC]

                def body(t, rows, first, last):
                    n = p * ET + t
                    dve.wait_ge(S["gen_edges", p // NC], (t + (p % NC * ET + 1)) * 32)
                    nc.vector.tensor_scalar(gen_col[0:rows, :], gen_dst[0:rows, :], -float(c0), None, ALU.add) \
                        .then_inc(S["gen_cols"], 1)
                    dve.wait_ge(S["gen_cols"], n + 1)
                    nc.vector.tensor_scalar(gen_hot[0:rows, 0:w], gen_iota[0:rows, 0:w], gen_col[0:rows, 0:1],
                                            None, ALU.is_equal).then_inc(S["gen_hots"], 1)

                edge_tiles(dve, body)

            with dve.If(exact < 1):
                dve.wait_ge(S["gen_iota_ready"], 1)
                for c in range(NC):
                    hot_rows(c)
                    from_degrees(c, NC + c + 1)
                dve.wait_ge(S["inv_done"], 2 * NC)
                nc.vector.memset(gen_col[:, :], 0.0)
            dve.nop()

            dve.wait_ge(S["bias_loaded"], 48)
            dve.wait_ge(S["inv_done"], len(CHUNKS))
            for l in range(LAYERS + 1):
                if l < LAYERS:
                    dve.wait_ge(S["wd_loaded", l], 16)
                    dve.wait_ge(S["wcat_loaded", l], 16)
                    nc.vector.tensor_tensor(Wd[:, l % 2], Wd[:, l % 2], Wcat[:, l % 2, :, 0:D], ALU.subtract) \
                        .then_inc(S["wd_done"], 1)
                for t in range(NT):
                    n = l * NT + t
                    if l < LAYERS:
                        dve.wait_ge(S["y_hi"], n + 1)
                        if t >= 2:
                            dve.wait_ge(S["y_lo"], n - 1)
                        nc.vector.tensor_tensor(tmp[:, t % 2, 0:D], ps[t % 2][:, 0:D], Yp[:, t, 0, :],
                                                ALU.subtract).then_inc(S["res_done"], 1)
                    else:
                        dve.wait_ge(S["y_done"], n + 1)
                    dve.wait_ge(S["att_added"], NT)
                    if l > 0:
                        dve.wait_ge(S["cat_added"], n + 1 - NT)
                    nc.vector.tensor_tensor(X[:, t, :], X[:, t, :], ps[t % 2][:, D:2 * D], ALU.add) \
                        .then_inc(S["cat_added"], 1)
                    if l < LAYERS:
                        dve.wait_ge(S["y_mid"], n + 1)
                        nc.vector.tensor_tensor(Yp[:, t, 2, :], tmp[:, t % 2, 0:D], Yp[:, t, 1, :],
                                                ALU.subtract).then_inc(S["y_lo"], 1)
                if l == LAYERS:
                    break
                dve.wait_ge(S["inv_done"], len(CHUNKS))
                for c, (c0, w) in enumerate(CHUNKS):
                    m = l * len(CHUNKS) + c
                    with dve.If(exact < 1):
                        hot_rows(NC + m)
                        dve.nop()
                    dve.wait_ge(S["agg_done"], m + 1)
                    if c:
                        dve.wait_ge(S["h_done"], m * KH)
                    else:
                        dve.wait_ge(S["y_lo"], (l + 1) * NT)
                    for k in range(KH):
                        nc.vector.tensor_tensor(tmp[:, k, 0:w], ps[(2 if c % 2 == 0 else 6) + k][:, 0:w],
                                                inv[:, c0:c0 + w], ALU.mult).then_inc(S["t1_done"], 1)
                    dve.wait_ge(S["u_done"], m + 1)
                    for k in range(KH):
                        dve.wait_ge(S["t1_done"], m * KH + k + 1)
                        nc.vector.tensor_tensor(tmp[:, k, 0:w], tmp[:, k, 0:w], ps[4 + k][:, 0:w],
                                                ALU.add).then_inc(S["t2_done"], 1)
                    for k in range(KH):
                        dve.wait_ge(S["t2_done"], m * KH + k + 1)
                        nc.vector.scalar_tensor_tensor(out=tmp[:, k, 0:w], in0=tmp[:, k, 0:w],
                                                       scalar=bcol[:, l, k:k + 1], in1=some[:, c0:c0 + w],
                                                       op0=ALU.add, op1=ALU.mult).then_inc(S["t3_done"], 1)

            dve.wait_ge(S["cat_added"], NT * (LAYERS + 1))
            norm_stats(X, lambda t: None, "x2_bn", "x2_stat")
            nc.vector.tensor_scalar(mean[:, :], stat[:, :, 1], EPS, None, ALU.add).then_inc(S["mean2_done"], 1)
            dve.wait_ge(S["std2_done"], 1)
            nc.vector.reciprocal(rstd[:, :], rstd[:, :]).then_inc(S["rstd2_done"], 1)
            dve.wait_ge(S["rstd2_done"], 1)
            for t in range(NT):
                if t >= 2:
                    dve.wait_ge(S["xt2_done"], t - 1)
                nc.vector.tensor_scalar(xn2[:, t % 2], X[:, t, :], stat[:, t, 0:1], rstd[:, t:t + 1],
                                        ALU.subtract, ALU.mult).then_inc(S["xn2_ready"], 1)

            dve.wait_ge(S["v_loaded"], 48)
            nc.vector.tensor_copy(Vhi, Vraw).then_inc(S["v_hi"], 1)
            dve.wait_ge(S["v_hi"], 1)
            nc.vector.tensor_tensor(Vlo, Vraw, Vhi, ALU.subtract).then_inc(S["v_lo"], 1)
            nc.vector.memset(warm[:, :], 0.0).then_inc(S["warm_done"], 1)
            nc.vector.memset(cell, 0.0).then_inc(S["st_init"], 1)
            nc.vector.memset(cell0, 0.0).then_inc(S["st_init"], 1)
            nc.vector.memset(h0, 0.0).then_inc(S["st_init"], 1)
            nc.vector.memset(hist, 0.0).then_inc(S["st_init"], 1)
            nc.vector.memset(h_hi, 0.0).then_inc(S["hhi_done"], 1)
            nc.vector.memset(h_lo, 0.0).then_inc(S["hlo_done"], 1)
            dve.wait_ge(S["g_stored"], (NP // (8 * L)) * 3 * KH)
            nc.vector.tensor_copy(xg[:, L, :], xg[:, 0, :]).then_inc(S["g_wrap"], 1)
            dve.wait_ge(S["st_init"], 4)

            def kc(ap):
                return ap.rearrange("p (k c) -> p k c", k=KH)

            before = hist[:, :, 0:CH * L].rearrange("p k (c t) -> p k c t", t=L)
            behind = hist[:, :, 1:CH * L + 1].rearrange("p k (c t) -> p k c t", t=L)

            def steps(r):
                with dve.Fori(0, L // UN) as j:
                    n = r * L + j * UN
                    for u in range(UN):
                        old, new = u % 2, (u + 1) % 2
                        h_old = before[:, :, :, ds(j * UN + u, 1)].rearrange("p k c t -> p k (c t)")
                        h_new = behind[:, :, :, ds(j * UN + u, 1)].rearrange("p k c t -> p k (c t)")
                        nc.vector.tensor_tensor(kc(hc), h_old, kc(cell[:, old]), ALU.mult) \
                            .then_inc(S["hc_done"], 1)
                        dve.wait_ge(S["gi_done"], n + (u + 1))
                        nc.vector.tensor_tensor(ig, gates[:, 0], gates[:, 1], ALU.mult) \
                            .then_inc(S["ig_done"], 1)
                        dve.wait_ge(S["hc_done"], n + (u + 1))
                        dve.wait_ge(S["ig_done"], n + (u + 1))
                        nc.vector.tensor_tensor(cell[:, new], hc, ig, ALU.add).then_inc(S["c_done"], 1)
                        dve.wait_ge(S["tc_done"], n + (u + 1))
                        nc.vector.tensor_tensor(h_hi[:, new], gates[:, 2], tc, ALU.mult) \
                            .then_inc(S["hhi_done"], 1)
                        nc.vector.tensor_tensor(h_new, kc(gates[:, 2]), kc(tc), ALU.mult) \
                            .then_inc(S["h_f32"], 1)
                        dve.wait_ge(S["h_f32"], n + (u + 1))
                        nc.vector.tensor_tensor(kc(h_lo[:, new]), h_new, kc(h_hi[:, new]), ALU.subtract) \
                            .then_inc(S["hlo_done"], 1)

            def after(r, look):
                dve.wait_ge(S["hlo_done"], (r + 1) * (L + 1))
                new_h, end_c = before[:, :, :, 0], kc(cell[:, 0])
                old_c = kc(cell0)
                if look is not None:
                    nc.vector.tensor_tensor(diff[:, 0, :, 1:USED], new_h[:, :, 1:USED],
                                            kc(h0)[:, :, 1:USED], ALU.subtract).then_inc(S["end_diff"], 1)
                    nc.vector.tensor_tensor(diff[:, 1, :, 1:USED], end_c[:, :, 0:USED - 1],
                                            old_c[:, :, 1:USED], ALU.subtract).then_inc(S["end_diff"], 1)
                    dve.wait_ge(S["end_diff"], look * 2)
                    nc.vector.tensor_reduce(moved[:, 0:1], diff[:, :, :, 1:USED], AX.XYZ, ALU.max,
                                            apply_absolute_value=True).then_inc(S["end_max"], 1)
                    dve.wait_ge(S["end_tr"], look)
                    nc.vector.tensor_reduce(warm[:, 0:1], ps[6][0:1, 0:P], AX.X, ALU.max) \
                        .then_inc(S["end_total"], 1)
                    dve.wait_ge(S["end_total"], look)
                    nc.vector.tensor_scalar(flag[0:1, 0:1], warm[:, 0:1], TOL, None, ALU.is_gt) \
                        .then_inc(S["end_flag"], 1)
                nc.vector.tensor_copy(kc(h_hi[:, 0]), new_h).then_inc(S["hhi_done"], 1)
                nc.vector.tensor_copy(old_c[:, :, 1:CH], end_c[:, :, 0:CH - 1]).then_inc(S["shift_c"], 1)
                dve.wait_ge(S["hhi_done"], (r + 1) * (L + 1) + 1)
                nc.vector.tensor_tensor(kc(h_lo[:, 0]), new_h, kc(h_hi[:, 0]), ALU.subtract) \
                    .then_inc(S["hlo_done"], 1)
                dve.wait_ge(S["shift_c"], r * 3 + 1)
                nc.vector.tensor_copy(cell[:, 0], cell0).then_inc(S["shift_c"], 1)
                nc.vector.tensor_copy(kc(h0), new_h).then_inc(S["shift_c"], 1)
                dve.wait_ge(S["shift_c"], r * 3 + 3)

            rounds(dve, steps, after)

            nc.vector.drain().then_inc(S["scan_done"], 1)
            for t in range(NT):
                dve.wait_ge(S["ht_done"], t + 1)
                nc.vector.tensor_tensor(X[:, t, :], X[:, t, :], ps[6 + t % 2][:, 0:D], ALU.add) \
                    .then_inc(S["y_added"], 1)

        @block.tensor
        def _(pe):
            def transposes(ready, done, copied, src_):
                for t in range(NT):
                    pe.wait_ge(S[ready], t + 1)
                    if t >= 2:
                        pe.wait_ge(S[copied], t - 1)
                    for k in range(KH):
                        ins = nc.tensor.transpose(ps[t % 2][:, col(k)], src_[:, t % 2, col(k)], ident[:, :])
                    ins.then_inc(S[done], 1)

            pe.wait_ge(S["iota_ready"], 10)
            transposes("xn_ready", "xt_done", "xt_copied", xn)

            def node_product(bank, t, w, off=0):
                for k in range(KH):
                    ins = nc.tensor.matmul(bank[:, off:off + w.shape[2]], hT[:, k, col(t)], w[:, k, :],
                                           start=(k == 0), stop=(k == KH - 1))
                return ins

            pe.wait_ge(S["xt_copied"], NT)
            pe.wait_ge(S["wmix_loaded"], 32)
            for t in range(NT):
                if t >= 2:
                    pe.wait_ge(S["kmax_done"], t)
                node_product(ps[2 + t % 2], t, wqkv[:, :, D:2 * D]).then_inc(S["k_done"], 1)

            def context(t):
                rows = LAST if t == NT - 1 else P
                pe.wait_ge(S["kexp_done"], t + 1)
                pe.wait_ge(S["v_copied"], t + 1)
                if t == 0:
                    pe.wait_ge(S["kmax_done"], NT + 1)
                for k in range(KH):
                    ins = nc.tensor.matmul(ps[2 + k][:, 0:P + 1], kexp[0:rows, t % 2, col(k)],
                                           v1[0:rows, t % 2, k, :], start=(t == 0), stop=(t == NT - 1))
                ins.then_inc(S["ctx_done"], 1)

            for t in range(NT):
                if t >= 2:
                    pe.wait_ge(S["kshift_done"], t - 1)
                    pe.wait_ge(S["v_copied"], t - 1)
                node_product(ps[t % 2], t, wqkv[:, :, D:2 * D])
                node_product(ps[4 + t % 2], t, wqkv[:, :, 2 * D:3 * D]).then_inc(S["kv_done"], 1)
                if t:
                    context(t - 1)
            context(NT - 1)

            def q_product(t):
                if t >= 2:
                    pe.wait_ge(S["qsub_done"], t - 1)
                node_product(ps[t % 2], t, wqkv[:, :, 0:D]).then_inc(S["q_done"], 1)

            pe.wait_ge(S["kshift_done"], NT)
            pe.wait_ge(S["v_copied"], NT)
            q_product(0)
            q_product(1)
            pe.wait_ge(S["ctx_norm"], KH)
            for k in range(KH):
                ins = nc.tensor.transpose(ps[4][:, col(k)], ctxn[:, k, :], ident[:, :])
            ins.then_inc(S["ctx_tr"], 1)
            pe.wait_ge(S["ctx_trc"], 1)
            for k in range(KH):
                ins = nc.tensor.matmul(ps[5][:, k * D:(k + 1) * D], ctxT[:, k, :], wout[:, k, :],
                                       start=True, stop=True)
            ins.then_inc(S["ctxw_done"], 1)
            pe.wait_ge(S["ctxw_copied"], 1)
            for t in range(NT):
                if t and t + 1 < NT:
                    q_product(t + 1)
                pe.wait_ge(S["qn_done"], t + 1)
                if t:
                    pe.wait_ge(S["qt_copied"], t)
                for k in range(KH):
                    ins = nc.tensor.transpose(ps[6][:, col(k)], qn[:, t % 2, col(k)], ident[:, :])
                ins.then_inc(S["qt_done"], 1)
                pe.wait_ge(S["qt_copied"], t + 1)
                if t:
                    pe.wait_ge(S["att_copied"], t)
                for k in range(KH):
                    ins = nc.tensor.matmul(ps[7][:, 0:D], qT[:, t % 2, k, :], ctxw[:, k, :],
                                           start=(k == 0), stop=(k == KH - 1))
                ins.then_inc(S["att_done"], 1)

            pe.wait_ge(S["ctxw_copied"], 1)
            pe.wait_ge(S["att_copied"], NT)
            for s, f in enumerate((fields, fields2, fields3)):
                pe.wait_ge(S["fields_f"], s + 1)
                for b in range(EB):
                    nc.tensor.transpose(ps[4 + s][:, col(b)], f[:, b, :], ident[:, :]) \
                        .then_inc(S["fields_tr"], 1)
            pe.wait_ge(S["less_done"], EB)
            for b in range(EB):
                ins = nc.tensor.matmul(ps[0][0:1, 0:NG + 2], onef, less[:, b, :],
                                       start=(b == 0), stop=(b == EB - 1))
            ins.then_inc(S["starts_sum"], 1)

            pe.sem_inc(S["counts_done"], 2)
            with pe.Fori(0, NG // 2) as j:
                for b in range(2):
                    g = j * 2 + b
                    pe.wait_ge(S["ohb_ready"], g + 1)
                    pe.wait_ge(S["ohu_ready"], g + 3)
                    pe.wait_ge(S["counts_stored"], g + 1)
                    for k in range(CAP):
                        ins = nc.tensor.matmul(ps[2 + b][:, 0:COMB], onehot_b[:, b, k, :],
                                               onehot_u[:, b, k, :], start=(k == 0), stop=(k == CAP - 1))
                    ins.then_inc(S["counts_done"], 1)

            pe.wait_ge(S["counts_stored"], NG + 2)
            pe.wait_ge(S["table_done"], 4)
            for c, (c0, w) in enumerate(CHUNKS):
                if c >= 2:
                    pe.wait_ge(S["some_done"], c - 1)
                for s in range(NT):
                    ins = nc.tensor.matmul(ps[4 + c % 2][:, 0:w], ones_b[:, :], AT[:, s, c0:c0 + w],
                                           start=(s == 0), stop=(s == NT - 1))
                ins.then_inc(S["cnt_done"], 1)

            pe.wait_ge(S["graph_flag"], 1)
            exact = pe.value_load(flag[0:1, 1:2], min_val=0, max_val=1)

            def edge_products(p, outs):
                w = CHUNKS[p % NC][1]

                def body(t, rows, first, last):
                    n = p * ET + t
                    pe.wait_ge(S["gen_hots"], n + 1)
                    if p >= NC:
                        pe.wait_ge(S["gen_gathered", p // NC], (t + (p % NC * ET + 1)) * 16)
                    for i, (bank, lhs, begin, end) in enumerate(outs):
                        ins = nc.tensor.matmul(bank[:, 0:w], lhs[0:rows], gen_hot[0:rows, 0:w],
                                               start=first and begin, stop=last and end)
                    ins.then_inc(S["gen_used"], 1)

                edge_tiles(pe, body)

            with pe.If(exact < 1):
                pe.sem_inc(S["gen_used"], 1)
                pe.wait_ge(S["some_done"], NC)
                for c in range(NC):
                    if c >= 2:
                        pe.wait_ge(S["some_done"], NC + c - 1)
                    edge_products(c, [(ps[4 + c % 2], ones_b, True, True)])
                    pe.drain().then_inc(S["cnt_done"], 1)
                pe.wait_ge(S["some_done"], 2 * NC)
                pe.drain()
            pe.nop()

            for l in range(LAYERS + 1):
                if l < LAYERS:
                    pe.wait_ge(S["wcat_loaded", l], 16)
                pe.wait_ge(S["wf_loaded", l], 16)
                if l:
                    pe.wait_ge(S["h_done"], l * len(CHUNKS) * KH)
                for t in range(NT):
                    n = l * NT + t
                    if n >= 2:
                        pe.wait_ge(S["cat_added"], n - 1)
                    if l < LAYERS:
                        ins = node_product(ps[t % 2], t, Wcat[:, l % 2, :, :])
                    else:
                        ins = node_product(ps[t % 2], t, Wcat[:, l % 2, :, D:2 * D], D)
                    ins.then_inc(S["y_done"], 1)
                if l == LAYERS:
                    break
                pe.wait_ge(S["y_lo"], (l + 1) * NT)
                pe.wait_ge(S["wd_done"], l + 1)
                pe.wait_ge(S["some_done"], len(CHUNKS))
                for c, (c0, w) in enumerate(CHUNKS):
                    m = l * len(CHUNKS) + c
                    base = 2 if c % 2 == 0 else 6
                    if m >= 1:
                        pe.wait_ge(S["t1_done"], m * KH)

                    def block_products(s, start, stop):
                        for part in range(3):
                            for k in range(KH):
                                lhs = Yp[:, ds(s, 1), part, col(k)].rearrange("p s n -> p (s n)")
                                rhs = AT[:, ds(s, 1), c0:c0 + w].rearrange("p s n -> p (s n)")
                                ins = nc.tensor.matmul(ps[base + k][:, 0:w], lhs, rhs,
                                                       start=start and part == 0, stop=stop and part == 2)
                        return ins

                    with pe.If(exact > 0):
                        block_products(0, True, False)
                        with pe.Fori(1, NT - 1) as s:
                            block_products(s, False, False)
                        block_products(NT - 1, False, True).then_inc(S["agg_done"], 1)
                    with pe.Else():
                        edge_products(NC + m, [(ps[base + k], gen_rows[:, part * D + k * P:part * D + (k + 1) * P],
                                                part == 0, part == 2) for k in range(KH) for part in range(3)])
                        pe.drain().then_inc(S["agg_done"], 1)
                    if m:
                        pe.wait_ge(S["t2_done"], m * KH)
                    for k in range(KH):
                        for h in range(KH):
                            ins = nc.tensor.matmul(ps[4 + k][:, 0:w], Wd[:, l % 2, h, col(k)],
                                                   hT[:, h, c0:c0 + w], start=(h == 0), stop=(h == KH - 1))
                    ins.then_inc(S["u_done"], 1)

            transposes("xn2_ready", "xt2_done", "xt2_copied", xn2)
            pe.wait_ge(S["xt2_copied"], NT)
            pe.wait_ge(S["u_loaded"], 48)
            TW = 8 * L
            for s in range(NP // TW):
                for b in range(3 * KH):
                    n = s * 3 * KH + b
                    if n >= 4:
                        pe.wait_ge(S["g_stored"], n - 3)
                    for k in range(KH):
                        ins = nc.tensor.matmul(ps[n % 4][:, 0:TW], Ucat[:, k, col(b)],
                                               hT[:, k, s * TW:(s + 1) * TW], start=(k == 0), stop=(k == KH - 1))
                    ins.then_inc(S["g_done"], 1)
            pe.wait_ge(S["g_wrap"], 1)
            pe.wait_ge(S["v_lo"], 1)

            def preload(u, t):
                row = xg[:, ds(t, 1), :].rearrange("p t n -> p (t n)")
                for g in range(3):
                    nc.tensor.matmul(ps[2 * g + u % 2][:, 0:GW], ident[:, :], row[:, g * GW:(g + 1) * GW],
                                     start=True, stop=False, skip_group_check=True)

            def steps(r):
                with pe.Fori(0, L // UN) as j:
                    nh = (r * (L + 1)) + j * UN
                    for u in range(UN):
                        def add(b, h, weights, last=False):
                            bank, o = ps[b // KH * 2 + u % 2], b % KH * CH
                            for k in range(KH):
                                for i, w in enumerate(weights):
                                    ins = nc.tensor.matmul(bank[:, o:o + CH], w[:, k, col(b)],
                                                           h[:, u % 2, k * CH:(k + 1) * CH], start=False,
                                                           stop=last and k == KH - 1, skip_group_check=True)
                            return ins

                        pe.wait_ge(S["hhi_done"], nh + (u + 1))
                        for b in (2, 3, 0, 1):
                            add(b, h_hi, (Vhi, Vlo))
                        pe.wait_ge(S["hlo_done"], nh + (u + 1))
                        add(2, h_lo, (Vhi,), True)
                        add(3, h_lo, (Vhi,), True).then_inc(S["cg_done"], 1)
                        add(0, h_lo, (Vhi,), True)
                        add(1, h_lo, (Vhi,), True).then_inc(S["ci_done"], 1)
                        for b in (4, 5):
                            add(b, h_hi, (Vhi, Vlo))
                            ins = add(b, h_lo, (Vhi,), True)
                        ins.then_inc(S["co_done"], 1)
                        preload(u + 1, j * UN + (u + 1))

            def after(r, look):
                if look is not None:
                    pe.wait_ge(S["end_max"], look)
                    nc.tensor.transpose(ps[6][0:1, 0:P], moved[:, 0:1], ident[:, :]).then_inc(S["end_tr"], 1)

            preload(0, 0)
            rounds(pe, steps, after)

            pe.wait_ge(S["scan_done"], 1)
            for t in range(NT):
                if t >= 2:
                    pe.wait_ge(S["y_added"], t - 1)
                for k in range(KH):
                    ins = nc.tensor.transpose(ps[6 + t % 2][:, col(k)],
                                              hist[:, k, 1 + t * P:1 + (t + 1) * P], ident[:, :])
                ins.then_inc(S["ht_done"], 1)


_INS = ["x", "src", "dst", "L0_gnn_W0", "L0_gnn_b0", "L0_gnn_W1", "L0_gnn_b1", "L0_gnn_W2", "L0_gnn_b2",
        "L0_gnn_Wf", "L0_gnn_bf", "L0_mix_Wqkv", "L0_mix_Wout", "L0_mix_gamma",
        "L0_ffn_U_i", "L0_ffn_V_i", "L0_ffn_b_i", "L0_ffn_U_f", "L0_ffn_V_f", "L0_ffn_b_f",
        "L0_ffn_U_c", "L0_ffn_V_c", "L0_ffn_b_c", "L0_ffn_U_o", "L0_ffn_V_o", "L0_ffn_b_o"]


def kernel(**inputs):
    import numpy as np
    import concourse.bacc as bacc
    from concourse.bass_utils import run_bass_kernel_spmd

    nc = bacc.Bacc("TRN2", target_bir_lowering=False, num_devices=1)
    arrays, args = {}, []
    for name in _INS:
        a = np.ascontiguousarray(inputs[name])
        arrays[f"in_{name}"] = a
        args.append(nc.dram_tensor(f"in_{name}", a.shape, mybir.dt.from_np(a.dtype), kind="ExternalInput").ap())
    out = nc.dram_tensor("out", inputs["x"].shape, F32, kind="ExternalOutput").ap()
    graph_layer_kernel(nc, *args, out)
    r = run_bass_kernel_spmd(nc, [arrays], core_ids=[0])
    return r.results[0]["out"]
```

```python
import concourse.bass as bass
from concourse import mybir
from contextlib import ExitStack

F32 = mybir.dt.float32
BF16 = mybir.dt.bfloat16
FP16 = mybir.dt.float16
I32 = mybir.dt.int32
U32 = mybir.dt.uint32
ALU = mybir.AluOpType
ACT = mybir.ActivationFunctionType
AX = mybir.AxisListType
ds = bass.ds


def graph_layer_kernel(nc, x, src, dst, W0, b0, W1, b1, W2, b2, Wf, bf, Wqkv, Wout, gamma,
                       U_i, V_i, b_i, U_f, V_f, b_f, U_c, V_c, b_c, U_o, V_o, b_o, out):
    P = nc.NUM_PARTITIONS
    N, D = x.shape
    E = src.shape[0]
    KH = D // P
    NT = -(-N // P)
    NP = NT * P
    LAST = N - (NT - 1) * P
    HEADS, DH = 8, 32
    SCALE = DH ** -0.5
    EPS = 1e-5
    LAYERS = 3

    G, CAP = 32, 6
    UG = 4
    NG = UG * (-(-N // (UG * G)))
    BA = 4
    ND = NG * G
    COMB = NT * G
    CB = COMB // 2
    ET = -(-E // P)
    EB = -(-ET // P)
    EL = E - (ET - 1) * P
    ETP = ET + CAP + 1
    CW = 512
    CHUNKS = [(c, min(CW, ND - c)) for c in range(0, ND, CW)]

    CH, L, UN = 32, 80, 8
    USED = -(-N // L)
    WARM = 3
    LEAD = 1
    TOL = 2.0 ** -15
    TC = 4
    GW = KH * CH
    assert CH * L == NP

    y_dram = nc.dram_tensor("y_dram", (NP, 2 * D), FP16, kind="Internal").ap()

    ctx = ExitStack()
    with ctx:
        def sb(name, shape, dt):
            return ctx.enter_context(nc.sbuf_tensor(name, shape, dt))

        def sem(name):
            return ctx.enter_context(nc.semaphore(name))

        ps = [ctx.enter_context(nc.psum_tensor(f"bank{i}", [P, 512], F32)) for i in range(8)]

        X = sb("X", [P, NT, D], F32)
        hT = sb("hT", [P, KH, NP], F32)
        AT = sb("AT", [P, NT, ND], FP16)
        Yp = sb("Yp", [P, NT, 2, D], FP16)
        rz = sb("rz", [P, ND + ND // 2], F32)
        inv = rz[:, 0:ND]
        some = rz[:, ND:ND + ND // 2].bitcast(FP16)
        Wcat = sb("Wcat", [P, 2, KH, 2 * D], F32)
        Wd = sb("Wd", [P, 2, KH, D], F32)
        tmp = sb("tmp", [P, KH, CW], F32)
        ident = sb("ident", [P, P], F32)
        ones_h = sb("ones_h", [P, P], FP16)
        ones_f = sb("ones_f", [P, P], F32)
        bcol = sb("bcol", [P, LAYERS, KH], F32)
        gcol = sb("gcol", [P, 3, KH], F32)
        mean = sb("mean", [P, NT], F32)
        rstd = sb("rstd", [P, NT], F32)
        stat = sb("stat", [P, NT, 2], F32)
        bn6 = sb("bn6", [P, 2, 6], F32)
        flag = sb("flag", [1, 4], I32)
        warm = sb("warm", [1, 2], F32)

        gen_rows = sb("gen_rows", [P, 2 * D], FP16)
        gen_hot = sb("gen_hot", [P, CW], FP16)
        gen_iota = sb("gen_iota", [P, CW], I32)
        gen_src = sb("gen_src", [P, 1], U32)
        gen_dst = sb("gen_dst", [P, 1], I32)
        gen_col = sb("gen_col", [P, 1], F32)
        norms = sb("norms", [P, 3], F32)
        bound = sb("bound", [P, 3], F32)
        scale = sb("scale", [P, LAYERS, 2], I32)
        scale_f = scale[:, :, :].bitcast(F32)
        expo = sb("expo", [P, 1], I32)
        degree = sb("degree", [1, 4, 8], F32)

        at32 = AT[:, :, :].rearrange("p a b -> p (a b)").bitcast(F32)
        yp32 = Yp[:, :, :, :].rearrange("p a b c -> p (a b c)").bitcast(F32)
        cut = [0]

        def early(n):
            cut[0] += n
            return at32[:, cut[0] - n:cut[0]]

        wqkv = early(KH * 3 * D).rearrange("p (k n) -> p k n", k=KH)
        wout = early(KH * D).rearrange("p (k n) -> p k n", k=KH)
        gam = early(D)
        bfb = early(D)
        kmax = early(D)
        kmaxb = early(D)
        kshift = early(2 * D).rearrange("p (b n) -> p b n", b=2)
        kexp = early(2 * D).rearrange("p (b n) -> p b n", b=2)
        v1 = early(2 * KH * (P + 1)).rearrange("p (b k n) -> p b k n", b=2, k=KH)
        ctxn = early(KH * P).rearrange("p (k n) -> p k n", k=KH)
        ctxT = early(KH * P).rearrange("p (k n) -> p k n", k=KH)
        den = early(2 * KH)
        hmask = early(P)
        ctxw = early(KH * D).rearrange("p (k n) -> p k n", k=KH)
        qs = early(2 * D).rearrange("p (b n) -> p b n", b=2)
        qn = early(2 * D).rearrange("p (b n) -> p b n", b=2)
        qT = early(2 * D).rearrange("p (b k n) -> p b k n", b=2, k=KH)
        qmx = early(2 * 3 * HEADS).rearrange("p (b s h) -> p b s h", b=2, s=3)
        xn = early(2 * D).rearrange("p (b n) -> p b n", b=2)
        att = yp32[:, 0:NT * D].rearrange("p (t n) -> p t n", t=NT)

        cut2 = [0]

        def build(n32):
            cut2[0] += n32
            assert cut2[0] <= ND + ND // 2
            return rz[:, cut2[0] - n32:cut2[0]]

        onehot_u = build(2 * CAP * COMB // 2).bitcast(FP16).rearrange("p (b k n) -> p b k n", b=2, k=CAP)
        iota_u = sb("iota_u", [P, COMB], FP16)
        iota_b = sb("iota_b", [P, P], FP16)
        iota_g = sb("iota_g", [P, NG + 2], F32)
        starts = sb("starts", [1, NG + 2], I32)
        onehot_a = tmp[:, :, :].rearrange("p k n -> p (k n)")[:, 0:UG * BA * P // 2] \
            .bitcast(FP16).rearrange("p (b k n) -> p b k n", b=UG, k=BA)
        away = gen_hot[:, :].rearrange("p (k n) -> p k n", k=BA)
        onehot_d = gen_rows[:, :].rearrange("p (b k n) -> p b k n", b=2, k=CAP - BA)
        tw = 3 * (ETP + ETP % 2) // 2
        w1 = max(tw, COMB, KH * D)
        widths = [w1, 3 * UG * CAP, UG * CAP, UG * CAP, EB * (NG + 2), EB * P, NG + 2, EB, UG]
        work = sb("work", [P, sum(widths)], F32)
        at = [sum(widths[:i]) for i in range(len(widths) + 1)]
        part = [work[:, at[i]:at[i + 1]] for i in range(len(widths))]
        iota_i = part[0][:, 0:COMB].bitcast(I32)
        table = part[0][:, 0:tw].bitcast(FP16).rearrange("p (s t) -> p s t", s=3)
        squares = part[0][:, 0:KH * D]
        window = part[1].rearrange("p (b s k) -> p b s k", b=UG, s=3)
        match = part[2].rearrange("p (b k) -> p b k", b=UG)
        bval = part[3].rearrange("p (b k) -> p b k", b=UG)
        less = part[4].rearrange("p (b g) -> p b g", b=EB)
        fields3 = part[5].rearrange("p (b e) -> p b e", b=EB)
        iota_first, first, number = part[6], part[7], part[8]
        wd32 = Wd[:, :, :, :].rearrange("p a k n -> p (a k n)")
        raw = Wcat[:, :, :, :].rearrange("p a k n -> p (a k n)")
        sraw = raw[:, 0:EB * P].bitcast(I32).rearrange("p (b e) -> p b e", b=EB)
        draw = raw[:, EB * P:2 * EB * P].bitcast(I32).rearrange("p (b e) -> p b e", b=EB)
        f_i = raw[:, 2 * EB * P:3 * EB * P].bitcast(I32).rearrange("p (b e) -> p b e", b=EB)
        f_j = raw[:, 3 * EB * P:4 * EB * P].bitcast(I32).rearrange("p (b e) -> p b e", b=EB)
        fields = wd32[:, 0:EB * P].rearrange("p (b e) -> p b e", b=EB)
        fields2 = wd32[:, EB * P:2 * EB * P].rearrange("p (b e) -> p b e", b=EB)

        xg = at32[:, 0:(L + 1) * 3 * GW].rearrange("p (t n) -> p t n", t=L + 1)
        o1 = (L + 1) * 3 * GW
        hist = at32[:, o1:o1 + KH * (CH * L + 1)].rearrange("p (k n) -> p k n", k=KH)
        assert o1 + KH * (CH * L + 1) <= NT * ND // 2
        Ucat = Wcat[:, :, :, :].rearrange("p a k n -> p (a k n)")[:, 0:KH * 3 * D] \
            .rearrange("p (k n) -> p k n", k=KH)
        Vraw = rz[:, 0:KH * 3 * D].rearrange("p (k n) -> p k n", k=KH)
        Vhi = rz[:, KH * 3 * D:KH * 3 * D + KH * 3 * D // 2].bitcast(FP16) \
            .rearrange("p (k n) -> p k n", k=KH)
        Vlo = wd32[:, 0:KH * 3 * D // 2].bitcast(FP16).rearrange("p (k n) -> p k n", k=KH)
        xn2 = yp32[:, 0:2 * D].rearrange("p (b n) -> p b n", b=2)

        st = yp32[:, 2 * D:]
        factors = st[:, 15 * GW:17 * GW].rearrange("p (n o) -> p n o", o=2)
        terms = st[:, 17 * GW:19 * GW].rearrange("p (n o) -> p n o", o=2)
        pairs = st[:, 19 * GW:23 * GW].rearrange("p (b n o) -> p b n o", b=2, o=2)
        cell = pairs[:, :, :, 1]
        cell0 = st[:, 2 * GW:3 * GW]
        h0 = st[:, 14 * GW:15 * GW]
        tc = st[:, 5 * GW:6 * GW]
        go = st[:, 6 * GW:7 * GW]
        diff = st[:, 9 * GW:11 * GW].rearrange("p (b k c) -> p b k c", b=2, k=KH)
        moved = st[:, 11 * GW:11 * GW + 2]
        h_hi = st[:, 12 * GW:13 * GW].bitcast(FP16).rearrange("p (b n) -> p b n", b=2)
        h_lo = st[:, 13 * GW:14 * GW].bitcast(FP16).rearrange("p (b n) -> p b n", b=2)

        names = """x_loaded x_last_loaded wmix_loaded mixvec_loaded edges_loaded 
        bias_loaded
        const_ready iota_ready x_bn x_stat var_done std_done rstd_done xn_ready xt_done xt_copied
        k_done kmax_done kmaxb_ready kv_done kshift_done kexp_done v_copied v_ones ctx_done
        ctx_den ctx_norm ctx_tr ctx_trc ctxw_done ctxw_copied
        q_done qmax_done qsub_done qexp_done qsum_done qrec_done qn_done qt_done qt_copied
        att_done att_copied att_bn att_stats att_std att_rstd att_n att_g att_added bf_added
        raw_set dve_step first_ready less_done starts_sum starts_done fields_tr table_done
        fields_f
        window_set match_ready bval_ready ohu_ready away_done oha_ready counts_done counts_stored
        cnt_done inv_a inv_done some_done
        wd_done y_done y_hi y_lo cat_added agg_done u_done t1_done t2_done t3_done h_done
        mean2_done norm_ready norm_sum scale_ready
        std2_done rstd2_done x2_bn x2_stat xn2_ready xt2_done xt2_copied
        u_loaded v_loaded gb_loaded g_done g_stored g_wrap v_hi v_lo st_init
        cg_done ci_done co_done gg_done gi_done go_done hc_done c_done tc_done hhi_done h_f32
        hlo_done end_diff end_total end_max end_tr end_flag shift_c 
noted gen_cols gen_hots gen_used y_stored gen_iota_ready  graph_flag scan_done ht_done y_added out_stored warm_done""".split()
        S = {n: sem(n) for n in names}
        for l_ in range(LAYERS + 1):
            for n_ in ("gen_edges", "gen_gathered"):
                S[n_, l_] = sem(f"{n_}{l_}")
            for n_ in ("wcat_loaded", "wf_loaded", "wd_loaded"):
                S[n_, l_] = sem(f"{n_}{l_}")

        block = ctx.enter_context(nc.Block())

        def col(t):
            return slice(t * P, (t + 1) * P)

        NC = len(CHUNKS)

        def edge_tiles(eng, body):
            body(0, P, True, False)
            with eng.Fori(1, ET - 1) as t:
                body(t, P, False, False)
            body(ET - 1, EL, False, True)

        def rounds(eng, steps, after):
            with eng.Fori(0, LEAD) as r:
                steps(r, False)
                after(r, None)
            with eng.Fori(LEAD, WARM) as r:
                steps(r, True)
                after(r, None)
            steps(WARM, True)
            after(WARM, 1)
            eng.wait_ge(S["end_flag"], 1)
            moving = eng.value_load(flag[0:1, 0:1], min_val=0, max_val=1)
            with eng.If(moving > 0):
                with eng.Fori(0, USED - WARM - 1) as r:
                    still = eng.value_load(flag[0:1, 0:1], min_val=0, max_val=1)
                    with eng.If(still > 0):
                        steps(r + (WARM + 1), True)
                        after(r + (WARM + 1), r + 2)
                        eng.wait_ge(S["end_flag"], r + 2)
                        eng.sem_inc(S["noted"], 1)
                    eng.nop()
                eng.nop()
            eng.nop()

        @block.sync
        def _(sp):
            sp.wait_ge(S["const_ready"], 1)
            full = x[0:(NT - 1) * P, :].rearrange("(t p) d -> p t d", p=P)
            sp.dma_start(X[:, 0:NT - 1, :], full).then_inc(S["x_loaded"], 16)
            sp.dma_start(X[0:LAST, NT - 1, :], x[(NT - 1) * P:N, :]).then_inc(S["x_last_loaded"], 16)
            sp.dma_start(wqkv, Wqkv.rearrange("(k p) n -> p k n", p=P)).then_inc(S["wmix_loaded"], 16)
            sp.dma_start(wout, Wout.rearrange("(k p) n -> p k n", p=P)).then_inc(S["wmix_loaded"], 16)
            sp.dma_start(gam, gamma.partition_broadcast(P)).then_inc(S["mixvec_loaded"], 16)
            sp.dma_start(bfb, bf.partition_broadcast(P)).then_inc(S["mixvec_loaded"], 16)
            with nc.allow_non_contiguous_dma("short bias columns"):
                for l, b in enumerate((b0, b1, b2)):
                    sp.dma_start(bcol[:, l, :], b.rearrange("(k p) -> p k", p=P)).then_inc(S["bias_loaded"], 16)
                for g, b in enumerate((b_i, b_c, b_o)):
                    sp.dma_start(gcol[:, g, :], b.rearrange("(k p) -> p k", p=P)).then_inc(S["gb_loaded"], 16)
            sp.wait_ge(S["raw_set"], 2)
            for raw_, e in ((sraw, src), (draw, dst)):
                full_b = (ET - 1) // P
                sp.dma_start(raw_[:, 0:full_b, :], e[0:full_b * P * P].rearrange("(b p e) -> p b e", p=P, e=P)) \
                    .then_inc(S["edges_loaded"], 16)
                rest = ET - 1 - full_b * P
                sp.dma_start(raw_[0:rest, full_b, :],
                             e[full_b * P * P:(ET - 1) * P].rearrange("(p e) -> p e", e=P)) \
                    .then_inc(S["edges_loaded"], 16)
                sp.dma_start(raw_[rest:rest + 1, full_b, 0:EL],
                             e[(ET - 1) * P:E].rearrange("(p e) -> p e", p=1)).then_inc(S["edges_loaded"], 16)
            Ws = (W0, W1, W2)
            for l in range(LAYERS + 1):
                if l == 0:
                    sp.wait_ge(S["fields_tr"], 9)
                if l >= 2:
                    sp.wait_ge(S["y_done"], NT * (l - 1))
                if l < LAYERS:
                    sp.dma_start(Wcat[:, l % 2, :, 0:D], Ws[l][D:2 * D, :].rearrange("(k p) n -> p k n", p=P)) \
                        .then_inc(S["wcat_loaded", l], 16)
                sp.dma_start(Wcat[:, l % 2, :, D:2 * D],
                             Wf[l * D:(l + 1) * D, :].rearrange("(k p) n -> p k n", p=P)) \
                    .then_inc(S["wf_loaded", l], 16)
                if l < LAYERS:
                    if l >= 2:
                        sp.wait_ge(S["u_done"], len(CHUNKS) * (l - 1))
                    sp.dma_start(Wd[:, l % 2, :, :], Ws[l][0:D, :].rearrange("(k p) n -> p k n", p=P)) \
                        .then_inc(S["wd_loaded", l], 16)
            sp.wait_ge(S["y_done"], NT * (LAYERS + 1))
            for g, u in enumerate((U_i, U_c, U_o)):
                sp.dma_start(Ucat[:, :, g * D:(g + 1) * D], u.rearrange("(k p) n -> p k n", p=P)) \
                    .then_inc(S["u_loaded"], 16)
            sp.wait_ge(S["h_done"], LAYERS * len(CHUNKS) * KH)
            for g, v in enumerate((V_i, V_c, V_o)):
                sp.dma_start(Vraw[:, :, g * D:(g + 1) * D], v.rearrange("(k p) n -> p k n", p=P)) \
                    .then_inc(S["v_loaded"], 16)
            for t in range(0, NT - 1, 4):
                n = min(4, NT - 1 - t)
                sp.wait_ge(S["y_added"], t + n)
                sp.dma_start(out[t * P:(t + n) * P, :].rearrange("(t p) d -> p t d", p=P),
                             X[:, t:t + n, :]).then_inc(S["out_stored"], 16)
            sp.wait_ge(S["y_added"], NT)
            sp.dma_start(out[(NT - 1) * P:N, :], X[0:LAST, NT - 1, :]).then_inc(S["out_stored"], 16)
            sp.wait_ge(S["out_stored"], 16 * (-(-(NT - 1) // 4) + 1))

        @block.gpsimd
        def _(pool):
            nc.gpsimd.memset(ident[:, :], 0.0).then_inc(S["iota_ready"], 1)
            nc.gpsimd.memset(hmask, 1.0).then_inc(S["iota_ready"], 1)
            nc.gpsimd.memset(ones_h[:, :], 1.0)
            nc.gpsimd.memset(ones_f[:, :], 1.0)
            pool.wait_ge(S["iota_ready"], 2)
            nc.gpsimd.affine_select(out=ident[:, :], in_=ident[:, :], compare_op=ALU.not_equal, fill=1.0,
                                    base=0, pattern=[[-1, P]], channel_multiplier=1).then_inc(S["iota_ready"], 1)
            hm = hmask.rearrange("p (h c) -> p h c", c=DH)
            nc.gpsimd.affine_select(out=hm, in_=hm, compare_op=ALU.is_ge, fill=0.0,
                                    base=0, pattern=[[-DH, P // DH], [0, DH]], channel_multiplier=1) \
                .then_inc(S["iota_ready"], 1)
            pool.wait_ge(S["iota_ready"], 4)
            nc.gpsimd.affine_select(out=hm, in_=hm, compare_op=ALU.is_ge, fill=0.0,
                                    base=DH - 1, pattern=[[DH, P // DH], [0, DH]], channel_multiplier=-1) \
                .then_inc(S["iota_ready"], 1)
            nc.gpsimd.iota(iota_i, [[1, COMB]], base=0, channel_multiplier=0).then_inc(S["iota_ready"], 1)
            pool.wait_ge(S["iota_ready"], 6)
            nc.gpsimd.tensor_scalar(iota_u[:, :], iota_i, 1.0, 0.0, ALU.mult, ALU.add) \
                .then_inc(S["iota_ready"], 1)
            nc.gpsimd.tensor_scalar(iota_b[:, :], iota_i[:, 0:P], -1.0, -1.0, ALU.mult, ALU.add) \
                .then_inc(S["iota_ready"], 1)
            nc.gpsimd.tensor_scalar(iota_g[:, :], iota_i[:, 0:NG + 2], 1.0, 0.0, ALU.mult, ALU.add) \
                .then_inc(S["iota_ready"], 1)
            nc.gpsimd.tensor_scalar(iota_first, iota_i[:, 0:NG + 2], float(G), 0.0, ALU.mult, ALU.add) \
                .then_inc(S["iota_ready"], 1)

            pool.wait_ge(S["kmax_done"], NT + 1)
            nc.gpsimd.partition_all_reduce(kmaxb, kmax, P, bass.bass_isa.ReduceOp.max) \
                .then_inc(S["kmaxb_ready"], 1)

            pool.wait_ge(S["table_done"], 4)
            pool.wait_ge(S["starts_done"], 1)
            with pool.Fori(0, NG // UG) as j:
                for b in range(UG):
                    g = j * UG + b
                    start = pool.value_load(starts[0:1, ds(g, 1)], min_val=0, max_val=ET - 1)
                    pool.wait_ge(S["ohu_ready"], g + 1)
                    pool.wait_ge(S["oha_ready"], g + 1)
                    nc.gpsimd.tensor_copy(window[:, b], table[:, :, ds(start, CAP)]) \
                        .then_inc(S["window_set"], 1)
                    nc.gpsimd.tensor_copy(number[:, b:b + 1], iota_g[:, ds(g, 1)]).then_inc(S["window_set"], 1)
                    pool.wait_ge(S["window_set"], g * 2 + 2)
                    pool.sem_inc(S["noted"], 1)
                    nc.gpsimd.tensor_scalar(match[:, b], window[:, b, 2, :], number[:, b:b + 1], None,
                                            ALU.is_equal).then_inc(S["match_ready"], 1)
                    pool.wait_ge(S["match_ready"], g + 1)
                    nc.gpsimd.tensor_tensor(bval[:, b], match[:, b], window[:, b, 1, :], ALU.mult) \
                        .then_inc(S["bval_ready"], 1)

            nc.gpsimd.iota(gen_iota[:, :], [[1, CW]], base=0, channel_multiplier=0) \
                .then_inc(S["gen_iota_ready"], 1)
            pool.wait_ge(S["graph_flag"], 1)
            exact = pool.value_load(flag[0:1, 1:2], min_val=0, max_val=1)

            def load_edges(p, gather):
                def body(t, rows, first, last):
                    n = p * ET + t
                    pool.wait_ge(S["gen_used"], n + 1)
                    if rows == P:
                        s_, d_ = src[ds(t * P, P)], dst[ds(t * P, P)]
                    else:
                        s_, d_ = src[(ET - 1) * P:E], dst[(ET - 1) * P:E]
                    pool.dma_start(gen_src[0:rows, :], s_.bitcast(U32).rearrange("(p o) -> p o", o=1)) \
                        .then_inc(S["gen_edges", p // NC], 16)
                    pool.dma_start(gen_dst[0:rows, :], d_.rearrange("(p o) -> p o", o=1)) \
                        .then_inc(S["gen_edges", p // NC], 16)
                    if gather:
                        pool.wait_ge(S["gen_edges", p // NC], (t + (p % NC * ET + 1)) * 32)
                        pool.sem_inc(S["noted"], 1)
                        nc.gpsimd.indirect_dma_start(
                            out=gen_rows[0:rows, :], out_offset=None, in_=y_dram[:, :],
                            in_offset=bass.IndirectOffsetOnAxis(ap=gen_src[0:rows, 0:1], axis=0)) \
                            .then_inc(S["gen_gathered", p // NC], 16)

                with nc.allow_non_contiguous_dma("edges to partitions"):
                    edge_tiles(pool, body)

            with pool.If(exact < 1):
                for c in range(NC):
                    load_edges(c, False)
                for l in range(LAYERS):
                    pool.wait_ge(S["y_lo"], (l + 1) * NT)
                    pool.dma_start(y_dram.rearrange("(s p) m -> p s m", p=P),
                                   Yp[:, :, :, :].rearrange("p s a m -> p s (a m)")).then_inc(S["y_stored"], 16)
                    pool.wait_ge(S["y_stored"], 16 * (l + 1))
                    for c in range(NC):
                        load_edges((l + 1) * NC + c, True)
                pool.nop()
            pool.nop()

        @block.scalar
        def _(act):
            def transposed_copies(done, copied, dest):
                for t in range(NT):
                    act.wait_ge(S[done], t + 1)
                    nc.scalar.copy(dest[:, :, col(t)], ps[t % 2][:, 0:D].rearrange("p (k n) -> p k n", k=KH)) \
                        .then_inc(S[copied], 1)

            act.wait_ge(S["var_done"], 1)
            nc.scalar.activation(rstd[:, :], mean[:, :], ACT.Sqrt).then_inc(S["std_done"], 1)
            transposed_copies("xt_done", "xt_copied", hT)

            for t in range(NT):
                rows = LAST if t == NT - 1 else P
                act.wait_ge(S["kv_done"], t + 1)
                act.wait_ge(S["v_ones"], 1)
                if t >= 2:
                    act.wait_ge(S["ctx_done"], t - 1)
                nc.scalar.copy(v1[0:rows, t % 2, :, 0:P],
                               ps[4 + t % 2][0:rows, 0:D].rearrange("p (k n) -> p k n", k=KH)) \
                    .then_inc(S["v_copied"], 1)
                act.wait_ge(S["kshift_done"], t + 1)
                nc.scalar.activation(kexp[0:rows, t % 2], kshift[0:rows, t % 2], ACT.Exp) \
                    .then_inc(S["kexp_done"], 1)
            act.wait_ge(S["ctx_tr"], 1)
            nc.scalar.copy(ctxT, ps[4][:, 0:D].rearrange("p (k n) -> p k n", k=KH)).then_inc(S["ctx_trc"], 1)
            act.wait_ge(S["ctxw_done"], 1)
            nc.scalar.copy(ctxw, ps[5][:, :].rearrange("p (k n) -> p k n", k=KH)).then_inc(S["ctxw_copied"], 1)
            for t in range(-1, NT):
                if t + 1 < NT:
                    act.wait_ge(S["qsub_done"], t + 2)
                    nc.scalar.activation(qs[:, (t + 1) % 2], qs[:, (t + 1) % 2], ACT.Exp) \
                        .then_inc(S["qexp_done"], 1)
                if t >= 0:
                    act.wait_ge(S["qt_done"], t + 1)
                    nc.scalar.copy(qT[:, t % 2], ps[6][:, 0:D].rearrange("p (k n) -> p k n", k=KH)) \
                        .then_inc(S["qt_copied"], 1)
                    act.wait_ge(S["att_done"], t + 1)
                    nc.scalar.copy(att[:, t, :], ps[7][:, 0:D]).then_inc(S["att_copied"], 1)
            act.wait_ge(S["att_stats"], NT + 1)
            nc.scalar.activation(rstd[:, :], mean[:, :], ACT.Sqrt).then_inc(S["att_std"], 1)

            def distances(g, b):
                act.wait_ge(S["bval_ready"], g + 1)
                act.wait_ge(S["oha_ready"], g + UG)
                for k in range(BA):
                    ins = nc.scalar.activation(away[:, k, :], iota_b[:, :], ACT.Abs,
                                               bias=bval[:, b % UG, k:k + 1], scale=-1.0)
                ins.then_inc(S["away_done"], 1)

            def from_distances(g, b):
                act.wait_ge(S["away_done"], g + 1)
                nc.scalar.activation(onehot_a[:, b % UG], away, ACT.Relu, bias=ones_f[:, 0:1], scale=-1.0) \
                    .then_inc(S["oha_ready"], 1)

            def store(g, b, ahead):
                if ahead:
                    distances(g + 2, b + 2)
                act.wait_ge(S["counts_done"], g + 3)
                for h in range(2):
                    ins = nc.scalar.copy(AT[:, h * (NT // 2):(h + 1) * (NT // 2), ds(g * G, G)],
                                         ps[2 * (b % 2) + h][:, 0:CB].rearrange("p (a n) -> p a n", n=G))
                ins.then_inc(S["counts_stored"], 1)
                if ahead:
                    from_distances(g + 2, b + 2)

            act.sem_inc(S["counts_stored"], 2)
            act.sem_inc(S["oha_ready"], UG)
            act.wait_ge(S["iota_ready"], 10)
            for g in range(2):
                distances(g, g)
                from_distances(g, g)
            with act.Fori(0, NG // UG - 1) as j:
                for b in range(UG):
                    store(j * UG + b, b, True)
            for b in range(UG):
                store(NG - UG + b, b, b + 2 < UG)

            for l in range(LAYERS):
                for t in range(NT):
                    n = l * NT + t
                    act.wait_ge(S["y_done"], n + 1)
                    act.wait_ge(S["scale_ready"], l + 1)
                    nc.scalar.activation(Yp[:, t, 0, :], ps[t % 2][:, 0:D], ACT.Identity,
                                         scale=scale_f[:, l, 0:1]).then_inc(S["y_hi"], 1)
                for c, (c0, w) in enumerate(CHUNKS):
                    for k in range(KH):
                        n = (l * len(CHUNKS) + c) * KH + k
                        act.wait_ge(S["t3_done"], n + 1)
                        act.wait_ge(S["u_done"], l * len(CHUNKS) + c + 1)
                        nc.scalar.activation(hT[:, k, c0:min(c0 + w, NP)], tmp[:, k, 0:min(w, NP - c0)],
                                             ACT.Relu).then_inc(S["h_done"], 1)

            act.wait_ge(S["mean2_done"], 1)
            nc.scalar.activation(rstd[:, :], mean[:, :], ACT.Sqrt).then_inc(S["std2_done"], 1)
            transposed_copies("xt2_done", "xt2_copied", hT)

            TW = TC * L
            act.wait_ge(S["gb_loaded"], 48)
            for s in range(NP // TW):
                for b in range(3 * KH):
                    n = s * 3 * KH + b
                    act.wait_ge(S["g_done"], n + 1)
                    dest = xg[:, 0:L, b * CH + TC * s:b * CH + TC * s + TC].rearrange("p t c -> p c t")
                    nc.scalar.activation(dest, ps[n % 4][:, 0:TW].rearrange("p (c t) -> p c t", c=TC),
                                         ACT.Identity, bias=gcol[:, b // KH, b % KH:b % KH + 1]) \
                        .then_inc(S["g_stored"], 1)
            act.wait_ge(S["warm_done"], 1)
            nc.scalar.activation(warm[:, 0:1], warm[:, 1:2], ACT.Sigmoid)

            def steps(r, full):
                with act.Fori(0, L // UN) as j:
                    n = r * L + j * UN
                    for u in range(UN):
                        act.wait_ge(S["cg_done"], n + (u + 1))
                        nc.scalar.activation(factors[:, :, 1], ps[2 + u % 2][:, 0:GW], ACT.Tanh) \
                            .then_inc(S["gg_done"], 1)
                        act.wait_ge(S["ci_done"], n + (u + 1))
                        nc.scalar.activation(terms[:, :, 0], ps[u % 2][:, 0:GW], ACT.Sigmoid) \
                            .then_inc(S["gi_done"], 1)
                        act.wait_ge(S["co_done"], n + (u + 1))
                        nc.scalar.activation(go, ps[4 + u % 2][:, 0:GW], ACT.Sigmoid) \
                            .then_inc(S["go_done"], 1)
                        act.wait_ge(S["c_done"], n + (u + 1))
                        nc.scalar.activation(tc, cell[:, (u + 1) % 2], ACT.Tanh).then_inc(S["tc_done"], 1)

            rounds(act, steps, lambda r, look: None)

        @block.vector
        def _(dve):
            nc.vector.memset(X[:, NT - 1, :], 0.0).then_inc(S["const_ready"], 1)
            nc.vector.memset(sraw, 0).then_inc(S["raw_set"], 1)
            nc.vector.memset(draw, 1 << 20).then_inc(S["raw_set"], 1)
            nc.vector.memset(kmax, -3.0e38).then_inc(S["kmax_done"], 1)
            nc.vector.memset(v1, 1.0).then_inc(S["v_ones"], 1)

            def norm_stats(data, ready, done, stats):
                for t in range(NT):
                    ready(t)
                    if t >= 2:
                        dve.wait_ge(S[stats], t - 1)
                    nc.vector.bn_stats(bn6[:, t % 2, :], data[:, t, :]).then_inc(S[done], 1)
                    dve.wait_ge(S[done], t + 1)
                    nc.vector.bn_aggr(stat[:, t, :], bn6[:, t % 2, :]).then_inc(S[stats], 1)
                dve.wait_ge(S[stats], NT)

            def x_ready(t):
                if t == 0:
                    dve.wait_ge(S["x_loaded"], 16)
                if t == NT - 1:
                    dve.wait_ge(S["x_last_loaded"], 16)

            norm_stats(X, x_ready, "x_bn", "x_stat")
            nc.vector.tensor_scalar(mean[:, :], stat[:, :, 1], EPS, None, ALU.add).then_inc(S["var_done"], 1)
            dve.wait_ge(S["std_done"], 1)
            nc.vector.reciprocal(rstd[:, :], rstd[:, :]).then_inc(S["rstd_done"], 1)
            dve.wait_ge(S["rstd_done"], 1)
            for t in range(NT):
                if t >= 2:
                    dve.wait_ge(S["xt_done"], t - 1)
                nc.vector.tensor_scalar(xn[:, t % 2], X[:, t, :], stat[:, t, 0:1], rstd[:, t:t + 1],
                                        ALU.subtract, ALU.mult).then_inc(S["xn_ready"], 1)

            for t in range(NT):
                rows = LAST if t == NT - 1 else P
                dve.wait_ge(S["k_done"], t + 1)
                dve.wait_ge(S["kmax_done"], t + 1)
                nc.vector.tensor_tensor(kmax[0:rows], ps[2 + t % 2][0:rows, 0:D], kmax[0:rows], ALU.max) \
                    .then_inc(S["kmax_done"], 1)
            dve.wait_ge(S["kmaxb_ready"], 1)
            for t in range(NT):
                rows = LAST if t == NT - 1 else P
                dve.wait_ge(S["kv_done"], t + 1)
                if t >= 2:
                    dve.wait_ge(S["kexp_done"], t - 1)
                nc.vector.tensor_tensor(kshift[0:rows, t % 2], ps[t % 2][0:rows, 0:D], kmaxb[0:rows],
                                        ALU.subtract).then_inc(S["kshift_done"], 1)
            dve.wait_ge(S["ctx_done"], NT)
            dve.wait_ge(S["iota_ready"], 5)
            for k in range(KH):
                nc.vector.reciprocal(den[:, 2 * k:2 * k + 1], ps[2 + k][:, P:P + 1]).then_inc(S["ctx_den"], 1)
                dve.wait_ge(S["ctx_den"], 2 * k + 1)
                nc.vector.tensor_scalar(den[:, 2 * k + 1:2 * k + 2], den[:, 2 * k:2 * k + 1], SCALE, None,
                                        ALU.mult).then_inc(S["ctx_den"], 1)
                dve.wait_ge(S["ctx_den"], 2 * k + 2)
                nc.vector.scalar_tensor_tensor(out=ctxn[:, k, :], in0=ps[2 + k][:, 0:P],
                                               scalar=den[:, 2 * k + 1:2 * k + 2], in1=hmask,
                                               op0=ALU.mult, op1=ALU.mult).then_inc(S["ctx_norm"], 1)
            for t in range(NT):
                b = t % 2
                mx, sm, rc = (qmx[:, b, i, :] for i in range(3))
                dve.wait_ge(S["q_done"], t + 1)
                q3 = ps[b][:, 0:D].rearrange("p (h c) -> p h c", c=DH)
                s3 = qs[:, b].rearrange("p (h c) -> p h c", c=DH)
                n3 = qn[:, b].rearrange("p (h c) -> p h c", c=DH)
                nc.vector.tensor_reduce(mx, q3, AX.X, ALU.max).then_inc(S["qmax_done"], 1)
                dve.wait_ge(S["qmax_done"], t + 1)
                if t >= 2:
                    dve.wait_ge(S["qn_done"], t - 1)
                nc.vector.tensor_tensor(s3, q3, mx.unsqueeze(2).to_broadcast([P, HEADS, DH]), ALU.subtract) \
                    .then_inc(S["qsub_done"], 1)
                dve.wait_ge(S["qexp_done"], t + 1)
                nc.vector.tensor_reduce(sm, s3, AX.X, ALU.add).then_inc(S["qsum_done"], 1)
                dve.wait_ge(S["qsum_done"], t + 1)
                nc.vector.reciprocal(rc, sm).then_inc(S["qrec_done"], 1)
                dve.wait_ge(S["qrec_done"], t + 1)
                if t >= 2:
                    dve.wait_ge(S["qt_done"], t - 1)
                nc.vector.tensor_tensor(n3, s3, rc.unsqueeze(2).to_broadcast([P, HEADS, DH]), ALU.mult) \
                    .then_inc(S["qn_done"], 1)
            norm_stats(att, lambda t: dve.wait_ge(S["att_copied"], t + 1), "att_bn", "att_stats")
            nc.vector.tensor_scalar(mean[:, :], stat[:, :, 1], EPS, None, ALU.add).then_inc(S["att_stats"], 1)
            dve.wait_ge(S["att_std"], 1)
            nc.vector.reciprocal(rstd[:, :], rstd[:, :]).then_inc(S["att_rstd"], 1)
            dve.wait_ge(S["att_rstd"], 1)
            dve.wait_ge(S["mixvec_loaded"], 32)
            for t in range(NT):
                nc.vector.tensor_tensor(X[:, t, :], X[:, t, :], bfb, ALU.add).then_inc(S["bf_added"], 1)
                nc.vector.tensor_scalar(att[:, t, :], att[:, t, :], stat[:, t, 0:1], rstd[:, t:t + 1],
                                        ALU.subtract, ALU.mult).then_inc(S["att_n"], 1)
                dve.wait_ge(S["att_n"], t + 1)
                nc.vector.tensor_tensor(att[:, t, :], att[:, t, :], gam, ALU.mult).then_inc(S["att_g"], 1)
                dve.wait_ge(S["att_g"], t + 1)
                dve.wait_ge(S["bf_added"], t + 1)
                nc.vector.tensor_tensor(X[:, t, :], X[:, t, :], att[:, t, :], ALU.add) \
                    .then_inc(S["att_added"], 1)

            done = [0]

            def step(ins):
                done[0] += 1
                ins.then_inc(S["dve_step"], 1)
                dve.wait_ge(S["dve_step"], done[0])

            dve.wait_ge(S["edges_loaded"], 96)
            log_p, log_g = P.bit_length() - 1, G.bit_length() - 1
            nc.vector.tensor_copy(first, draw[:, :, 0]).then_inc(S["first_ready"], 1)
            step(nc.vector.tensor_scalar(f_i, sraw, log_p, log_g, ALU.arith_shift_right, ALU.arith_shift_left))
            step(nc.vector.tensor_scalar(f_j, draw, G - 1, None, ALU.bitwise_and))
            step(nc.vector.tensor_tensor(f_i, f_i, f_j, ALU.bitwise_or))
            nc.vector.tensor_copy(fields, f_i).then_inc(S["fields_f"], 1)
            step(nc.vector.tensor_scalar(f_j, sraw, P - 1, None, ALU.bitwise_and))
            nc.vector.tensor_copy(fields2, f_j).then_inc(S["fields_f"], 1)
            dve.wait_ge(S["fields_f"], 2)
            step(nc.vector.tensor_scalar(f_i, draw, log_g, None, ALU.arith_shift_right))
            nc.vector.tensor_copy(fields3, f_i).then_inc(S["fields_f"], 1)
            dve.wait_ge(S["first_ready"], 1)
            dve.wait_ge(S["iota_ready"], 10)
            for b in range(EB):
                nc.vector.tensor_scalar(less[:, b, :], iota_first, first[:, b:b + 1], None, ALU.is_gt) \
                    .then_inc(S["less_done"], 1)
            dve.wait_ge(S["starts_sum"], 1)
            step(nc.vector.tensor_scalar(tmp[0:1, 0, 0:NG + 2], ps[0][0:1, 0:NG + 2], -1.0, 0.0,
                                         ALU.add, ALU.max))
            nc.vector.tensor_copy(starts[:, :], tmp[0:1, 0, 0:NG + 2]).then_inc(S["starts_done"], 1)
            nc.vector.memset(table, -1.0).then_inc(S["table_done"], 1)
            dve.wait_ge(S["table_done"], 1)
            for s, (m, a) in enumerate(((1.0, 0.0), (-1.0, -1.0), (1.0, 0.0))):
                dve.wait_ge(S["fields_tr"], EB * (s + 1))
                nc.vector.tensor_scalar(table[:, s, 0:ET], ps[4 + s][:, 0:ET], m, a, ALU.mult, ALU.add) \
                    .then_inc(S["table_done"], 1)

            dve.wait_ge(S["starts_done"], 1)
            nc.vector.memset(window, 0.0).then_inc(S["ohu_ready"], UG)
            with dve.Fori(0, NG // UG) as j:
                for b in range(UG):
                    g = j * UG + b
                    dve.wait_ge(S["bval_ready"], g + 1)
                    dve.wait_ge(S["counts_done"], g + 1)
                    for k in range(BA, CAP):
                        nc.vector.tensor_scalar(onehot_d[:, b % 2, k - BA, :], iota_b[:, :],
                                                bval[:, b, k:k + 1], None, ALU.is_equal)
                    for k in range(CAP):
                        ins = nc.vector.tensor_scalar(onehot_u[:, b % 2, k, :], iota_u[:, :],
                                                      window[:, b, 0, k:k + 1], None, ALU.is_equal)
                    ins.then_inc(S["ohu_ready"], 1)

            def weight_norms(l):
                dve.wait_ge(S["wd_loaded", l], 16)
                dve.wait_ge(S["wcat_loaded", l], 16)
                lower, d_ = Wcat[:, l % 2, :, 0:D], Wd[:, l % 2]
                nc.vector.tensor_tensor(d_, d_, lower, ALU.subtract).then_inc(S["wd_done"], 1)
                dve.wait_ge(S["wd_done"], l + 1)
                sq = squares.rearrange("p (k n) -> p k n", k=KH)
                for i, w_ in enumerate((d_, lower)):
                    step(nc.vector.tensor_tensor(sq, w_, w_, ALU.mult))
                    step(nc.vector.tensor_reduce(norms[:, i:i + 1], sq, AX.XY, ALU.add))
                step(nc.vector.tensor_tensor(squares[:, 0:KH], bcol[:, l, :], bcol[:, l, :], ALU.mult))
                nc.vector.tensor_reduce(norms[:, 2:3], squares[:, 0:KH], AX.X, ALU.add) \
                    .then_inc(S["norm_ready"], 1)

            def set_scale(l):
                dve.wait_ge(S["norm_sum"], l + 1)
                total = ps[1][:, 0:3]
                step(nc.vector.tensor_tensor(bound[:, 1:2], bound[:, 0:1], total[:, 1:2], ALU.mult))
                step(nc.vector.tensor_scalar(expo[:, :], bound[:, 1:2].bitcast(I32), 23, None,
                                             ALU.arith_shift_right))
                step(nc.vector.tensor_scalar(expo[:, :], expo[:, :], -125.0, None, ALU.add))
                step(nc.vector.tensor_scalar(expo[:, :], expo[:, :], 1, None, ALU.arith_shift_right))
                step(nc.vector.tensor_scalar(expo[:, :], expo[:, :], -1.0, 15.0 + 127.0, ALU.mult, ALU.add))
                step(nc.vector.tensor_scalar(expo[:, :], expo[:, :], 127.0, None, ALU.min))
                step(nc.vector.tensor_scalar(scale[:, l, 0:1], expo[:, :], 23, None, ALU.arith_shift_left))
                step(nc.vector.tensor_scalar(expo[:, :], expo[:, :], -1.0, 254.0, ALU.mult, ALU.add))
                step(nc.vector.tensor_scalar(scale[:, l, 1:2], expo[:, :], 23, None, ALU.arith_shift_left))
                step(nc.vector.tensor_copy(norms[:, :], total))
                step(nc.vector.tensor_tensor(bound[:, 1:2], norms[:, 0:1], norms[:, 1:2], ALU.add))
                step(nc.vector.tensor_tensor(bound[:, 1:2], bound[:, 1:2], bound[:, 0:1], ALU.mult))
                step(nc.vector.tensor_scalar(bound[:, 1:2], bound[:, 1:2], 2.0, None, ALU.mult))
                step(nc.vector.tensor_tensor(bound[:, 0:1], bound[:, 1:2], norms[:, 2:3], ALU.add))
                step(nc.vector.tensor_scalar(bound[:, 0:1], bound[:, 0:1], 2.0, None, ALU.mult))
                nc.vector.tensor_scalar(bound[:, 0:1], bound[:, 0:1], 1.0, None, ALU.mult) \
                    .then_inc(S["scale_ready"], 1)

            dve.wait_ge(S["bias_loaded"], 48)
            step(nc.vector.memset(bound[:, :], float(D)))
            weight_norms(0)
            set_scale(0)

            def from_degrees(c, n):
                c0, w = CHUNKS[c]
                dve.wait_ge(S["cnt_done"], n)
                bank = ps[4 + c % 2]
                nc.vector.tensor_scalar(tmp[:, c % 2, 0:w], bank[:, 0:w], 1.0, None, ALU.max) \
                    .then_inc(S["inv_a"], 1)
                nc.vector.tensor_scalar(some[:, c0:c0 + w], bank[:, 0:w], 1.0, None, ALU.min) \
                    .then_inc(S["some_done"], 1)
                dve.wait_ge(S["inv_a"], n)
                nc.vector.reciprocal(inv[:, c0:c0 + w], tmp[:, c % 2, 0:w]).then_inc(S["inv_done"], 1)

            dve.wait_ge(S["counts_stored"], NG + 2)
            for c, (c0, w) in enumerate(CHUNKS):
                dve.wait_ge(S["cnt_done"], c + 1)
                step(nc.vector.tensor_reduce(degree[:, 0, c:c + 1], ps[4 + c % 2][0:1, 0:w], AX.X, ALU.add))
                step(nc.vector.tensor_reduce(degree[:, 1, c:c + 1], ps[4 + c % 2][0:1, 0:w], AX.X, ALU.max))
                from_degrees(c, c + 1)
            step(nc.vector.tensor_reduce(degree[:, 2, 0:1], degree[:, 0, 0:NC], AX.X, ALU.add))
            step(nc.vector.tensor_reduce(degree[:, 2, 1:2], degree[:, 1, 0:NC], AX.X, ALU.max))
            step(nc.vector.tensor_scalar(degree[:, 2, 2:3], degree[:, 2, 0:1], float(E), None, ALU.is_equal))
            step(nc.vector.tensor_scalar(degree[:, 2, 3:4], degree[:, 2, 1:2], 2048.0, None, ALU.is_lt))
            nc.vector.tensor_tensor(flag[0:1, 1:2], degree[:, 2, 2:3], degree[:, 2, 3:4], ALU.mult) \
                .then_inc(S["graph_flag"], 1)
            dve.wait_ge(S["graph_flag"], 1)
            exact = dve.value_load(flag[0:1, 1:2], min_val=0, max_val=1)

            def hot_rows(p):
                c0, w = CHUNKS[p % NC]

                def body(t, rows, first, last):
                    n = p * ET + t
                    dve.wait_ge(S["gen_edges", p // NC], (t + (p % NC * ET + 1)) * 32)
                    nc.vector.tensor_scalar(gen_col[0:rows, :], gen_dst[0:rows, :], -float(c0), None, ALU.add) \
                        .then_inc(S["gen_cols"], 1)
                    dve.wait_ge(S["gen_cols"], n + 1)
                    nc.vector.tensor_scalar(gen_hot[0:rows, 0:w], gen_iota[0:rows, 0:w], gen_col[0:rows, 0:1],
                                            None, ALU.is_equal).then_inc(S["gen_hots"], 1)

                edge_tiles(dve, body)

            with dve.If(exact < 1):
                dve.wait_ge(S["gen_iota_ready"], 1)
                for c in range(NC):
                    hot_rows(c)
                    from_degrees(c, NC + c + 1)
                dve.wait_ge(S["inv_done"], 2 * NC)
                nc.vector.memset(gen_col[:, :], 0.0)
            dve.nop()

            dve.wait_ge(S["inv_done"], len(CHUNKS))
            for l in range(LAYERS + 1):
                for t in range(NT):
                    n = l * NT + t
                    if l < LAYERS:
                        dve.wait_ge(S["y_hi"], n + 1)
                        nc.vector.scalar_tensor_tensor(out=Yp[:, t, 1, :], in0=ps[t % 2][:, 0:D],
                                                       scalar=scale_f[:, l, 0:1], in1=Yp[:, t, 0, :],
                                                       op0=ALU.mult, op1=ALU.subtract).then_inc(S["y_lo"], 1)
                    else:
                        dve.wait_ge(S["y_done"], n + 1)
                    dve.wait_ge(S["att_added"], NT)
                    if l > 0:
                        dve.wait_ge(S["cat_added"], n + 1 - NT)
                    nc.vector.tensor_tensor(X[:, t, :], X[:, t, :], ps[t % 2][:, D:2 * D], ALU.add) \
                        .then_inc(S["cat_added"], 1)
                if l == LAYERS:
                    break
                dve.wait_ge(S["inv_done"], len(CHUNKS))
                for c, (c0, w) in enumerate(CHUNKS):
                    m = l * len(CHUNKS) + c
                    with dve.If(exact < 1):
                        hot_rows(NC + m)
                        dve.nop()
                    dve.wait_ge(S["agg_done"], m + 1)
                    if c:
                        dve.wait_ge(S["h_done"], m * KH)
                    else:
                        dve.wait_ge(S["y_lo"], (l + 1) * NT)
                    for k in range(KH):
                        nc.vector.scalar_tensor_tensor(
                            out=tmp[:, k, 0:w], in0=ps[(2 if c % 2 == 0 else 6) + k][:, 0:w],
                            scalar=scale_f[:, l, 1:2], in1=inv[:, c0:c0 + w], op0=ALU.mult, op1=ALU.mult) \
                            .then_inc(S["t1_done"], 1)
                    dve.wait_ge(S["u_done"], m + 1)
                    for k in range(KH):
                        dve.wait_ge(S["t1_done"], m * KH + k + 1)
                        nc.vector.tensor_tensor(tmp[:, k, 0:w], tmp[:, k, 0:w], ps[4 + k][:, 0:w],
                                                ALU.add).then_inc(S["t2_done"], 1)
                    for k in range(KH):
                        dve.wait_ge(S["t2_done"], m * KH + k + 1)
                        nc.vector.scalar_tensor_tensor(out=tmp[:, k, 0:w], in0=tmp[:, k, 0:w],
                                                       scalar=bcol[:, l, k:k + 1], in1=some[:, c0:c0 + w],
                                                       op0=ALU.add, op1=ALU.mult).then_inc(S["t3_done"], 1)
                    if l + 1 < LAYERS and c == 1:
                        weight_norms(l + 1)
                    if l + 1 < LAYERS and c == 2:
                        set_scale(l + 1)

            dve.wait_ge(S["cat_added"], NT * (LAYERS + 1))
            norm_stats(X, lambda t: None, "x2_bn", "x2_stat")
            nc.vector.tensor_scalar(mean[:, :], stat[:, :, 1], EPS, None, ALU.add).then_inc(S["mean2_done"], 1)
            dve.wait_ge(S["std2_done"], 1)
            nc.vector.reciprocal(rstd[:, :], rstd[:, :]).then_inc(S["rstd2_done"], 1)
            dve.wait_ge(S["rstd2_done"], 1)
            for t in range(NT):
                if t >= 2:
                    dve.wait_ge(S["xt2_done"], t - 1)
                nc.vector.tensor_scalar(xn2[:, t % 2], X[:, t, :], stat[:, t, 0:1], rstd[:, t:t + 1],
                                        ALU.subtract, ALU.mult).then_inc(S["xn2_ready"], 1)

            dve.wait_ge(S["v_loaded"], 48)
            nc.vector.tensor_copy(Vhi, Vraw).then_inc(S["v_hi"], 1)
            dve.wait_ge(S["v_hi"], 1)
            nc.vector.tensor_tensor(Vlo, Vraw, Vhi, ALU.subtract).then_inc(S["v_lo"], 1)
            nc.vector.memset(warm[:, :], 0.0).then_inc(S["warm_done"], 1)
            nc.vector.memset(st[:, 15 * GW:23 * GW], 0.0).then_inc(S["st_init"], 1)
            nc.vector.memset(cell0, 0.0).then_inc(S["st_init"], 1)
            nc.vector.memset(h0, 0.0).then_inc(S["st_init"], 1)
            nc.vector.memset(hist, 0.0).then_inc(S["st_init"], 1)
            nc.vector.memset(h_hi, 0.0).then_inc(S["hhi_done"], 1)
            nc.vector.memset(h_lo, 0.0).then_inc(S["hlo_done"], 1)
            dve.wait_ge(S["g_stored"], (NP // (TC * L)) * 3 * KH)
            nc.vector.tensor_copy(xg[:, L, :], xg[:, 0, :]).then_inc(S["g_wrap"], 1)
            dve.wait_ge(S["st_init"], 4)

            def kc(ap):
                return ap.rearrange("p (k c) -> p k c", k=KH)

            before = hist[:, :, 0:CH * L].rearrange("p k (c t) -> p k c t", t=L)
            behind = hist[:, :, 1:CH * L + 1].rearrange("p k (c t) -> p k c t", t=L)

            def steps(r, full):
                with dve.Fori(0, L // UN) as j:
                    n = r * L + j * UN
                    for u in range(UN):
                        old, new = u % 2, (u + 1) % 2
                        h_old = before[:, :, :, ds(j * UN + u, 1)].rearrange("p k c t -> p k (c t)")
                        h_new = behind[:, :, :, ds(j * UN + u, 1)].rearrange("p k c t -> p k (c t)")
                        nc.vector.tensor_tensor(kc(terms[:, :, 1]), h_old, kc(cell[:, old]), ALU.mult) \
                            .then_inc(S["hc_done"], 1)
                        dve.wait_ge(S["gi_done"], n + (u + 1))
                        dve.wait_ge(S["hc_done"], n + (u + 1))
                        nc.vector.tensor_tensor_scan(pairs[:, new].rearrange("p n o -> p (n o)"),
                                                     factors.rearrange("p n o -> p (n o)"),
                                                     terms.rearrange("p n o -> p (n o)"),
                                                     0.0, ALU.mult, ALU.add).then_inc(S["c_done"], 1)
                        dve.wait_ge(S["tc_done"], n + (u + 1))
                        nc.vector.tensor_tensor(h_hi[:, new], go, tc, ALU.mult) \
                            .then_inc(S["hhi_done"], 1)
                        nc.vector.tensor_tensor(h_new, kc(go), kc(tc), ALU.mult) \
                            .then_inc(S["h_f32"], 1)
                        dve.wait_ge(S["h_f32"], n + (u + 1))
                        nc.vector.tensor_tensor(kc(h_lo[:, new]), h_new, kc(h_hi[:, new]), ALU.subtract) \
                            .then_inc(S["hlo_done"], 1)

            def after(r, look):
                dve.wait_ge(S["hlo_done"], (r + 1) * (L + 1))
                new_h, end_c = before[:, :, :, 0], kc(cell[:, 0])
                old_c = kc(cell0)
                if look is not None:
                    nc.vector.tensor_tensor(diff[:, 0, :, 1:USED], new_h[:, :, 1:USED],
                                            kc(h0)[:, :, 1:USED], ALU.subtract).then_inc(S["end_diff"], 1)
                    nc.vector.tensor_tensor(diff[:, 1, :, 1:USED], end_c[:, :, 0:USED - 1],
                                            old_c[:, :, 1:USED], ALU.subtract).then_inc(S["end_diff"], 1)
                    dve.wait_ge(S["end_diff"], look * 2)
                    nc.vector.tensor_reduce(moved[:, 0:1], diff[:, :, :, 1:USED], AX.XYZ, ALU.max,
                                            apply_absolute_value=True).then_inc(S["end_max"], 1)
                    dve.wait_ge(S["end_tr"], look)
                    nc.vector.tensor_reduce(warm[:, 0:1], ps[6][0:1, 0:P], AX.X, ALU.max) \
                        .then_inc(S["end_total"], 1)
                    dve.wait_ge(S["end_total"], look)
                    nc.vector.tensor_scalar(flag[0:1, 0:1], warm[:, 0:1], TOL, None, ALU.is_gt) \
                        .then_inc(S["end_flag"], 1)
                nc.vector.tensor_copy(kc(h_hi[:, 0]), new_h).then_inc(S["hhi_done"], 1)
                nc.vector.tensor_copy(old_c[:, :, 1:CH], end_c[:, :, 0:CH - 1]).then_inc(S["shift_c"], 1)
                dve.wait_ge(S["hhi_done"], (r + 1) * (L + 1) + 1)
                nc.vector.tensor_tensor(kc(h_lo[:, 0]), new_h, kc(h_hi[:, 0]), ALU.subtract) \
                    .then_inc(S["hlo_done"], 1)
                dve.wait_ge(S["shift_c"], r * 3 + 1)
                nc.vector.tensor_copy(cell[:, 0], cell0).then_inc(S["shift_c"], 1)
                nc.vector.tensor_copy(kc(h0), new_h).then_inc(S["shift_c"], 1)
                dve.wait_ge(S["shift_c"], r * 3 + 3)

            rounds(dve, steps, after)

            nc.vector.drain().then_inc(S["scan_done"], 1)
            for t in range(NT):
                dve.wait_ge(S["ht_done"], t + 1)
                nc.vector.tensor_tensor(X[:, t, :], X[:, t, :], ps[6 + t % 2][:, 0:D], ALU.add) \
                    .then_inc(S["y_added"], 1)

        @block.tensor
        def _(pe):
            def transposes(ready, done, copied, src_):
                for t in range(NT):
                    pe.wait_ge(S[ready], t + 1)
                    if t >= 2:
                        pe.wait_ge(S[copied], t - 1)
                    for k in range(KH):
                        ins = nc.tensor.transpose(ps[t % 2][:, col(k)], src_[:, t % 2, col(k)], ident[:, :])
                    ins.then_inc(S[done], 1)

            pe.wait_ge(S["iota_ready"], 10)
            transposes("xn_ready", "xt_done", "xt_copied", xn)

            def node_product(bank, t, w, off=0):
                for k in range(KH):
                    ins = nc.tensor.matmul(bank[:, off:off + w.shape[2]], hT[:, k, col(t)], w[:, k, :],
                                           start=(k == 0), stop=(k == KH - 1))
                return ins

            pe.wait_ge(S["xt_copied"], NT)
            pe.wait_ge(S["wmix_loaded"], 32)
            for t in range(NT):
                if t >= 2:
                    pe.wait_ge(S["kmax_done"], t)
                node_product(ps[2 + t % 2], t, wqkv[:, :, D:2 * D]).then_inc(S["k_done"], 1)

            def context(t):
                rows = LAST if t == NT - 1 else P
                pe.wait_ge(S["kexp_done"], t + 1)
                pe.wait_ge(S["v_copied"], t + 1)
                if t == 0:
                    pe.wait_ge(S["kmax_done"], NT + 1)
                for k in range(KH):
                    ins = nc.tensor.matmul(ps[2 + k][:, 0:P + 1], kexp[0:rows, t % 2, col(k)],
                                           v1[0:rows, t % 2, k, :], start=(t == 0), stop=(t == NT - 1))
                ins.then_inc(S["ctx_done"], 1)

            for t in range(NT):
                if t >= 2:
                    pe.wait_ge(S["kshift_done"], t - 1)
                    pe.wait_ge(S["v_copied"], t - 1)
                node_product(ps[t % 2], t, wqkv[:, :, D:2 * D])
                node_product(ps[4 + t % 2], t, wqkv[:, :, 2 * D:3 * D]).then_inc(S["kv_done"], 1)
                if t:
                    context(t - 1)
            context(NT - 1)

            def q_product(t):
                if t >= 2:
                    pe.wait_ge(S["qsub_done"], t - 1)
                node_product(ps[t % 2], t, wqkv[:, :, 0:D]).then_inc(S["q_done"], 1)

            pe.wait_ge(S["kshift_done"], NT)
            pe.wait_ge(S["v_copied"], NT)
            q_product(0)
            q_product(1)
            pe.wait_ge(S["ctx_norm"], KH)
            for k in range(KH):
                ins = nc.tensor.transpose(ps[4][:, col(k)], ctxn[:, k, :], ident[:, :])
            ins.then_inc(S["ctx_tr"], 1)
            pe.wait_ge(S["ctx_trc"], 1)
            for k in range(KH):
                ins = nc.tensor.matmul(ps[5][:, k * D:(k + 1) * D], ctxT[:, k, :], wout[:, k, :],
                                       start=True, stop=True)
            ins.then_inc(S["ctxw_done"], 1)
            pe.wait_ge(S["ctxw_copied"], 1)
            for t in range(NT):
                if t and t + 1 < NT:
                    q_product(t + 1)
                pe.wait_ge(S["qn_done"], t + 1)
                if t:
                    pe.wait_ge(S["qt_copied"], t)
                for k in range(KH):
                    ins = nc.tensor.transpose(ps[6][:, col(k)], qn[:, t % 2, col(k)], ident[:, :])
                ins.then_inc(S["qt_done"], 1)
                pe.wait_ge(S["qt_copied"], t + 1)
                if t:
                    pe.wait_ge(S["att_copied"], t)
                for k in range(KH):
                    ins = nc.tensor.matmul(ps[7][:, 0:D], qT[:, t % 2, k, :], ctxw[:, k, :],
                                           start=(k == 0), stop=(k == KH - 1))
                ins.then_inc(S["att_done"], 1)

            pe.wait_ge(S["ctxw_copied"], 1)
            pe.wait_ge(S["att_copied"], NT)
            for s, f in enumerate((fields, fields2, fields3)):
                pe.wait_ge(S["fields_f"], s + 1)
                for b in range(EB):
                    nc.tensor.transpose(ps[4 + s][:, col(b)], f[:, b, :], ident[:, :]) \
                        .then_inc(S["fields_tr"], 1)
            pe.wait_ge(S["less_done"], EB)
            for b in range(EB):
                ins = nc.tensor.matmul(ps[0][0:1, 0:NG + 2], ones_f[:, 0:1], less[:, b, :],
                                       start=(b == 0), stop=(b == EB - 1))
            ins.then_inc(S["starts_sum"], 1)

            pe.sem_inc(S["counts_done"], 2)
            with pe.Fori(0, NG // UG) as j:
                for b in range(UG):
                    g = j * UG + b
                    pe.wait_ge(S["oha_ready"], g + (1 + UG))
                    pe.wait_ge(S["ohu_ready"], g + (1 + UG))
                    pe.wait_ge(S["counts_stored"], g + 1)
                    for k in range(CAP):
                        lhs = onehot_a[:, b, k, :] if k < BA else onehot_d[:, b % 2, k - BA, :]
                        for h in range(2):
                            ins = nc.tensor.matmul(ps[2 * (b % 2) + h][:, 0:CB], lhs,
                                                   onehot_u[:, b % 2, k, h * CB:(h + 1) * CB],
                                                   start=(k == 0), stop=(k == CAP - 1))
                    ins.then_inc(S["counts_done"], 1)

            def sum_norms(l):
                pe.wait_ge(S["norm_ready"], l + 1)
                nc.tensor.matmul(ps[1][:, 0:3], ones_f[:, :], norms[:, :], start=True, stop=True) \
                    .then_inc(S["norm_sum"], 1)

            pe.wait_ge(S["counts_stored"], NG + 2)
            sum_norms(0)
            for c, (c0, w) in enumerate(CHUNKS):
                if c >= 2:
                    pe.wait_ge(S["some_done"], c - 1)
                for s in range(NT):
                    ins = nc.tensor.matmul(ps[4 + c % 2][:, 0:w], ones_h[:, :], AT[:, s, c0:c0 + w],
                                           start=(s == 0), stop=(s == NT - 1))
                ins.then_inc(S["cnt_done"], 1)

            pe.wait_ge(S["graph_flag"], 1)
            exact = pe.value_load(flag[0:1, 1:2], min_val=0, max_val=1)

            def edge_products(p, outs):
                w = CHUNKS[p % NC][1]

                def body(t, rows, first, last):
                    n = p * ET + t
                    pe.wait_ge(S["gen_hots"], n + 1)
                    if p >= NC:
                        pe.wait_ge(S["gen_gathered", p // NC], (t + (p % NC * ET + 1)) * 16)
                    for i, (bank, lhs, begin, end) in enumerate(outs):
                        ins = nc.tensor.matmul(bank[:, 0:w], lhs[0:rows], gen_hot[0:rows, 0:w],
                                               start=first and begin, stop=last and end)
                    ins.then_inc(S["gen_used"], 1)

                edge_tiles(pe, body)

            with pe.If(exact < 1):
                pe.sem_inc(S["gen_used"], 1)
                pe.wait_ge(S["some_done"], NC)
                for c in range(NC):
                    if c >= 2:
                        pe.wait_ge(S["some_done"], NC + c - 1)
                    edge_products(c, [(ps[4 + c % 2], ones_h, True, True)])
                    pe.drain().then_inc(S["cnt_done"], 1)
                pe.wait_ge(S["some_done"], 2 * NC)
                pe.drain()
            pe.nop()

            for l in range(LAYERS + 1):
                if l < LAYERS:
                    pe.wait_ge(S["wcat_loaded", l], 16)
                pe.wait_ge(S["wf_loaded", l], 16)
                if l < LAYERS:
                    pe.wait_ge(S["scale_ready"], l + 1)
                if l:
                    pe.wait_ge(S["h_done"], l * len(CHUNKS) * KH)
                for t in range(NT):
                    n = l * NT + t
                    if n >= 2:
                        pe.wait_ge(S["cat_added"], n - 1)
                    if l < LAYERS:
                        ins = node_product(ps[t % 2], t, Wcat[:, l % 2, :, :])
                    else:
                        ins = node_product(ps[t % 2], t, Wcat[:, l % 2, :, D:2 * D], D)
                    ins.then_inc(S["y_done"], 1)
                if l == LAYERS:
                    break
                pe.wait_ge(S["y_lo"], (l + 1) * NT)
                pe.wait_ge(S["wd_done"], l + 1)
                pe.wait_ge(S["some_done"], len(CHUNKS))
                for c, (c0, w) in enumerate(CHUNKS):
                    m = l * len(CHUNKS) + c
                    base = 2 if c % 2 == 0 else 6
                    if m >= 1:
                        pe.wait_ge(S["t1_done"], m * KH)

                    def block_products(s, start, stop):
                        for part in range(2):
                            for k in range(KH):
                                lhs = Yp[:, ds(s, 1), part, col(k)].rearrange("p s n -> p (s n)")
                                rhs = AT[:, ds(s, 1), c0:c0 + w].rearrange("p s n -> p (s n)")
                                ins = nc.tensor.matmul(ps[base + k][:, 0:w], lhs, rhs,
                                                       start=start and part == 0, stop=stop and part == 1)
                        return ins

                    with pe.If(exact > 0):
                        block_products(0, True, False)
                        with pe.Fori(1, NT - 1) as s:
                            block_products(s, False, False)
                        block_products(NT - 1, False, True).then_inc(S["agg_done"], 1)
                    with pe.Else():
                        edge_products(NC + m, [(ps[base + k], gen_rows[:, part * D + k * P:part * D + (k + 1) * P],
                                                part == 0, part == 1) for k in range(KH) for part in range(2)])
                        pe.drain().then_inc(S["agg_done"], 1)
                    if m:
                        pe.wait_ge(S["t2_done"], m * KH)
                    for k in range(KH):
                        for h in range(KH):
                            ins = nc.tensor.matmul(ps[4 + k][:, 0:w], Wd[:, l % 2, h, col(k)],
                                                   hT[:, h, c0:c0 + w], start=(h == 0), stop=(h == KH - 1))
                    ins.then_inc(S["u_done"], 1)
                    if l + 1 < LAYERS and c == 2:
                        sum_norms(l + 1)

            transposes("xn2_ready", "xt2_done", "xt2_copied", xn2)
            pe.wait_ge(S["xt2_copied"], NT)
            pe.wait_ge(S["u_loaded"], 48)
            TW = TC * L
            for s in range(NP // TW):
                for b in range(3 * KH):
                    n = s * 3 * KH + b
                    if n >= 4:
                        pe.wait_ge(S["g_stored"], n - 3)
                    for k in range(KH):
                        ins = nc.tensor.matmul(ps[n % 4][:, 0:TW], Ucat[:, k, col(b)],
                                               hT[:, k, s * TW:(s + 1) * TW], start=(k == 0), stop=(k == KH - 1))
                    ins.then_inc(S["g_done"], 1)
            pe.wait_ge(S["g_wrap"], 1)
            pe.wait_ge(S["v_lo"], 1)

            def preload(u, t):
                row = xg[:, ds(t, 1), :].rearrange("p t n -> p (t n)")
                for g in range(3):
                    nc.tensor.matmul(ps[2 * g + u % 2][:, 0:GW], ident[:, :], row[:, g * GW:(g + 1) * GW],
                                     start=True, stop=False, skip_group_check=True)

            def steps(r, full):
                with pe.Fori(0, L // UN) as j:
                    nh = (r * (L + 1)) + j * UN
                    for u in range(UN):
                        def add(b, h, weights, last=False):
                            bank, o = ps[b // KH * 2 + u % 2], b % KH * CH
                            for k in range(KH):
                                for i, w in enumerate(weights):
                                    ins = nc.tensor.matmul(bank[:, o:o + CH], w[:, k, col(b)],
                                                           h[:, u % 2, k * CH:(k + 1) * CH], start=False,
                                                           stop=last and k == KH - 1, skip_group_check=True)
                            return ins

                        pe.wait_ge(S["hhi_done"], nh + (u + 1))
                        if not full:
                            for pair, done in (((2, 3), "cg_done"), ((0, 1), "ci_done"), ((4, 5), "co_done")):
                                if done == "co_done":
                                    pe.wait_ge(S["hlo_done"], nh + (u + 1))
                                for b in pair:
                                    ins = add(b, h_hi, (Vhi,), True)
                                ins.then_inc(S[done], 1)
                            preload(u + 1, j * UN + (u + 1))
                            continue
                        for b in (2, 3, 0, 1):
                            add(b, h_hi, (Vhi, Vlo))
                        pe.wait_ge(S["hlo_done"], nh + (u + 1))
                        add(2, h_lo, (Vhi,), True)
                        add(3, h_lo, (Vhi,), True).then_inc(S["cg_done"], 1)
                        add(0, h_lo, (Vhi,), True)
                        add(1, h_lo, (Vhi,), True).then_inc(S["ci_done"], 1)
                        for b in (4, 5):
                            add(b, h_hi, (Vhi, Vlo))
                            ins = add(b, h_lo, (Vhi,), True)
                        ins.then_inc(S["co_done"], 1)
                        preload(u + 1, j * UN + (u + 1))

            def after(r, look):
                if look is not None:
                    pe.wait_ge(S["end_max"], look)
                    nc.tensor.transpose(ps[6][0:1, 0:P], moved[:, 0:1], ident[:, :]).then_inc(S["end_tr"], 1)

            preload(0, 0)
            rounds(pe, steps, after)

            pe.wait_ge(S["scan_done"], 1)
            for t in range(NT):
                if t >= 2:
                    pe.wait_ge(S["y_added"], t - 1)
                for k in range(KH):
                    ins = nc.tensor.transpose(ps[6 + t % 2][:, col(k)],
                                              hist[:, k, 1 + t * P:1 + (t + 1) * P], ident[:, :])
                ins.then_inc(S["ht_done"], 1)


_INS = ["x", "src", "dst", "L0_gnn_W0", "L0_gnn_b0", "L0_gnn_W1", "L0_gnn_b1", "L0_gnn_W2", "L0_gnn_b2",
        "L0_gnn_Wf", "L0_gnn_bf", "L0_mix_Wqkv", "L0_mix_Wout", "L0_mix_gamma",
        "L0_ffn_U_i", "L0_ffn_V_i", "L0_ffn_b_i", "L0_ffn_U_f", "L0_ffn_V_f", "L0_ffn_b_f",
        "L0_ffn_U_c", "L0_ffn_V_c", "L0_ffn_b_c", "L0_ffn_U_o", "L0_ffn_V_o", "L0_ffn_b_o"]


def kernel(**inputs):
    import numpy as np
    import concourse.bacc as bacc
    from concourse.bass_utils import run_bass_kernel_spmd

    nc = bacc.Bacc("TRN2", target_bir_lowering=False, num_devices=1)
    arrays, args = {}, []
    for name in _INS:
        a = np.ascontiguousarray(inputs[name])
        arrays[f"in_{name}"] = a
        args.append(nc.dram_tensor(f"in_{name}", a.shape, mybir.dt.from_np(a.dtype), kind="ExternalInput").ap())
    out = nc.dram_tensor("out", inputs["x"].shape, F32, kind="ExternalOutput").ap()
    graph_layer_kernel(nc, *args, out)
    r = run_bass_kernel_spmd(nc, [arrays], core_ids=[0])
    return r.results[0]["out"]
```

```python
import concourse.bass as bass
from concourse import mybir
from contextlib import ExitStack

F32 = mybir.dt.float32
FP16 = mybir.dt.float16
I32 = mybir.dt.int32
U32 = mybir.dt.uint32
ALU = mybir.AluOpType
ACT = mybir.ActivationFunctionType
AX = mybir.AxisListType
ds = bass.ds


def graph_layer_kernel(nc, x, src, dst, W0, b0, W1, b1, W2, b2, Wf, bf, Wqkv, Wout, gamma,
                       U_i, V_i, b_i, U_f, V_f, b_f, U_c, V_c, b_c, U_o, V_o, b_o, out):
    P = nc.NUM_PARTITIONS
    N, D = x.shape
    E = src.shape[0]
    KH = D // P
    NT = -(-N // P)
    NP = NT * P
    LAST = N - (NT - 1) * P
    HEADS, DH = 8, 32
    SCALE = DH ** -0.5
    EPS = 1e-5
    LAYERS = 3

    G, CAP = 32, 6
    UG = 4
    NG = UG * (-(-N // (UG * G)))
    BA = 3
    ND = NG * G
    COMB = NT * G
    CB = COMB // 2
    ET = -(-E // P)
    EB = -(-ET // P)
    EL = E - (ET - 1) * P
    ETP = ET + CAP + 1
    CW = 512
    CHUNKS = [(c, min(CW, ND - c)) for c in range(0, ND, CW)]

    CH, L, UN = 32, 80, 8
    USED = -(-N // L)
    WARM = 3
    SKIP = UN
    COARSE = 7 * UN
    TOL = 2.0 ** -15
    TC = 4
    GW = KH * CH
    assert CH * L == NP and (NT - 2) % 3 == 0

    y_dram = nc.dram_tensor("y_dram", (NP, 2 * D), FP16, kind="Internal").ap()

    ctx = ExitStack()
    with ctx:
        def sb(name, shape, dt):
            return ctx.enter_context(nc.sbuf_tensor(name, shape, dt))

        def sem(name):
            return ctx.enter_context(nc.semaphore(name))

        ps = [ctx.enter_context(nc.psum_tensor(f"bank{i}", [P, 512], F32)) for i in range(8)]

        X = sb("X", [P, NT, D], F32)
        hT = sb("hT", [P, KH, NP], F32)
        AT = sb("AT", [P, NT, ND], FP16)
        Yp = sb("Yp", [P, NT, 2, D], FP16)
        rz = sb("rz", [P, ND + ND // 2], F32)
        inv = rz[:, 0:ND]
        some = rz[:, ND:ND + ND // 2].bitcast(FP16)
        Wcat = sb("Wcat", [P, 2, KH, 2 * D], F32)
        Wd = sb("Wd", [P, 2, KH, D], F32)
        tmp = sb("tmp", [P, KH, CW], F32)
        ident = sb("ident", [P, P], F32)
        ones_h = sb("ones_h", [P, P], FP16)
        ones_f = sb("ones_f", [P, P], F32)
        bcol = sb("bcol", [P, LAYERS, KH], F32)
        gcol = sb("gcol", [P, 3, KH], F32)
        mean = sb("mean", [P, NT], F32)
        rstd = sb("rstd", [P, NT], F32)
        stat = sb("stat", [P, NT, 2], F32)
        bn6 = sb("bn6", [P, 2, 6], F32)
        flag = sb("flag", [1, 4], I32)
        warm = sb("warm", [1, 2], F32)

        gen_rows = sb("gen_rows", [P, 2 * D], FP16)
        gen_hot = sb("gen_hot", [P, CW], FP16)
        gen_iota = sb("gen_iota", [P, CW], I32)
        gen_src = sb("gen_src", [P, 1], U32)
        gen_dst = sb("gen_dst", [P, 1], I32)
        gen_col = sb("gen_col", [P, 1], F32)
        norms = sb("norms", [P, 3], F32)
        bound = sb("bound", [P, 3], F32)
        scale = sb("scale", [P, LAYERS, 2], I32)
        scale_f = scale[:, :, :].bitcast(F32)
        expo = sb("expo", [P, 1], I32)
        degree = sb("degree", [1, 4, 8], F32)

        at32 = AT[:, :, :].rearrange("p a b -> p (a b)").bitcast(F32)
        yp32 = Yp[:, :, :, :].rearrange("p a b c -> p (a b c)").bitcast(F32)
        cut = [0]

        def early(n):
            cut[0] += n
            return at32[:, cut[0] - n:cut[0]]

        wqkv = early(KH * 3 * D).rearrange("p (k n) -> p k n", k=KH)
        wout = early(KH * D).rearrange("p (k n) -> p k n", k=KH)
        gam = early(D)
        bfb = early(D)
        kmax = early(D)
        kmaxb = early(D)
        kshift = early(2 * D).rearrange("p (b n) -> p b n", b=2)
        kexp = early(2 * D).rearrange("p (b n) -> p b n", b=2)
        kraw = early(NT * D).rearrange("p (t n) -> p t n", t=NT)
        v1 = early(NT * KH * (P + 1)).rearrange("p (t k n) -> p t k n", t=NT, k=KH)
        ctxn = early(KH * P).rearrange("p (k n) -> p k n", k=KH)
        ctxT = early(KH * P).rearrange("p (k n) -> p k n", k=KH)
        den = early(2 * KH)
        hmask = early(P)
        ctxw = early(KH * D).rearrange("p (k n) -> p k n", k=KH)
        qs = early(2 * D).rearrange("p (b n) -> p b n", b=2)
        qn = early(2 * D).rearrange("p (b n) -> p b n", b=2)
        qT = early(2 * D).rearrange("p (b k n) -> p b k n", b=2, k=KH)
        qmx = early(2 * 3 * HEADS).rearrange("p (b s h) -> p b s h", b=2, s=3)
        xn = early(2 * D).rearrange("p (b n) -> p b n", b=2)
        att = kraw

        cut2 = [0]

        def build(n32):
            cut2[0] += n32
            assert cut2[0] <= ND + ND // 2
            return rz[:, cut2[0] - n32:cut2[0]]

        onehot_u = build(2 * CAP * COMB // 2).bitcast(FP16).rearrange("p (b k n) -> p b k n", b=2, k=CAP)
        iota_u = sb("iota_u", [P, COMB], FP16)
        iota_b = sb("iota_b", [P, P], FP16)
        iota_g = sb("iota_g", [P, NG + 2], F32)
        starts = sb("starts", [1, NG + 2], I32)
        onehot_a = tmp[:, :, :].rearrange("p k n -> p (k n)")[:, 0:UG * BA * P // 2] \
            .bitcast(FP16).rearrange("p (b k n) -> p b k n", b=UG, k=BA)
        away = gen_hot[:, 0:BA * P].rearrange("p (k n) -> p k n", k=BA)
        onehot_d = sb("onehot_d", [P, 2, CAP - BA, P], FP16)
        tw = 3 * (ETP + ETP % 2) // 2
        w1 = max(tw, COMB, KH * D)
        widths = [w1, 3 * UG * CAP, UG * CAP, UG * CAP, EB * (NG + 2), EB * P, NG + 2, EB, UG]
        work = sb("work", [P, sum(widths)], F32)
        at = [sum(widths[:i]) for i in range(len(widths) + 1)]
        part = [work[:, at[i]:at[i + 1]] for i in range(len(widths))]
        iota_i = part[0][:, 0:COMB].bitcast(I32)
        table = part[0][:, 0:tw].bitcast(FP16).rearrange("p (s t) -> p s t", s=3)
        squares = part[0][:, 0:KH * D]
        window = part[1].rearrange("p (b s k) -> p b s k", b=UG, s=3)
        match = part[2].rearrange("p (b k) -> p b k", b=UG)
        bval = part[3].rearrange("p (b k) -> p b k", b=UG)
        less = part[4].rearrange("p (b g) -> p b g", b=EB)
        fields3 = part[5].rearrange("p (b e) -> p b e", b=EB)
        iota_first, first, number = part[6], part[7], part[8]
        wd32 = Wd[:, :, :, :].rearrange("p a k n -> p (a k n)")
        raw = Wcat[:, :, :, :].rearrange("p a k n -> p (a k n)")
        sraw = raw[:, 0:EB * P].bitcast(I32).rearrange("p (b e) -> p b e", b=EB)
        draw = raw[:, EB * P:2 * EB * P].bitcast(I32).rearrange("p (b e) -> p b e", b=EB)
        f_i = raw[:, 2 * EB * P:3 * EB * P].bitcast(I32).rearrange("p (b e) -> p b e", b=EB)
        f_j = raw[:, 3 * EB * P:4 * EB * P].bitcast(I32).rearrange("p (b e) -> p b e", b=EB)
        fields = wd32[:, 0:EB * P].rearrange("p (b e) -> p b e", b=EB)
        fields2 = wd32[:, EB * P:2 * EB * P].rearrange("p (b e) -> p b e", b=EB)

        xg = at32[:, 0:(L + 1) * 3 * GW].rearrange("p (t n) -> p t n", t=L + 1)
        o1 = (L + 1) * 3 * GW
        hist = at32[:, o1:o1 + KH * (CH * L + 1)].rearrange("p (k n) -> p k n", k=KH)
        assert o1 + KH * (CH * L + 1) <= NT * ND // 2
        Ucat = Wcat[:, :, :, :].rearrange("p a k n -> p (a k n)")[:, 0:KH * 3 * D] \
            .rearrange("p (k n) -> p k n", k=KH)
        Vraw = rz[:, 0:KH * 3 * D].rearrange("p (k n) -> p k n", k=KH)
        Vhi = rz[:, KH * 3 * D:KH * 3 * D + KH * 3 * D // 2].bitcast(FP16) \
            .rearrange("p (k n) -> p k n", k=KH)
        Vlo = wd32[:, 0:KH * 3 * D // 2].bitcast(FP16).rearrange("p (k n) -> p k n", k=KH)
        xn2 = yp32[:, 0:2 * D].rearrange("p (b n) -> p b n", b=2)

        st = yp32[:, 2 * D:]
        factors = st[:, 15 * GW:17 * GW].rearrange("p (n o) -> p n o", o=2)
        terms = st[:, 17 * GW:19 * GW].rearrange("p (n o) -> p n o", o=2)
        pairs = st[:, 19 * GW:23 * GW].rearrange("p (b n o) -> p b n o", b=2, o=2)
        cell = pairs[:, :, :, 1]
        cell0 = st[:, 2 * GW:3 * GW]
        h0 = st[:, 14 * GW:15 * GW]
        tc = st[:, 5 * GW:6 * GW]
        go = st[:, 6 * GW:7 * GW]
        diff = st[:, 9 * GW:11 * GW].rearrange("p (b k c) -> p b k c", b=2, k=KH)
        moved = st[:, 11 * GW:11 * GW + 2]
        h_hi = st[:, 12 * GW:13 * GW].bitcast(FP16).rearrange("p (b n) -> p b n", b=2)
        h_lo = st[:, 13 * GW:14 * GW].bitcast(FP16).rearrange("p (b n) -> p b n", b=2)

        names = """x_last_loaded wmix_loaded mixvec_loaded edges_loaded bias_loaded
        const_ready iota_ready x_bn x_stat var_done std_done rstd_done xn_ready xt_done xt_copied
        kv_done k_copied kmax_done kmaxb_ready kshift_done kexp_done v_copied v_ones ctx_done
        ctx_den ctx_norm ctx_tr ctx_trc ctxw_done ctxw_copied
        q_done qmax_done qsub_done qexp_done qsum_done qrec_done qn_done qt_done qt_copied
        att_done att_copied att_bn att_stats att_std att_rstd att_n att_added bf_added
        raw_set dve_step first_ready less_done starts_sum starts_done fields_tr table_done
        fields_f
        window_set match_ready bval_ready ohu_ready away_done oha_ready counts_done counts_stored
        cnt_done inv_a inv_done some_done
        wd_done y_done y_hi y_lo cat_added agg_done u_done t1_done t2_done t3_done h_done
        mean2_done norm_ready norm_sum scale_ready
        std2_done rstd2_done x2_bn x2_stat xn2_ready xt2_done xt2_copied
        u_loaded v_loaded gb_loaded g_done g_stored g_wrap v_hi v_lo st_init
        cg_done ci_done co_done gg_done gi_done go_done hc_done c_done tc_done hhi_done h_f32
        hlo_done end_diff end_total end_max end_tr end_flag shift_c noted
        gen_cols gen_hots gen_used y_stored gen_iota_ready graph_flag
        scan_done ht_done y_added out_stored warm_done""".split()
        S = {n: sem(n) for n in names}
        for l_ in range(LAYERS + 1):
            S["x_loaded", l_] = sem(f"x_loaded{l_}")
            for n_ in ("gen_edges", "gen_gathered"):
                S[n_, l_] = sem(f"{n_}{l_}")
            for n_ in ("wcat_loaded", "wf_loaded", "wd_loaded"):
                S[n_, l_] = sem(f"{n_}{l_}")

        XT = -(-(NT - 1) // (LAYERS + 1))
        FT = 13

        block = ctx.enter_context(nc.Block())

        def col(t):
            return slice(t * P, (t + 1) * P)

        NC = len(CHUNKS)

        def degree_bank(c):
            return ps[(4 + c) % 8]

        def edge_tiles(eng, body):
            body(0, P, True, False)
            with eng.Fori(1, ET - 1) as t:
                body(t, P, False, False)
            body(ET - 1, EL, False, True)

        def rounds(eng, steps, after):
            steps(0, SKIP, L, False)
            after(0, None)
            steps(1, 0, COARSE, False)
            steps(1, COARSE, L, True)
            after(1, None)
            with eng.Fori(2, WARM) as r:
                steps(r, 0, L, True)
                after(r, None)
            steps(WARM, 0, L, True)
            after(WARM, 1)
            eng.wait_ge(S["end_flag"], 1)
            moving = eng.value_load(flag[0:1, 0:1], min_val=0, max_val=1)
            with eng.If(moving > 0):
                with eng.Fori(0, USED + 1 - WARM) as r:
                    still = eng.value_load(flag[0:1, 0:1], min_val=0, max_val=1)
                    with eng.If(still > 0):
                        steps(r + (WARM + 1), 0, L, True)
                        after(r + (WARM + 1), r + 2)
                        eng.wait_ge(S["end_flag"], r + 2)
                        eng.sem_inc(S["noted"], 1)
                    eng.nop()
                eng.nop()
            eng.nop()

        TW = TC * L

        def gate_input_order(transpose, gates):
            t = 0
            for s in range(-1, NP // TW):
                while t < min(NT, -(-(s + 2) * TW // P)):
                    transpose(t)
                    t += 1
                if s >= 0:
                    gates(s)

        @block.sync
        def _(sp):
            sp.wait_ge(S["const_ready"], 1)
            full = x[0:(NT - 1) * P, :].rearrange("(t p) d -> p t d", p=P)
            for i, t in enumerate(range(0, NT - 1, XT)):
                u = min(t + XT, NT - 1)
                sp.dma_start(X[:, t:u, :], full[:, t:u, :]).then_inc(S["x_loaded", i], 16)
            sp.dma_start(X[0:LAST, NT - 1, :], x[(NT - 1) * P:N, :]).then_inc(S["x_last_loaded"], 16)
            sp.dma_start(wqkv, Wqkv.rearrange("(k p) n -> p k n", p=P)).then_inc(S["wmix_loaded"], 16)
            sp.dma_start(wout, Wout.rearrange("(k p) n -> p k n", p=P)).then_inc(S["wmix_loaded"], 16)
            sp.dma_start(gam, gamma.partition_broadcast(P)).then_inc(S["mixvec_loaded"], 16)
            sp.dma_start(bfb, bf.partition_broadcast(P)).then_inc(S["mixvec_loaded"], 16)
            with nc.allow_non_contiguous_dma("short bias columns"):
                for l, b in enumerate((b0, b1, b2)):
                    sp.dma_start(bcol[:, l, :], b.rearrange("(k p) -> p k", p=P)).then_inc(S["bias_loaded"], 16)
                for g, b in enumerate((b_i, b_c, b_o)):
                    sp.dma_start(gcol[:, g, :], b.rearrange("(k p) -> p k", p=P)).then_inc(S["gb_loaded"], 16)
            sp.wait_ge(S["raw_set"], 2)
            for raw_, e in ((sraw, src), (draw, dst)):
                full_b = (ET - 1) // P
                sp.dma_start(raw_[:, 0:full_b, :], e[0:full_b * P * P].rearrange("(b p e) -> p b e", p=P, e=P)) \
                    .then_inc(S["edges_loaded"], 16)
                rest = ET - 1 - full_b * P
                sp.dma_start(raw_[0:rest, full_b, :],
                             e[full_b * P * P:(ET - 1) * P].rearrange("(p e) -> p e", e=P)) \
                    .then_inc(S["edges_loaded"], 16)
                sp.dma_start(raw_[rest:rest + 1, full_b, 0:EL],
                             e[(ET - 1) * P:E].rearrange("(p e) -> p e", p=1)).then_inc(S["edges_loaded"], 16)
            Ws = (W0, W1, W2)
            for l in range(LAYERS + 1):
                if l == 0:
                    sp.wait_ge(S["fields_tr"], 9)
                if l >= 2:
                    sp.wait_ge(S["y_done"], NT * (l - 1))
                if l < LAYERS:
                    sp.dma_start(Wcat[:, l % 2, :, 0:D], Ws[l][D:2 * D, :].rearrange("(k p) n -> p k n", p=P)) \
                        .then_inc(S["wcat_loaded", l], 16)
                sp.dma_start(Wcat[:, l % 2, :, D:2 * D],
                             Wf[l * D:(l + 1) * D, :].rearrange("(k p) n -> p k n", p=P)) \
                    .then_inc(S["wf_loaded", l], 16)
                if l < LAYERS:
                    if l >= 2:
                        sp.wait_ge(S["u_done"], len(CHUNKS) * (l - 1))
                    sp.dma_start(Wd[:, l % 2, :, :], Ws[l][0:D, :].rearrange("(k p) n -> p k n", p=P)) \
                        .then_inc(S["wd_loaded", l], 16)
            sp.wait_ge(S["y_done"], NT * (LAYERS + 1))
            for g, u in enumerate((U_i, U_c, U_o)):
                sp.dma_start(Ucat[:, :, g * D:(g + 1) * D], u.rearrange("(k p) n -> p k n", p=P)) \
                    .then_inc(S["u_loaded"], 16)
            sp.wait_ge(S["h_done"], LAYERS * len(CHUNKS) * KH)
            for g, v in enumerate((V_i, V_c, V_o)):
                sp.dma_start(Vraw[:, :, g * D:(g + 1) * D], v.rearrange("(k p) n -> p k n", p=P)) \
                    .then_inc(S["v_loaded"], 16)
            for t in range(0, NT - 1, 4):
                n = min(4, NT - 1 - t)
                sp.wait_ge(S["y_added"], t + n)
                sp.dma_start(out[t * P:(t + n) * P, :].rearrange("(t p) d -> p t d", p=P),
                             X[:, t:t + n, :]).then_inc(S["out_stored"], 16)
            sp.wait_ge(S["y_added"], NT)
            sp.dma_start(out[(NT - 1) * P:N, :], X[0:LAST, NT - 1, :]).then_inc(S["out_stored"], 16)
            sp.wait_ge(S["out_stored"], 16 * (-(-(NT - 1) // 4) + 1))

        @block.gpsimd
        def _(pool):
            nc.gpsimd.memset(ident[:, :], 0.0).then_inc(S["iota_ready"], 1)
            nc.gpsimd.memset(hmask, 1.0).then_inc(S["iota_ready"], 1)
            nc.gpsimd.memset(ones_h[:, :], 1.0)
            nc.gpsimd.memset(ones_f[:, :], 1.0)
            pool.wait_ge(S["iota_ready"], 2)
            nc.gpsimd.affine_select(out=ident[:, :], in_=ident[:, :], compare_op=ALU.not_equal, fill=1.0,
                                    base=0, pattern=[[-1, P]], channel_multiplier=1).then_inc(S["iota_ready"], 1)
            hm = hmask.rearrange("p (h c) -> p h c", c=DH)
            nc.gpsimd.affine_select(out=hm, in_=hm, compare_op=ALU.is_ge, fill=0.0,
                                    base=0, pattern=[[-DH, P // DH], [0, DH]], channel_multiplier=1) \
                .then_inc(S["iota_ready"], 1)
            pool.wait_ge(S["iota_ready"], 4)
            nc.gpsimd.affine_select(out=hm, in_=hm, compare_op=ALU.is_ge, fill=0.0,
                                    base=DH - 1, pattern=[[DH, P // DH], [0, DH]], channel_multiplier=-1) \
                .then_inc(S["iota_ready"], 1)
            nc.gpsimd.iota(iota_i, [[1, COMB]], base=0, channel_multiplier=0).then_inc(S["iota_ready"], 1)
            pool.wait_ge(S["iota_ready"], 6)
            nc.gpsimd.tensor_scalar(iota_u[:, :], iota_i, 1.0, 0.0, ALU.mult, ALU.add) \
                .then_inc(S["iota_ready"], 1)
            nc.gpsimd.tensor_scalar(iota_b[:, :], iota_i[:, 0:P], -1.0, -1.0, ALU.mult, ALU.add) \
                .then_inc(S["iota_ready"], 1)
            nc.gpsimd.tensor_scalar(iota_g[:, :], iota_i[:, 0:NG + 2], 1.0, 0.0, ALU.mult, ALU.add) \
                .then_inc(S["iota_ready"], 1)
            nc.gpsimd.tensor_scalar(iota_first, iota_i[:, 0:NG + 2], float(G), 0.0, ALU.mult, ALU.add) \
                .then_inc(S["iota_ready"], 1)

            pool.wait_ge(S["kmax_done"], NT + 1)
            nc.gpsimd.partition_all_reduce(kmaxb, kmax, P, bass.bass_isa.ReduceOp.max) \
                .then_inc(S["kmaxb_ready"], 1)
            pool.wait_ge(S["mixvec_loaded"], 32)
            pool.wait_ge(S["xn_ready"], NT)
            for t in range(NT):
                ins = nc.gpsimd.tensor_tensor(X[:, t, :], X[:, t, :], bfb, ALU.add)
            ins.then_inc(S["bf_added"], 1)

            pool.wait_ge(S["table_done"], 4)
            pool.wait_ge(S["starts_done"], 1)
            with pool.Fori(0, NG // UG) as j:
                for b in range(UG):
                    g = j * UG + b
                    start = pool.value_load(starts[0:1, ds(g, 1)], min_val=0, max_val=ET - 1)
                    pool.wait_ge(S["ohu_ready"], g + 1)
                    pool.wait_ge(S["oha_ready"], g + 1)
                    nc.gpsimd.tensor_copy(window[:, b], table[:, :, ds(start, CAP)]) \
                        .then_inc(S["window_set"], 1)
                    nc.gpsimd.tensor_copy(number[:, b:b + 1], iota_g[:, ds(g, 1)]).then_inc(S["window_set"], 1)
                    pool.wait_ge(S["window_set"], g * 2 + 2)
                    pool.sem_inc(S["noted"], 1)
                    nc.gpsimd.tensor_scalar(match[:, b], window[:, b, 2, :], number[:, b:b + 1], None,
                                            ALU.is_equal).then_inc(S["match_ready"], 1)
                    pool.wait_ge(S["match_ready"], g + 1)
                    nc.gpsimd.tensor_tensor(bval[:, b], match[:, b], window[:, b, 1, :], ALU.mult) \
                        .then_inc(S["bval_ready"], 1)

            nc.gpsimd.iota(gen_iota[:, :], [[1, CW]], base=0, channel_multiplier=0) \
                .then_inc(S["gen_iota_ready"], 1)
            pool.wait_ge(S["graph_flag"], 1)
            exact = pool.value_load(flag[0:1, 1:2], min_val=0, max_val=1)

            def load_edges(p, gather):
                def body(t, rows, first, last):
                    n = p * ET + t
                    pool.wait_ge(S["gen_used"], n + 1)
                    if rows == P:
                        s_, d_ = src[ds(t * P, P)], dst[ds(t * P, P)]
                    else:
                        s_, d_ = src[(ET - 1) * P:E], dst[(ET - 1) * P:E]
                    pool.dma_start(gen_src[0:rows, :], s_.bitcast(U32).rearrange("(p o) -> p o", o=1)) \
                        .then_inc(S["gen_edges", p // NC], 16)
                    pool.dma_start(gen_dst[0:rows, :], d_.rearrange("(p o) -> p o", o=1)) \
                        .then_inc(S["gen_edges", p // NC], 16)
                    if gather:
                        pool.wait_ge(S["gen_edges", p // NC], (t + (p % NC * ET + 1)) * 32)
                        pool.sem_inc(S["noted"], 1)
                        nc.gpsimd.indirect_dma_start(
                            out=gen_rows[0:rows, :], out_offset=None, in_=y_dram[:, :],
                            in_offset=bass.IndirectOffsetOnAxis(ap=gen_src[0:rows, 0:1], axis=0)) \
                            .then_inc(S["gen_gathered", p // NC], 16)

                with nc.allow_non_contiguous_dma("edges to partitions"):
                    edge_tiles(pool, body)

            with pool.If(exact < 1):
                for c in range(NC):
                    load_edges(c, False)
                for l in range(LAYERS):
                    pool.wait_ge(S["y_lo"], (l + 1) * NT)
                    pool.dma_start(y_dram.rearrange("(s p) m -> p s m", p=P),
                                   Yp[:, :, :, :].rearrange("p s a m -> p s (a m)")).then_inc(S["y_stored"], 16)
                    pool.wait_ge(S["y_stored"], 16 * (l + 1))
                    for c in range(NC):
                        load_edges((l + 1) * NC + c, True)
                pool.nop()
            pool.nop()

        @block.scalar
        def _(act):
            def transposed_copies(done, copied, dest):
                for t in range(NT):
                    act.wait_ge(S[done], t + 1)
                    nc.scalar.copy(dest[:, :, col(t)], ps[t % 2][:, 0:D].rearrange("p (k n) -> p k n", k=KH)) \
                        .then_inc(S[copied], 1)

            act.wait_ge(S["var_done"], 1)
            nc.scalar.activation(rstd[:, :], mean[:, :], ACT.Sqrt).then_inc(S["std_done"], 1)
            transposed_copies("xt_done", "xt_copied", hT)

            for t in range(NT):
                rows = LAST if t == NT - 1 else P
                act.wait_ge(S["kv_done"], t + 1)
                nc.scalar.copy(kraw[0:rows, t, :], ps[2 + t % 2][0:rows, 0:D]).then_inc(S["k_copied"], 1)
                nc.scalar.copy(v1[0:rows, t, :, 0:P],
                               ps[2 + t % 2][0:rows, D:2 * D].rearrange("p (k n) -> p k n", k=KH)) \
                    .then_inc(S["v_copied"], 1)
            for t in range(NT):
                rows = LAST if t == NT - 1 else P
                act.wait_ge(S["kshift_done"], t + 1)
                if t >= 2:
                    act.wait_ge(S["ctx_done"], t - 1)
                nc.scalar.activation(kexp[0:rows, t % 2], kshift[0:rows, t % 2], ACT.Exp) \
                    .then_inc(S["kexp_done"], 1)
            act.wait_ge(S["ctx_tr"], 1)
            nc.scalar.copy(ctxT, ps[4][:, 0:D].rearrange("p (k n) -> p k n", k=KH)).then_inc(S["ctx_trc"], 1)
            act.wait_ge(S["ctxw_done"], 1)
            nc.scalar.copy(ctxw, ps[5][:, :].rearrange("p (k n) -> p k n", k=KH)).then_inc(S["ctxw_copied"], 1)
            for t in range(NT + 2):
                if t < NT:
                    act.wait_ge(S["qsub_done"], t + 1)
                    nc.scalar.activation(qs[:, t % 2], qs[:, t % 2], ACT.Exp).then_inc(S["qexp_done"], 1)
                if 1 <= t <= NT:
                    act.wait_ge(S["qt_done"], t)
                    nc.scalar.copy(qT[:, (t - 1) % 2],
                                   ps[2 + (t - 1) % 2][:, 0:D].rearrange("p (k n) -> p k n", k=KH)) \
                        .then_inc(S["qt_copied"], 1)
                if t >= 2:
                    act.wait_ge(S["att_done"], t - 1)
                    nc.scalar.copy(att[:, t - 2, :], ps[6 + t % 2][:, 0:D]).then_inc(S["att_copied"], 1)
            act.wait_ge(S["att_stats"], NT + 1)
            nc.scalar.activation(rstd[:, :], mean[:, :], ACT.Sqrt).then_inc(S["att_std"], 1)

            def first_parts(l):
                act.wait_ge(S["scale_ready"], l + 1)
                for t in range(NT):
                    n = l * NT + t
                    act.wait_ge(S["y_done"], n + 1)
                    nc.scalar.activation(Yp[:, t, 0, :], ps[t % 2][:, 0:D], ACT.Identity,
                                         scale=scale_f[:, l, 0:1]).then_inc(S["y_hi"], 1)

            first_parts(0)

            def distances(g, b):
                act.wait_ge(S["bval_ready"], g + 1)
                act.wait_ge(S["oha_ready"], g + UG)
                for k in range(BA):
                    ins = nc.scalar.activation(away[:, k, :], iota_b[:, :], ACT.Abs,
                                               bias=bval[:, b % UG, k:k + 1], scale=-1.0)
                ins.then_inc(S["away_done"], 1)

            def from_distances(g, b):
                act.wait_ge(S["away_done"], g + 1)
                nc.scalar.activation(onehot_a[:, b % UG], away, ACT.Relu, bias=ones_f[:, 0:1], scale=-1.0) \
                    .then_inc(S["oha_ready"], 1)

            def store(g, b, ahead):
                if ahead:
                    distances(g + 2, b + 2)
                act.wait_ge(S["counts_done"], g + 3)
                for h in range(2):
                    ins = nc.scalar.copy(AT[:, h * (NT // 2):(h + 1) * (NT // 2), ds(g * G, G)],
                                         ps[2 * (b % 2) + h][:, 0:CB].rearrange("p (a n) -> p a n", n=G))
                ins.then_inc(S["counts_stored"], 1)
                if ahead:
                    from_distances(g + 2, b + 2)

            act.sem_inc(S["counts_stored"], 2)
            act.sem_inc(S["oha_ready"], UG)
            act.wait_ge(S["iota_ready"], 10)
            for g in range(2):
                distances(g, g)
                from_distances(g, g)
            with act.Fori(0, NG // UG - 1) as j:
                for b in range(UG):
                    store(j * UG + b, b, True)
            for b in range(UG):
                store(NG - UG + b, b, b + 2 < UG)

            for l in range(LAYERS):
                if l:
                    first_parts(l)
                for c, (c0, w) in enumerate(CHUNKS):
                    for k in range(KH):
                        n = (l * len(CHUNKS) + c) * KH + k
                        act.wait_ge(S["t3_done"], n + 1)
                        act.wait_ge(S["u_done"], l * len(CHUNKS) + c + 1)
                        nc.scalar.activation(hT[:, k, c0:min(c0 + w, NP)], tmp[:, k, 0:min(w, NP - c0)],
                                             ACT.Relu).then_inc(S["h_done"], 1)

            act.wait_ge(S["mean2_done"], 1)
            nc.scalar.activation(rstd[:, :], mean[:, :], ACT.Sqrt).then_inc(S["std2_done"], 1)
            act.wait_ge(S["gb_loaded"], 48)

            def copy_transposed(t):
                act.wait_ge(S["xt2_done"], t + 1)
                nc.scalar.copy(hT[:, :, col(t)], ps[4 + t % 2][:, 0:D].rearrange("p (k n) -> p k n", k=KH)) \
                    .then_inc(S["xt2_copied"], 1)

            def store_gates(s):
                for b in range(3 * KH):
                    n = s * 3 * KH + b
                    act.wait_ge(S["g_done"], n + 1)
                    dest = xg[:, 0:L, b * CH + TC * s:b * CH + TC * s + TC].rearrange("p t c -> p c t")
                    nc.scalar.activation(dest, ps[n % 4][:, 0:TW].rearrange("p (c t) -> p c t", c=TC),
                                         ACT.Identity, bias=gcol[:, b // KH, b % KH:b % KH + 1]) \
                        .then_inc(S["g_stored"], 1)

            gate_input_order(copy_transposed, store_gates)
            act.wait_ge(S["warm_done"], 1)
            nc.scalar.activation(warm[:, 0:1], warm[:, 1:2], ACT.Sigmoid)

            def steps(r, first, end, full):
                with act.Fori(first // UN, end // UN) as j:
                    n = r * L + j * UN - SKIP
                    for u in range(UN):
                        act.wait_ge(S["cg_done"], n + (u + 1))
                        nc.scalar.activation(factors[:, :, 1], ps[2 + u % 2][:, 0:GW], ACT.Tanh) \
                            .then_inc(S["gg_done"], 1)
                        act.wait_ge(S["ci_done"], n + (u + 1))
                        nc.scalar.activation(terms[:, :, 0], ps[u % 2][:, 0:GW], ACT.Sigmoid) \
                            .then_inc(S["gi_done"], 1)
                        act.wait_ge(S["co_done"], n + (u + 1))
                        nc.scalar.activation(go, ps[4 + u % 2][:, 0:GW], ACT.Sigmoid) \
                            .then_inc(S["go_done"], 1)
                        act.wait_ge(S["c_done"], n + (u + 1))
                        nc.scalar.activation(tc, cell[:, (u + 1) % 2], ACT.Tanh).then_inc(S["tc_done"], 1)

            rounds(act, steps, lambda r, look: None)

        @block.vector
        def _(dve):
            nc.vector.memset(X[:, NT - 1, :], 0.0).then_inc(S["const_ready"], 1)
            nc.vector.memset(sraw, 0).then_inc(S["raw_set"], 1)
            nc.vector.memset(draw, 1 << 20).then_inc(S["raw_set"], 1)
            nc.vector.memset(kmax, -3.0e38).then_inc(S["kmax_done"], 1)
            nc.vector.memset(v1[:, :, :, P:P + 1], 1.0).then_inc(S["v_ones"], 1)

            def norm_stats(data, ready, done, stats):
                for t in range(NT):
                    ready(t)
                    if t >= 2:
                        dve.wait_ge(S[stats], t - 1)
                    nc.vector.bn_stats(bn6[:, t % 2, :], data[:, t, :]).then_inc(S[done], 1)
                    dve.wait_ge(S[done], t + 1)
                    nc.vector.bn_aggr(stat[:, t, :], bn6[:, t % 2, :]).then_inc(S[stats], 1)
                dve.wait_ge(S[stats], NT)

            def x_ready(t):
                if t % XT == 0 and t < NT - 1:
                    dve.wait_ge(S["x_loaded", t // XT], 16)
                if t == NT - 1:
                    dve.wait_ge(S["x_last_loaded"], 16)

            norm_stats(X, x_ready, "x_bn", "x_stat")
            nc.vector.tensor_scalar(mean[:, :], stat[:, :, 1], EPS, None, ALU.add).then_inc(S["var_done"], 1)
            dve.wait_ge(S["std_done"], 1)
            nc.vector.reciprocal(rstd[:, :], rstd[:, :]).then_inc(S["rstd_done"], 1)
            dve.wait_ge(S["rstd_done"], 1)
            for t in range(NT):
                if t >= 2:
                    dve.wait_ge(S["xt_done"], t - 1)
                nc.vector.tensor_scalar(xn[:, t % 2], X[:, t, :], stat[:, t, 0:1], rstd[:, t:t + 1],
                                        ALU.subtract, ALU.mult).then_inc(S["xn_ready"], 1)

            done = [0]
            log_p, log_g = P.bit_length() - 1, G.bit_length() - 1

            def step(ins):
                done[0] += 1
                ins.then_inc(S["dve_step"], 1)
                dve.wait_ge(S["dve_step"], done[0])

            def pair_field():
                dve.wait_ge(S["edges_loaded"], 96)
                nc.vector.tensor_copy(first, draw[:, :, 0]).then_inc(S["first_ready"], 1)
                nc.vector.tensor_scalar(f_i, sraw, log_p, log_g, ALU.arith_shift_right, ALU.arith_shift_left)
                step(nc.vector.tensor_scalar(f_j, draw, G - 1, None, ALU.bitwise_and))
                step(nc.vector.tensor_tensor(f_i, f_i, f_j, ALU.bitwise_or))
                nc.vector.tensor_copy(fields, f_i).then_inc(S["fields_f"], 1)

            def source_and_group_fields():
                step(nc.vector.tensor_scalar(f_j, sraw, P - 1, None, ALU.bitwise_and))
                nc.vector.tensor_copy(fields2, f_j).then_inc(S["fields_f"], 1)
                dve.wait_ge(S["fields_f"], 2)
                step(nc.vector.tensor_scalar(f_i, draw, log_g, None, ALU.arith_shift_right))
                nc.vector.tensor_copy(fields3, f_i).then_inc(S["fields_f"], 1)

            def starts_below():
                dve.wait_ge(S["first_ready"], 1)
                dve.wait_ge(S["iota_ready"], 10)
                for b in range(EB):
                    nc.vector.tensor_scalar(less[:, b, :], iota_first, first[:, b:b + 1], None, ALU.is_gt) \
                        .then_inc(S["less_done"], 1)

            def starts_and_table():
                dve.wait_ge(S["starts_sum"], 1)
                step(nc.vector.tensor_scalar(tmp[0:1, 0, 0:NG + 2], ps[0][0:1, 0:NG + 2], -1.0, 0.0,
                                             ALU.add, ALU.max))
                nc.vector.tensor_copy(starts[:, :], tmp[0:1, 0, 0:NG + 2]).then_inc(S["starts_done"], 1)
                nc.vector.memset(table, -1.0).then_inc(S["table_done"], 1)
                dve.wait_ge(S["table_done"], 1)
                for s, (m, a) in enumerate(((1.0, 0.0), (-1.0, -1.0), (1.0, 0.0))):
                    dve.wait_ge(S["fields_tr"], EB * (s + 1))
                    nc.vector.tensor_scalar(table[:, s, 0:ET], ps[4 + s][:, 0:ET], m, a, ALU.mult, ALU.add) \
                        .then_inc(S["table_done"], 1)

            def weight_norms(l):
                dve.wait_ge(S["wd_loaded", l], 16)
                dve.wait_ge(S["wcat_loaded", l], 16)
                lower, d_ = Wcat[:, l % 2, :, 0:D], Wd[:, l % 2]
                nc.vector.tensor_tensor(d_, d_, lower, ALU.subtract).then_inc(S["wd_done"], 1)
                dve.wait_ge(S["wd_done"], l + 1)
                square = tmp[:, 0, 0:KH * D] if l == 0 else squares
                sq = square.rearrange("p (k n) -> p k n", k=KH)
                for i, w_ in enumerate((d_, lower)):
                    step(nc.vector.tensor_tensor(sq, w_, w_, ALU.mult))
                    step(nc.vector.tensor_reduce(norms[:, i:i + 1], sq, AX.XY, ALU.add))
                step(nc.vector.tensor_tensor(square[:, 0:KH], bcol[:, l, :], bcol[:, l, :], ALU.mult))
                nc.vector.tensor_reduce(norms[:, 2:3], square[:, 0:KH], AX.X, ALU.add) \
                    .then_inc(S["norm_ready"], 1)

            def set_scale(l):
                dve.wait_ge(S["norm_sum"], l + 1)
                total = ps[1][:, 0:3]
                step(nc.vector.tensor_tensor(bound[:, 1:2], bound[:, 0:1], total[:, 1:2], ALU.mult))
                step(nc.vector.tensor_scalar(expo[:, :], bound[:, 1:2].bitcast(I32), 23, None,
                                             ALU.arith_shift_right))
                step(nc.vector.tensor_scalar(expo[:, :], expo[:, :], -125.0, None, ALU.add))
                step(nc.vector.tensor_scalar(expo[:, :], expo[:, :], 1, None, ALU.arith_shift_right))
                step(nc.vector.tensor_scalar(expo[:, :], expo[:, :], -1.0, 15.0 + 127.0, ALU.mult, ALU.add))
                step(nc.vector.tensor_scalar(expo[:, :], expo[:, :], 127.0, None, ALU.min))
                step(nc.vector.tensor_scalar(scale[:, l, 0:1], expo[:, :], 23, None, ALU.arith_shift_left))
                step(nc.vector.tensor_scalar(expo[:, :], expo[:, :], -1.0, 254.0, ALU.mult, ALU.add))
                step(nc.vector.tensor_scalar(scale[:, l, 1:2], expo[:, :], 23, None, ALU.arith_shift_left))
                step(nc.vector.tensor_copy(norms[:, :], total))
                step(nc.vector.tensor_tensor(bound[:, 1:2], norms[:, 0:1], norms[:, 1:2], ALU.add))
                step(nc.vector.tensor_tensor(bound[:, 1:2], bound[:, 1:2], bound[:, 0:1], ALU.mult))
                step(nc.vector.tensor_scalar(bound[:, 1:2], bound[:, 1:2], 2.0, None, ALU.mult))
                step(nc.vector.tensor_tensor(bound[:, 0:1], bound[:, 1:2], norms[:, 2:3], ALU.add))
                step(nc.vector.tensor_scalar(bound[:, 0:1], bound[:, 0:1], 2.0, None, ALU.mult))
                nc.vector.tensor_scalar(bound[:, 0:1], bound[:, 0:1], 1.0, None, ALU.mult) \
                    .then_inc(S["scale_ready"], 1)

            for t in range(NT):
                rows = LAST if t == NT - 1 else P
                dve.wait_ge(S["k_copied"], t + 1)
                dve.wait_ge(S["kmax_done"], t + 1)
                nc.vector.tensor_tensor(kmax[0:rows], kraw[0:rows, t, :], kmax[0:rows], ALU.max) \
                    .then_inc(S["kmax_done"], 1)
                if t == 8:
                    pair_field()
                if t == 10:
                    source_and_group_fields()
                if t == 11:
                    starts_below()
                if t == FT + 2:
                    starts_and_table()
            dve.wait_ge(S["bias_loaded"], 48)
            step(nc.vector.memset(bound[:, :], float(D)))
            weight_norms(0)
            set_scale(0)
            dve.wait_ge(S["kmaxb_ready"], 1)
            for t in range(NT):
                rows = LAST if t == NT - 1 else P
                if t >= 2:
                    dve.wait_ge(S["kexp_done"], t - 1)
                nc.vector.tensor_tensor(kshift[0:rows, t % 2], kraw[0:rows, t, :], kmaxb[0:rows],
                                        ALU.subtract).then_inc(S["kshift_done"], 1)
            dve.wait_ge(S["ctx_done"], NT)
            dve.wait_ge(S["iota_ready"], 5)
            for k in range(KH):
                nc.vector.reciprocal(den[:, 2 * k:2 * k + 1], ps[2 + k][:, P:P + 1]).then_inc(S["ctx_den"], 1)
                dve.wait_ge(S["ctx_den"], 2 * k + 1)
                nc.vector.tensor_scalar(den[:, 2 * k + 1:2 * k + 2], den[:, 2 * k:2 * k + 1], SCALE, None,
                                        ALU.mult).then_inc(S["ctx_den"], 1)
                dve.wait_ge(S["ctx_den"], 2 * k + 2)
                nc.vector.scalar_tensor_tensor(out=ctxn[:, k, :], in0=ps[2 + k][:, 0:P],
                                               scalar=den[:, 2 * k + 1:2 * k + 2], in1=hmask,
                                               op0=ALU.mult, op1=ALU.mult).then_inc(S["ctx_norm"], 1)
            def heads(ap):
                return ap.rearrange("p (h c) -> p h c", c=DH)

            def spread(ap):
                return ap.unsqueeze(2).to_broadcast([P, HEADS, DH])

            for t in range(NT + 3):
                now, was, b, c = t < NT, 1 <= t <= NT, t % 2, (t - 1) % 2
                if now:
                    dve.wait_ge(S["q_done"], t + 1)
                    nc.vector.tensor_reduce(qmx[:, b, 0, :], heads(ps[b][:, 0:D]), AX.X, ALU.max) \
                        .then_inc(S["qmax_done"], 1)
                if was:
                    dve.wait_ge(S["qexp_done"], t)
                    nc.vector.tensor_reduce(qmx[:, c, 1, :], heads(qs[:, c]), AX.X, ALU.add) \
                        .then_inc(S["qsum_done"], 1)
                if now:
                    dve.wait_ge(S["qmax_done"], t + 1)
                    if t >= 2:
                        dve.wait_ge(S["qn_done"], t - 1)
                    nc.vector.tensor_tensor(heads(qs[:, b]), heads(ps[b][:, 0:D]), spread(qmx[:, b, 0, :]),
                                            ALU.subtract).then_inc(S["qsub_done"], 1)
                if was:
                    dve.wait_ge(S["qsum_done"], t)
                    nc.vector.reciprocal(qmx[:, c, 2, :], qmx[:, c, 1, :]).then_inc(S["qrec_done"], 1)
                if t >= 3:
                    dve.wait_ge(S["att_copied"], t - 2)
                    if t >= 5:
                        dve.wait_ge(S["att_stats"], t - 4)
                    nc.vector.bn_stats(bn6[:, b, :], att[:, t - 3, :]).then_inc(S["att_bn"], 1)
                if was:
                    dve.wait_ge(S["qrec_done"], t)
                    if t >= 3:
                        dve.wait_ge(S["qt_done"], t - 2)
                    nc.vector.tensor_tensor(heads(qn[:, c]), heads(qs[:, c]), spread(qmx[:, c, 2, :]),
                                            ALU.mult).then_inc(S["qn_done"], 1)
                if t >= 3:
                    dve.wait_ge(S["att_bn"], t - 2)
                    nc.vector.bn_aggr(stat[:, t - 3, :], bn6[:, b, :]).then_inc(S["att_stats"], 1)
            dve.wait_ge(S["att_stats"], NT)
            nc.vector.tensor_scalar(mean[:, :], stat[:, :, 1], EPS, None, ALU.add).then_inc(S["att_stats"], 1)
            dve.wait_ge(S["att_std"], 1)
            nc.vector.reciprocal(rstd[:, :], rstd[:, :]).then_inc(S["att_rstd"], 1)
            dve.wait_ge(S["att_rstd"], 1)
            dve.wait_ge(S["bf_added"], 1)

            def second_part(l, t):
                n = l * NT + t
                if l < LAYERS:
                    dve.wait_ge(S["y_hi"], n + 1)
                    nc.vector.scalar_tensor_tensor(out=Yp[:, t, 1, :], in0=ps[t % 2][:, 0:D],
                                                   scalar=scale_f[:, l, 0:1], in1=Yp[:, t, 0, :],
                                                   op0=ALU.mult, op1=ALU.subtract).then_inc(S["y_lo"], 1)
                else:
                    dve.wait_ge(S["y_done"], n + 1)
                dve.wait_ge(S["att_added"], t + 1 if l == 0 else NT)
                if l > 0:
                    dve.wait_ge(S["cat_added"], n + 1 - NT)
                nc.vector.tensor_tensor(X[:, t, :], X[:, t, :], ps[t % 2][:, D:2 * D], ALU.add) \
                    .then_inc(S["cat_added"], 1)
                if l == LAYERS:
                    dve.wait_ge(S["cat_added"], n + 1)
                    if t >= 2:
                        dve.wait_ge(S["x2_stat"], t - 1)
                    nc.vector.bn_stats(bn6[:, t % 2, :], X[:, t, :]).then_inc(S["x2_bn"], 1)
                    dve.wait_ge(S["x2_bn"], t + 1)
                    nc.vector.bn_aggr(stat[:, t, :], bn6[:, t % 2, :]).then_inc(S["x2_stat"], 1)

            for t in range(NT + 1):
                if t < NT:
                    nc.vector.scalar_tensor_tensor(out=att[:, t, :], in0=att[:, t, :], scalar=stat[:, t, 0:1],
                                                   in1=gam, op0=ALU.subtract, op1=ALU.mult) \
                        .then_inc(S["att_n"], 1)
                if t:
                    dve.wait_ge(S["att_n"], t)
                    nc.vector.scalar_tensor_tensor(out=X[:, t - 1, :], in0=att[:, t - 1, :],
                                                   scalar=rstd[:, t - 1:t], in1=X[:, t - 1, :],
                                                   op0=ALU.mult, op1=ALU.add).then_inc(S["att_added"], 1)
                    second_part(0, t - 1)

            dve.wait_ge(S["starts_done"], 1)
            nc.vector.memset(window, 0.0).then_inc(S["ohu_ready"], UG)
            with dve.Fori(0, NG // UG) as j:
                for b in range(UG):
                    g = j * UG + b
                    dve.wait_ge(S["bval_ready"], g + 1)
                    dve.wait_ge(S["counts_done"], g + 1)
                    for k in range(BA, CAP):
                        nc.vector.tensor_scalar(onehot_d[:, b % 2, k - BA, :], iota_b[:, :],
                                                bval[:, b, k:k + 1], None, ALU.is_equal)
                    for k in range(CAP):
                        ins = nc.vector.tensor_scalar(onehot_u[:, b % 2, k, :], iota_u[:, :],
                                                      window[:, b, 0, k:k + 1], None, ALU.is_equal)
                    ins.then_inc(S["ohu_ready"], 1)

            def bounds(c, n):
                c0, w = CHUNKS[c]
                dve.wait_ge(S["cnt_done"], n)
                nc.vector.tensor_scalar(tmp[:, c % 2, 0:w], degree_bank(c)[:, 0:w], 1.0, None, ALU.max) \
                    .then_inc(S["inv_a"], 1)
                nc.vector.tensor_scalar(some[:, c0:c0 + w], degree_bank(c)[:, 0:w], 1.0, None, ALU.min) \
                    .then_inc(S["some_done"], 1)

            def inverse(c, n):
                c0, w = CHUNKS[c]
                dve.wait_ge(S["inv_a"], n)
                nc.vector.reciprocal(inv[:, c0:c0 + w], tmp[:, c % 2, 0:w]).then_inc(S["inv_done"], 1)

            for c, (c0, w) in enumerate(CHUNKS):
                bank = degree_bank(c)[0:1, 0:w]
                dve.wait_ge(S["cnt_done"], c + 1)
                for row, op in enumerate((ALU.add, ALU.max)):
                    nc.vector.tensor_reduce(degree[:, row, c:c + 1], bank, AX.X, op).then_inc(S["dve_step"], 1)
            done[0] += 2 * NC
            dve.wait_ge(S["dve_step"], done[0])
            step(nc.vector.tensor_reduce(degree[:, 2, 0:1], degree[:, 0, 0:NC], AX.X, ALU.add))
            step(nc.vector.tensor_reduce(degree[:, 2, 1:2], degree[:, 1, 0:NC], AX.X, ALU.max))
            step(nc.vector.tensor_scalar(degree[:, 2, 2:3], degree[:, 2, 0:1], float(E), None, ALU.is_equal))
            step(nc.vector.tensor_scalar(degree[:, 2, 3:4], degree[:, 2, 1:2], 2048.0, None, ALU.is_lt))
            nc.vector.tensor_tensor(flag[0:1, 1:2], degree[:, 2, 2:3], degree[:, 2, 3:4], ALU.mult) \
                .then_inc(S["graph_flag"], 1)
            for c in range(NC):
                bounds(c, c + 1)
                inverse(c, c + 1)

            def hot_rows(p):
                c0, w = CHUNKS[p % NC]

                def body(t, rows, first, last):
                    n = p * ET + t
                    dve.wait_ge(S["gen_edges", p // NC], (t + (p % NC * ET + 1)) * 32)
                    nc.vector.tensor_scalar(gen_col[0:rows, :], gen_dst[0:rows, :], -float(c0), None, ALU.add) \
                        .then_inc(S["gen_cols"], 1)
                    dve.wait_ge(S["gen_cols"], n + 1)
                    nc.vector.tensor_scalar(gen_hot[0:rows, 0:w], gen_iota[0:rows, 0:w], gen_col[0:rows, 0:1],
                                            None, ALU.is_equal).then_inc(S["gen_hots"], 1)

                edge_tiles(dve, body)

            for l in range(LAYERS + 1):
                if l:
                    for t in range(NT):
                        second_part(l, t)
                if l == LAYERS:
                    break
                if l == 0:
                    dve.wait_ge(S["graph_flag"], 1)
                    exact = dve.value_load(flag[0:1, 1:2], min_val=0, max_val=1)
                    with dve.If(exact < 1):
                        dve.wait_ge(S["gen_iota_ready"], 1)
                        for c in range(NC):
                            hot_rows(c)
                            bounds(c, NC + c + 1)
                            inverse(c, NC + c + 1)
                        dve.wait_ge(S["inv_done"], 2 * NC)
                        dve.nop()
                    dve.nop()
                dve.wait_ge(S["inv_done"], len(CHUNKS))
                for c, (c0, w) in enumerate(CHUNKS):
                    m = l * len(CHUNKS) + c
                    with dve.If(exact < 1):
                        hot_rows(NC + m)
                        dve.nop()
                    dve.wait_ge(S["agg_done"], m + 1)
                    if c:
                        dve.wait_ge(S["h_done"], m * KH)
                    else:
                        dve.wait_ge(S["y_lo"], (l + 1) * NT)
                    for k in range(KH):
                        nc.vector.scalar_tensor_tensor(
                            out=tmp[:, k, 0:w], in0=ps[(2 if c % 2 == 0 else 6) + k][:, 0:w],
                            scalar=scale_f[:, l, 1:2], in1=inv[:, c0:c0 + w], op0=ALU.mult, op1=ALU.mult) \
                            .then_inc(S["t1_done"], 1)
                    dve.wait_ge(S["u_done"], m + 1)
                    for k in range(KH):
                        dve.wait_ge(S["t1_done"], m * KH + k + 1)
                        nc.vector.tensor_tensor(tmp[:, k, 0:w], tmp[:, k, 0:w], ps[4 + k][:, 0:w],
                                                ALU.add).then_inc(S["t2_done"], 1)
                    for k in range(KH):
                        dve.wait_ge(S["t2_done"], m * KH + k + 1)
                        nc.vector.scalar_tensor_tensor(out=tmp[:, k, 0:w], in0=tmp[:, k, 0:w],
                                                       scalar=bcol[:, l, k:k + 1], in1=some[:, c0:c0 + w],
                                                       op0=ALU.add, op1=ALU.mult).then_inc(S["t3_done"], 1)
                    if l + 1 < LAYERS and c == 1:
                        weight_norms(l + 1)
                    if l + 1 < LAYERS and c == 2:
                        set_scale(l + 1)

            dve.wait_ge(S["x2_stat"], NT)
            nc.vector.tensor_scalar(mean[:, :], stat[:, :, 1], EPS, None, ALU.add).then_inc(S["mean2_done"], 1)
            dve.wait_ge(S["std2_done"], 1)
            nc.vector.reciprocal(rstd[:, :], rstd[:, :]).then_inc(S["rstd2_done"], 1)
            dve.wait_ge(S["rstd2_done"], 1)
            for t in range(NT):
                if t >= 2:
                    dve.wait_ge(S["xt2_done"], t - 1)
                nc.vector.tensor_scalar(xn2[:, t % 2], X[:, t, :], stat[:, t, 0:1], rstd[:, t:t + 1],
                                        ALU.subtract, ALU.mult).then_inc(S["xn2_ready"], 1)

            dve.wait_ge(S["v_loaded"], 48)
            nc.vector.tensor_copy(Vhi, Vraw).then_inc(S["v_hi"], 1)
            dve.wait_ge(S["v_hi"], 1)
            nc.vector.tensor_tensor(Vlo, Vraw, Vhi, ALU.subtract).then_inc(S["v_lo"], 1)
            nc.vector.memset(warm[:, :], 0.0).then_inc(S["warm_done"], 1)
            nc.vector.memset(st[:, 15 * GW:23 * GW], 0.0).then_inc(S["st_init"], 1)
            nc.vector.memset(cell0, 0.0).then_inc(S["st_init"], 1)
            nc.vector.memset(h0, 0.0).then_inc(S["st_init"], 1)
            nc.vector.memset(hist, 0.0).then_inc(S["st_init"], 1)
            nc.vector.memset(h_hi, 0.0).then_inc(S["hhi_done"], 1)
            nc.vector.memset(h_lo, 0.0).then_inc(S["hlo_done"], 1)
            dve.wait_ge(S["g_stored"], (NP // TW) * 3 * KH)
            nc.vector.tensor_copy(xg[:, L, :], xg[:, 0, :]).then_inc(S["g_wrap"], 1)
            dve.wait_ge(S["st_init"], 4)

            def kc(ap):
                return ap.rearrange("p (k c) -> p k c", k=KH)

            before = hist[:, :, 0:CH * L].rearrange("p k (c t) -> p k c t", t=L)
            behind = hist[:, :, 1:CH * L + 1].rearrange("p k (c t) -> p k c t", t=L)

            def steps(r, first, end, full):
                with dve.Fori(first // UN, end // UN) as j:
                    n = r * L + j * UN - SKIP
                    for u in range(UN):
                        old, new = u % 2, (u + 1) % 2
                        h_old = before[:, :, :, ds(j * UN + u, 1)].rearrange("p k c t -> p k (c t)")
                        h_new = behind[:, :, :, ds(j * UN + u, 1)].rearrange("p k c t -> p k (c t)")
                        nc.vector.tensor_tensor(kc(terms[:, :, 1]), h_old, kc(cell[:, old]), ALU.mult) \
                            .then_inc(S["hc_done"], 1)
                        dve.wait_ge(S["gi_done"], n + (u + 1))
                        dve.wait_ge(S["hc_done"], n + (u + 1))
                        nc.vector.tensor_tensor_scan(pairs[:, new].rearrange("p n o -> p (n o)"),
                                                     factors.rearrange("p n o -> p (n o)"),
                                                     terms.rearrange("p n o -> p (n o)"),
                                                     0.0, ALU.mult, ALU.add).then_inc(S["c_done"], 1)
                        dve.wait_ge(S["tc_done"], n + (u + 1))
                        nc.vector.tensor_tensor(h_hi[:, new], go, tc, ALU.mult) \
                            .then_inc(S["hhi_done"], 1)
                        nc.vector.tensor_tensor(h_new, kc(go), kc(tc), ALU.mult) \
                            .then_inc(S["h_f32"], 1)
                        dve.wait_ge(S["h_f32"], n + (u + 1))
                        nc.vector.tensor_tensor(kc(h_lo[:, new]), h_new, kc(h_hi[:, new]), ALU.subtract) \
                            .then_inc(S["hlo_done"], 1)

            def after(r, look):
                dve.wait_ge(S["hlo_done"], (r + 1) * (L + 1) - SKIP)
                new_h, end_c = before[:, :, :, 0], kc(cell[:, 0])
                old_c = kc(cell0)
                if look is not None:
                    nc.vector.tensor_tensor(diff[:, 0, :, 1:USED], new_h[:, :, 1:USED],
                                            kc(h0)[:, :, 1:USED], ALU.subtract).then_inc(S["end_diff"], 1)
                    nc.vector.tensor_tensor(diff[:, 1, :, 1:USED], end_c[:, :, 0:USED - 1],
                                            old_c[:, :, 1:USED], ALU.subtract).then_inc(S["end_diff"], 1)
                    dve.wait_ge(S["end_diff"], look * 2)
                    nc.vector.tensor_reduce(moved[:, 0:1], diff[:, :, :, 1:USED], AX.XYZ, ALU.max,
                                            apply_absolute_value=True).then_inc(S["end_max"], 1)
                    dve.wait_ge(S["end_tr"], look)
                    nc.vector.tensor_reduce(warm[:, 0:1], ps[6][0:1, 0:P], AX.X, ALU.max) \
                        .then_inc(S["end_total"], 1)
                    dve.wait_ge(S["end_total"], look)
                    nc.vector.tensor_scalar(flag[0:1, 0:1], warm[:, 0:1], TOL, None, ALU.is_gt) \
                        .then_inc(S["end_flag"], 1)
                nc.vector.tensor_copy(kc(h_hi[:, 0]), new_h).then_inc(S["hhi_done"], 1)
                nc.vector.tensor_copy(old_c[:, :, 1:CH], end_c[:, :, 0:CH - 1]).then_inc(S["shift_c"], 1)
                dve.wait_ge(S["hhi_done"], (r + 1) * (L + 1) + 1 - SKIP)
                nc.vector.tensor_tensor(kc(h_lo[:, 0]), new_h, kc(h_hi[:, 0]), ALU.subtract) \
                    .then_inc(S["hlo_done"], 1)
                dve.wait_ge(S["shift_c"], r * 3 + 1)
                nc.vector.tensor_copy(cell[:, 0], cell0).then_inc(S["shift_c"], 1)
                nc.vector.tensor_copy(kc(h0), new_h).then_inc(S["shift_c"], 1)
                dve.wait_ge(S["shift_c"], r * 3 + 3)

            rounds(dve, steps, after)

            nc.vector.drain().then_inc(S["scan_done"], 1)
            for t in range(NT):
                dve.wait_ge(S["ht_done"], t + 1)
                nc.vector.tensor_tensor(X[:, t, :], X[:, t, :], ps[6 + t % 2][:, 0:D], ALU.add) \
                    .then_inc(S["y_added"], 1)

        @block.tensor
        def _(pe):
            def transposes(ready, done, copied, src_):
                for t in range(NT):
                    pe.wait_ge(S[ready], t + 1)
                    if t >= 2:
                        pe.wait_ge(S[copied], t - 1)
                    for k in range(KH):
                        ins = nc.tensor.transpose(ps[t % 2][:, col(k)], src_[:, t % 2, col(k)], ident[:, :])
                    ins.then_inc(S[done], 1)

            pe.wait_ge(S["iota_ready"], 10)
            transposes("xn_ready", "xt_done", "xt_copied", xn)

            def node_product(bank, t, w, off=0):
                for k in range(KH):
                    ins = nc.tensor.matmul(bank[:, off:off + w.shape[2]], hT[:, k, col(t)], w[:, k, :],
                                           start=(k == 0), stop=(k == KH - 1))
                return ins

            def sum_norms(l):
                pe.wait_ge(S["norm_ready"], l + 1)
                nc.tensor.matmul(ps[1][:, 0:3], ones_f[:, :], norms[:, :], start=True, stop=True) \
                    .then_inc(S["norm_sum"], 1)

            pe.wait_ge(S["xt_copied"], NT)
            pe.wait_ge(S["wmix_loaded"], 32)
            for t in range(NT):
                if t >= 2:
                    pe.wait_ge(S["v_copied"], t - 1)
                node_product(ps[2 + t % 2], t, wqkv[:, :, D:3 * D]).then_inc(S["kv_done"], 1)
                if t == FT:
                    for s, f in enumerate((fields, fields2, fields3)):
                        pe.wait_ge(S["fields_f"], s + 1)
                        for b in range(EB):
                            nc.tensor.transpose(ps[4 + s][:, col(b)], f[:, b, :], ident[:, :]) \
                                .then_inc(S["fields_tr"], 1)
                    pe.wait_ge(S["less_done"], EB)
                    for b in range(EB):
                        ins = nc.tensor.matmul(ps[0][0:1, 0:NG + 2], ones_f[:, 0:1], less[:, b, :],
                                               start=(b == 0), stop=(b == EB - 1))
                    ins.then_inc(S["starts_sum"], 1)

            def q_product(t):
                if t >= 2:
                    pe.wait_ge(S["qsub_done"], t - 1)
                node_product(ps[t % 2], t, wqkv[:, :, 0:D]).then_inc(S["q_done"], 1)

            sum_norms(0)
            pe.wait_ge(S["starts_done"], 1)
            q_product(0)
            pe.wait_ge(S["scale_ready"], 1)
            q_product(1)
            pe.wait_ge(S["v_copied"], NT)
            pe.wait_ge(S["v_ones"], 1)
            for t in range(NT):
                rows = LAST if t == NT - 1 else P
                pe.wait_ge(S["kexp_done"], t + 1)
                for k in range(KH):
                    ins = nc.tensor.matmul(ps[2 + k][:, 0:P + 1], kexp[0:rows, t % 2, col(k)],
                                           v1[0:rows, t, k, :], start=(t == 0), stop=(t == NT - 1))
                ins.then_inc(S["ctx_done"], 1)
            pe.wait_ge(S["table_done"], 4)
            pe.wait_ge(S["ctx_norm"], KH)
            for k in range(KH):
                ins = nc.tensor.transpose(ps[4][:, col(k)], ctxn[:, k, :], ident[:, :])
            ins.then_inc(S["ctx_tr"], 1)
            pe.wait_ge(S["ctx_trc"], 1)
            for k in range(KH):
                ins = nc.tensor.matmul(ps[5][:, k * D:(k + 1) * D], ctxT[:, k, :], wout[:, k, :],
                                       start=True, stop=True)
            ins.then_inc(S["ctxw_done"], 1)
            pe.wait_ge(S["ctxw_copied"], 1)
            for t in range(NT + 2):
                if t and t + 1 < NT:
                    q_product(t + 1)
                if 1 <= t <= NT:
                    pe.wait_ge(S["qn_done"], t)
                    if t >= 3:
                        pe.wait_ge(S["qt_copied"], t - 2)
                    for k in range(KH):
                        ins = nc.tensor.transpose(ps[2 + (t - 1) % 2][:, col(k)], qn[:, (t - 1) % 2, col(k)],
                                                  ident[:, :])
                    ins.then_inc(S["qt_done"], 1)
                if t >= 2:
                    pe.wait_ge(S["qt_copied"], t - 1)
                    if t >= 4:
                        pe.wait_ge(S["att_copied"], t - 3)
                    for k in range(KH):
                        ins = nc.tensor.matmul(ps[6 + t % 2][:, 0:D], qT[:, t % 2, k, :], ctxw[:, k, :],
                                               start=(k == 0), stop=(k == KH - 1))
                    ins.then_inc(S["att_done"], 1)

            def y_tiles(l):
                if l < LAYERS:
                    pe.wait_ge(S["wcat_loaded", l], 16)
                pe.wait_ge(S["wf_loaded", l], 16)
                if l < LAYERS:
                    pe.wait_ge(S["scale_ready"], l + 1)
                for t in range(NT):
                    n = l * NT + t
                    if l and t * P % CW == 0:
                        pe.wait_ge(S["h_done"], ((l - 1) * NC + t * P // CW + 1) * KH)
                    if n >= 2:
                        pe.wait_ge(S["cat_added"], n - 1)
                    if l < LAYERS:
                        ins = node_product(ps[t % 2], t, Wcat[:, l % 2, :, :])
                    else:
                        ins = node_product(ps[t % 2], t, Wcat[:, l % 2, :, D:2 * D], D)
                    ins.then_inc(S["y_done"], 1)

            pe.wait_ge(S["qsub_done"], NT)
            y_tiles(0)

            pe.sem_inc(S["counts_done"], 2)
            with pe.Fori(0, NG // UG) as j:
                for b in range(UG):
                    g = j * UG + b
                    pe.wait_ge(S["oha_ready"], g + (1 + UG))
                    pe.wait_ge(S["ohu_ready"], g + (1 + UG))
                    pe.wait_ge(S["counts_stored"], g + 1)
                    for k in range(CAP):
                        lhs = onehot_a[:, b, k, :] if k < BA else onehot_d[:, b % 2, k - BA, :]
                        for h in range(2):
                            ins = nc.tensor.matmul(ps[2 * (b % 2) + h][:, 0:CB], lhs,
                                                   onehot_u[:, b % 2, k, h * CB:(h + 1) * CB],
                                                   start=(k == 0), stop=(k == CAP - 1))
                    ins.then_inc(S["counts_done"], 1)

            def degrees(c):
                c0, w = CHUNKS[c]
                for s in range(NT):
                    ins = nc.tensor.matmul(degree_bank(c)[:, 0:w], ones_h[:, :], AT[:, s, c0:c0 + w],
                                           start=(s == 0), stop=(s == NT - 1))
                ins.then_inc(S["cnt_done"], 1)

            def edge_products(p, outs):
                w = CHUNKS[p % NC][1]

                def body(t, rows, first, last):
                    n = p * ET + t
                    pe.wait_ge(S["gen_hots"], n + 1)
                    if p >= NC:
                        pe.wait_ge(S["gen_gathered", p // NC], (t + (p % NC * ET + 1)) * 16)
                    for i, (bank, lhs, begin, end) in enumerate(outs):
                        ins = nc.tensor.matmul(bank[:, 0:w], lhs[0:rows], gen_hot[0:rows, 0:w],
                                               start=first and begin, stop=last and end)
                    ins.then_inc(S["gen_used"], 1)

                edge_tiles(pe, body)

            pe.wait_ge(S["counts_stored"], NG + 2)
            for c in range(NC):
                degrees(c)
            for l in range(LAYERS + 1):
                if l:
                    y_tiles(l)
                if l == LAYERS:
                    break
                if l == 0:
                    pe.wait_ge(S["graph_flag"], 1)
                    exact = pe.value_load(flag[0:1, 1:2], min_val=0, max_val=1)
                    with pe.If(exact < 1):
                        pe.sem_inc(S["gen_used"], 1)
                        pe.wait_ge(S["some_done"], NC)
                        for c in range(NC):
                            edge_products(c, [(degree_bank(c), ones_h, True, True)])
                            pe.drain().then_inc(S["cnt_done"], 1)
                        pe.wait_ge(S["some_done"], 2 * NC)
                        pe.drain()
                    pe.nop()
                pe.wait_ge(S["y_lo"], (l + 1) * NT)
                pe.wait_ge(S["wd_done"], l + 1)
                for c, (c0, w) in enumerate(CHUNKS):
                    m = l * len(CHUNKS) + c
                    base = 2 if c % 2 == 0 else 6
                    if m >= 1:
                        pe.wait_ge(S["t1_done"], m * KH)

                    def block_products(s, start, stop):
                        for part in range(2):
                            for k in range(KH):
                                lhs = Yp[:, ds(s, 1), part, col(k)].rearrange("p s n -> p (s n)")
                                rhs = AT[:, ds(s, 1), c0:c0 + w].rearrange("p s n -> p (s n)")
                                ins = nc.tensor.matmul(ps[base + k][:, 0:w], lhs, rhs,
                                                       start=start and part == 0, stop=stop and part == 1)
                        return ins

                    with pe.If(exact > 0):
                        block_products(0, True, False)
                        with pe.Fori(0, (NT - 2) // 3) as j:
                            for s in range(1, 4):
                                block_products(j * 3 + s, False, False)
                        block_products(NT - 1, False, True).then_inc(S["agg_done"], 1)
                    with pe.Else():
                        edge_products(NC + m, [(ps[base + k], gen_rows[:, part * D + k * P:part * D + (k + 1) * P],
                                                part == 0, part == 1) for k in range(KH) for part in range(2)])
                        pe.drain().then_inc(S["agg_done"], 1)
                    if m:
                        pe.wait_ge(S["t2_done"], m * KH)
                    else:
                        pe.wait_ge(S["some_done"], NC)
                    for k in range(KH):
                        for h in range(KH):
                            ins = nc.tensor.matmul(ps[4 + k][:, 0:w], Wd[:, l % 2, h, col(k)],
                                                   hT[:, h, c0:c0 + w], start=(h == 0), stop=(h == KH - 1))
                    ins.then_inc(S["u_done"], 1)
                    if l + 1 < LAYERS and c == 2:
                        sum_norms(l + 1)

            def transpose(t):
                pe.wait_ge(S["xn2_ready"], t + 1)
                if t >= 2:
                    pe.wait_ge(S["xt2_copied"], t - 1)
                for k in range(KH):
                    ins = nc.tensor.transpose(ps[4 + t % 2][:, col(k)], xn2[:, t % 2, col(k)], ident[:, :])
                ins.then_inc(S["xt2_done"], 1)

            def gate_products(s):
                pe.wait_ge(S["xt2_copied"], min(NT, -(-(s + 1) * TW // P)))
                if s == 0:
                    pe.wait_ge(S["u_loaded"], 48)
                for b in range(3 * KH):
                    n = s * 3 * KH + b
                    if n >= 4:
                        pe.wait_ge(S["g_stored"], n - 3)
                    for k in range(KH):
                        ins = nc.tensor.matmul(ps[n % 4][:, 0:TW], Ucat[:, k, col(b)],
                                               hT[:, k, s * TW:(s + 1) * TW], start=(k == 0), stop=(k == KH - 1))
                    ins.then_inc(S["g_done"], 1)

            gate_input_order(transpose, gate_products)
            pe.wait_ge(S["g_wrap"], 1)
            pe.wait_ge(S["v_lo"], 1)

            def preload(u, t):
                row = xg[:, ds(t, 1), :].rearrange("p t n -> p (t n)")
                for g in range(3):
                    nc.tensor.matmul(ps[2 * g + u % 2][:, 0:GW], ident[:, :], row[:, g * GW:(g + 1) * GW],
                                     start=True, stop=False, skip_group_check=True)

            def steps(r, first, end, full):
                with pe.Fori(first // UN, end // UN) as j:
                    nh = r * (L + 1) + j * UN - SKIP
                    for u in range(UN):
                        def add(b, h, weights, last=False):
                            bank, o = ps[b // KH * 2 + u % 2], b % KH * CH
                            for k in range(KH):
                                for i, w in enumerate(weights):
                                    ins = nc.tensor.matmul(bank[:, o:o + CH], w[:, k, col(b)],
                                                           h[:, u % 2, k * CH:(k + 1) * CH], start=False,
                                                           stop=last and k == KH - 1, skip_group_check=True)
                            return ins

                        pe.wait_ge(S["hhi_done"], nh + (u + 1))
                        if not full:
                            for pair, done in (((2, 3), "cg_done"), ((0, 1), "ci_done"), ((4, 5), "co_done")):
                                if done == "co_done":
                                    pe.wait_ge(S["hlo_done"], nh + (u + 1))
                                for b in pair:
                                    ins = add(b, h_hi, (Vhi,), True)
                                ins.then_inc(S[done], 1)
                            preload(u + 1, j * UN + (u + 1))
                            continue
                        for b in (2, 3, 0, 1):
                            add(b, h_hi, (Vhi, Vlo))
                        pe.wait_ge(S["hlo_done"], nh + (u + 1))
                        add(2, h_lo, (Vhi,), True)
                        add(3, h_lo, (Vhi,), True).then_inc(S["cg_done"], 1)
                        add(0, h_lo, (Vhi,), True)
                        add(1, h_lo, (Vhi,), True).then_inc(S["ci_done"], 1)
                        for b in (4, 5):
                            add(b, h_hi, (Vhi, Vlo))
                            ins = add(b, h_lo, (Vhi,), True)
                        ins.then_inc(S["co_done"], 1)
                        preload(u + 1, j * UN + (u + 1))

            def after(r, look):
                if look is not None:
                    pe.wait_ge(S["end_max"], look)
                    nc.tensor.transpose(ps[6][0:1, 0:P], moved[:, 0:1], ident[:, :]).then_inc(S["end_tr"], 1)

            preload(0, SKIP)
            rounds(pe, steps, after)

            pe.wait_ge(S["scan_done"], 1)
            for t in range(NT):
                if t >= 2:
                    pe.wait_ge(S["y_added"], t - 1)
                for k in range(KH):
                    ins = nc.tensor.transpose(ps[6 + t % 2][:, col(k)],
                                              hist[:, k, 1 + t * P:1 + (t + 1) * P], ident[:, :])
                ins.then_inc(S["ht_done"], 1)


_INS = ["x", "src", "dst", "L0_gnn_W0", "L0_gnn_b0", "L0_gnn_W1", "L0_gnn_b1", "L0_gnn_W2", "L0_gnn_b2",
        "L0_gnn_Wf", "L0_gnn_bf", "L0_mix_Wqkv", "L0_mix_Wout", "L0_mix_gamma",
        "L0_ffn_U_i", "L0_ffn_V_i", "L0_ffn_b_i", "L0_ffn_U_f", "L0_ffn_V_f", "L0_ffn_b_f",
        "L0_ffn_U_c", "L0_ffn_V_c", "L0_ffn_b_c", "L0_ffn_U_o", "L0_ffn_V_o", "L0_ffn_b_o"]


def kernel(**inputs):
    import numpy as np
    import concourse.bacc as bacc
    from concourse.bass_utils import run_bass_kernel_spmd

    nc = bacc.Bacc("TRN2", target_bir_lowering=False, num_devices=1)
    arrays, args = {}, []
    for name in _INS:
        a = np.ascontiguousarray(inputs[name])
        arrays[f"in_{name}"] = a
        args.append(nc.dram_tensor(f"in_{name}", a.shape, mybir.dt.from_np(a.dtype), kind="ExternalInput").ap())
    out = nc.dram_tensor("out", inputs["x"].shape, F32, kind="ExternalOutput").ap()
    graph_layer_kernel(nc, *args, out)
    r = run_bass_kernel_spmd(nc, [arrays], core_ids=[0])
    return r.results[0]["out"]
```
